# Optimizing a Trainium2 kernel written in Bass

```python
import numpy as np
import jax
import jax.numpy as jnp

def _softmax(x, axis=-1):
    return jax.nn.softmax(x, axis=axis)

def _gelu(x):
    return jax.nn.gelu(x, approximate=True)

def _silu(x):
    return jax.nn.silu(x)

def _sigmoid(x):
    return jax.nn.sigmoid(x)

def _layernorm(x, axis=-1, eps=1e-05):
    m = jnp.mean(x, axis=axis, keepdims=True)
    v = jnp.var(x, axis=axis, keepdims=True)
    return (x - m) / jnp.sqrt(v + eps)

def _scatter_add(tgt, idx, src, axis=0):
    return tgt.at[idx].add(src)

def _segment_sum(src, seg, n):
    return jax.ops.segment_sum(src, seg, n)
kernel_name = 'mk_sandwich_d1_jaxref_r4_0303fb'

def setup_inputs(seed: int=0):
    np.random.seed(seed)
    _w = jnp.asarray

    def _L0_attn_setup():
        import math
        import jax, jax.numpy as jnp
        import numpy as np
        N_HEADS = 32
        ALIBI_BIAS_MAX = 8

        def _alibi_slopes(n_heads, alibi_bias_max=8):
            _n = 2 ** math.ceil(math.log2(n_heads))
            m = jnp.arange(1, _n + 1, dtype=jnp.float32) * (alibi_bias_max / _n)
            slopes = 1.0 / jnp.power(2.0, m)
            if _n != n_heads:
                slopes = jnp.concatenate([slopes[1::2], slopes[::2]])[:n_heads]
            return slopes
        key = jax.random.key(seed)
        k1, k2, k3 = jax.random.split(key, 3)
        B, S, D = (1, 512, 1024)
        x = jax.random.normal(k1, (B, S, D), dtype=jnp.float32)
        w_qkv = jax.random.normal(k2, (3 * D, D), dtype=jnp.float32) * 0.02
        b_qkv = jnp.zeros((3 * D,), dtype=jnp.float32)
        w_out = jax.random.normal(k3, (D, D), dtype=jnp.float32) * 0.02
        b_out = jnp.zeros((D,), dtype=jnp.float32)
        return {'x': x, 'w_qkv': w_qkv, 'b_qkv': b_qkv, 'w_out': w_out, 'b_out': b_out}
    _L0_attn_in = _L0_attn_setup()

    def _L0_ffn_setup():
        import jax, jax.numpy as jnp
        import numpy as np
        NF4_CODE = jnp.array([-1.0, -0.6961928009986877, -0.5250730514526367, -0.39491748809814453, -0.28444138169288635, -0.18477343022823334, -0.09105003625154495, 0.0, 0.07958029955625534, 0.16093020141124725, 0.24611230194568634, 0.33791524171829224, 0.44070982933044434, 0.5626170039176941, 0.7229568362236023, 1.0], dtype=jnp.float32)
        BLOCKSIZE = 64

        def nf4_quant_dequant(w):
            shape = w.shape
            flat = w.reshape(-1, BLOCKSIZE)
            absmax = jnp.max(jnp.abs(flat), axis=1, keepdims=True)
            normalized = flat / jnp.where(absmax == 0, 1.0, absmax)
            bounds = (NF4_CODE[:-1] + NF4_CODE[1:]) * 0.5
            idx = jnp.searchsorted(bounds, normalized)
            return (NF4_CODE[idx] * absmax).reshape(shape)
        key = jax.random.key(seed)
        k1, k2, k3, kx = jax.random.split(key, 4)
        D, H = (1024, 2752)
        scale = 0.02
        w1 = jax.random.normal(k1, (H, D), jnp.float32) * scale
        w2 = jax.random.normal(k2, (H, D), jnp.float32) * scale
        w3 = jax.random.normal(k3, (D, H), jnp.float32) * scale
        x = jax.random.normal(kx, (2, 512, D), jnp.float32)
        return {'x': x, 'w1': w1, 'w2': w2, 'w3': w3}
    _L0_ffn_in = _L0_ffn_setup()
    _d = {'L0_attn_x': _L0_attn_in['x'], 'L0_attn_w_qkv': _L0_attn_in['w_qkv'], 'L0_attn_b_qkv': _L0_attn_in['b_qkv'], 'L0_attn_w_out': _L0_attn_in['w_out'], 'L0_attn_b_out': _L0_attn_in['b_out'], 'L0_ffn_w1': _L0_ffn_in['w1'], 'L0_ffn_w2': _L0_ffn_in['w2'], 'L0_ffn_w3': _L0_ffn_in['w3']}
    _x0 = _d['L0_attn_x']
    _d['L0_attn_x'] = jax.random.normal(jax.random.fold_in(jax.random.key(seed), 1), (2, 1024, 1024), dtype=_x0.dtype)
    del _x0
    return _d

def reference(L0_attn_x, L0_attn_w_qkv, L0_attn_b_qkv, L0_attn_w_out, L0_attn_b_out, L0_ffn_w1, L0_ffn_w2, L0_ffn_w3):

    def _L0_attn_ref(x, w_qkv, b_qkv, w_out, b_out):
        import math
        import jax, jax.numpy as jnp
        import numpy as np
        N_HEADS = 32
        ALIBI_BIAS_MAX = 8

        def _alibi_slopes(n_heads, alibi_bias_max=8):
            _n = 2 ** math.ceil(math.log2(n_heads))
            m = jnp.arange(1, _n + 1, dtype=jnp.float32) * (alibi_bias_max / _n)
            slopes = 1.0 / jnp.power(2.0, m)
            if _n != n_heads:
                slopes = jnp.concatenate([slopes[1::2], slopes[::2]])[:n_heads]
            return slopes
        B, S, D = x.shape
        H = N_HEADS
        hd = D // H
        qkv = jnp.einsum('bsd,od->bso', x, w_qkv) + b_qkv
        q, k, v = jnp.split(qkv, 3, axis=-1)
        q = q.reshape(B, S, H, hd)
        k = k.reshape(B, S, H, hd)
        v = v.reshape(B, S, H, hd)
        scale = 1.0 / math.sqrt(hd)
        scores = jnp.einsum('bqhd,bkhd->bhqk', q, k) * scale
        slopes = _alibi_slopes(H, ALIBI_BIAS_MAX)
        positions = jnp.arange(1 - S, 1, dtype=jnp.float32)
        alibi = slopes[:, None] * positions[None, :]
        scores = scores + alibi[None, :, None, :]
        causal = jnp.arange(S)[:, None] >= jnp.arange(S)[None, :]
        scores = jnp.where(causal[None, None, :, :], scores, jnp.float32(-1000000000.0))
        attn = jax.nn.softmax(scores, axis=-1)
        out = jnp.einsum('bhqk,bkhd->bqhd', attn, v).reshape(B, S, D)
        return jnp.einsum('bsd,od->bso', out, w_out) + b_out

    def _L0_ffn_ref(x, w1, w2, w3):
        import jax, jax.numpy as jnp
        import numpy as np
        NF4_CODE = jnp.array([-1.0, -0.6961928009986877, -0.5250730514526367, -0.39491748809814453, -0.28444138169288635, -0.18477343022823334, -0.09105003625154495, 0.0, 0.07958029955625534, 0.16093020141124725, 0.24611230194568634, 0.33791524171829224, 0.44070982933044434, 0.5626170039176941, 0.7229568362236023, 1.0], dtype=jnp.float32)
        BLOCKSIZE = 64

        def nf4_quant_dequant(w):
            shape = w.shape
            flat = w.reshape(-1, BLOCKSIZE)
            absmax = jnp.max(jnp.abs(flat), axis=1, keepdims=True)
            normalized = flat / jnp.where(absmax == 0, 1.0, absmax)
            bounds = (NF4_CODE[:-1] + NF4_CODE[1:]) * 0.5
            idx = jnp.searchsorted(bounds, normalized)
            return (NF4_CODE[idx] * absmax).reshape(shape)
        dq1 = nf4_quant_dequant(w1)
        dq2 = nf4_quant_dequant(w2)
        dq3 = nf4_quant_dequant(w3)
        gate = jnp.einsum('bsd,hd->bsh', x, dq1)
        up = jnp.einsum('bsd,hd->bsh', x, dq2)
        h = jax.nn.silu(gate) * up
        return jnp.einsum('bsh,dh->bsd', h, dq3)
    x = L0_attn_x
    x = x + _layernorm(_L0_attn_ref(_layernorm(x, axis=-1), L0_attn_w_qkv, L0_attn_b_qkv, L0_attn_w_out, L0_attn_b_out), axis=-1)
    x = x + _layernorm(_L0_ffn_ref(_layernorm(x, axis=-1), L0_ffn_w1, L0_ffn_w2, L0_ffn_w3), axis=-1)
    return x

_drawn_inputs = setup_inputs


def setup_inputs(seed=0):
    import zlib

    import numpy as np

    out = dict(_drawn_inputs(seed))
    spreads = {'L0_attn_b_qkv': (0.0, 0.1), 'L0_attn_b_out': (0.0, 0.1)}
    factors = {}
    for name, (base, spread) in spreads.items():
        noise = np.random.default_rng([zlib.crc32(name.encode()), seed]).standard_normal(out[name].shape)
        drawn = base * np.exp(spread * noise) if base else spread * noise
        out[name] = jnp.asarray(drawn.astype(out[name].dtype))
    for name, factor in factors.items():
        out[name] = (out[name] * factor).astype(out[name].dtype)
    return out
```

```python
import concourse.bass as bass
from concourse import mybir
from contextlib import ExitStack

F32 = mybir.dt.float32
F32R = mybir.dt.float32r
BF16 = mybir.dt.bfloat16
I32 = mybir.dt.int32
ALU = mybir.AluOpType
ACT = mybir.ActivationFunctionType
AX = mybir.AxisListType

P = 128
B, S, D = 2, 1024, 1024
HEADS, HD = 32, 32
F = 2752
TOK = B * S
KT = D // P
FT = -(-F // P)
NT = TOK // P
CH = 512
NCH = TOK // CH
G4 = P // HD
HG = HEADS // G4
GROUPS = B * HG
QT = S // P
SCALE = HD ** -0.5
EPS = 1e-5
MASKED = -1e30
QB = 64
NB = D // QB

CODE = [-1.0, -0.6961928009986877, -0.5250730514526367, -0.39491748809814453, -0.28444138169288635,
        -0.18477343022823334, -0.09105003625154495, 0.0, 0.07958029955625534, 0.16093020141124725,
        0.24611230194568634, 0.33791524171829224, 0.44070982933044434, 0.5626170039176941,
        0.7229568362236023, 1.0]


def nf4_steps():
    import numpy as np
    code = np.array(CODE, np.float32)
    bounds = (code[:-1] + code[1:]) * np.float32(0.5)
    return [float(b) for b in bounds], [float(c + np.float32(1.0)) for c in code[1:]]


BOUNDS, STEPS = nf4_steps()
NQ = len(BOUNDS)


def wait(eng, sem, value):
    if isinstance(value, int) and value <= 0:
        return
    eng.wait_ge(sem, value)


def wait_apart(eng, sem, value, passed):
    eng.wait_ge(sem, value)
    eng.sem_inc(passed, 1)


def tiles(eng, n, body, first=1, last=0, start=0):
    for j in range(start, start + first):
        body(j)
    if n - last > start + first:
        with eng.Fori(start + first, n - last) as j:
            body(j)
    for j in range(n - last, n):
        body(j)


class Nf4:

    def __init__(self, nc, ctx, name, dq_slots, sign_slots):
        sb = lambda n, shape, dt: ctx.enter_context(nc.sbuf_tensor(f"{name}_{n}", shape, dt))
        sem = lambda n: ctx.enter_context(nc.semaphore(f"{name}_{n}"))
        self.nc = nc
        self.raw = sb("raw", [P, 2, D], F32)
        self.code = sb("code", [P, D], F32)
        self.dq_slots = dq_slots
        self.dq = sb("dq", [P, dq_slots, D], F32)
        assert NQ % sign_slots == 0
        self.sign_slots = sign_slots
        self.sign = sb("sign", [P, sign_slots, D], BF16)
        self.top = sb("top", [P, 2, NB], F32)
        self.safe = sb("safe", [P, 2, NB], F32)
        self.inv = sb("inv", [P, 2, NB], F32)
        self.bias = sb("bias", [P, NQ], F32)
        self.bias_ready = sem("bias_ready")
        self.loaded = [sem(f"loaded{s}") for s in range(2)]
        self.top_ready = sem("top_ready")
        self.safe_ready = sem("safe_ready")
        self.inv_ready = sem("inv_ready")
        self.scaled = sem("scaled")
        self.signs = sem("signs")
        self.coded = sem("coded")
        self.dq_ready = sem("dq_ready")

    def load(self, sp, n, j, p, src):
        wait(sp, self.signs, NQ * (n - 1))
        sp.dma_start(self.raw[:, p, :], src).then_inc(self.loaded[p], 16)

    def biases(self, dve):
        for i in range(NQ):
            self.nc.vector.memset(self.bias[:, i:i + 1], -BOUNDS[i]).then_inc(self.bias_ready, 1)

    def prepare(self, dve, n, j, p):
        nc = self.nc
        blocks = self.raw[:, p, :].rearrange("p (b k) -> p b k", k=QB)
        dve.wait_ge(self.loaded[p], 16 * (j + 1))
        wait(dve, self.dq_ready, n - 1)
        nc.vector.reduce_max(self.top[:, p, :], blocks, AX.X, apply_absolute_value=True).then_inc(self.top_ready, 1)
        dve.wait_ge(self.top_ready, n + 1)
        nc.vector.scalar_tensor_tensor(out=self.safe[:, p, :], in0=self.top[:, p, :], scalar=0.0,
                                       in1=self.top[:, p, :], op0=ALU.is_equal, op1=ALU.add).then_inc(self.safe_ready, 1)
        dve.wait_ge(self.safe_ready, n + 1)
        nc.vector.reciprocal(self.inv[:, p, :], self.safe[:, p, :]).then_inc(self.inv_ready, 1)
        dve.wait_ge(self.inv_ready, n + 1)
        inv = self.inv[:, p, :].unsqueeze(2).broadcast_to([P, NB, QB])
        nc.vector.tensor_tensor(blocks, blocks, inv, ALU.mult).then_inc(self.scaled, 1)

    def make_sign(self, act, n, p, i):
        if i == 0:
            act.wait_ge(self.scaled, n + 1)
            act.wait_ge(self.bias_ready, NQ)
        wait(act, self.coded, 2 * (NQ * n + i - self.sign_slots + 1))
        self.nc.scalar.activation(self.sign[:, i % self.sign_slots, :], self.raw[:, p, :], ACT.Sign,
                                  bias=self.bias[:, i:i + 1]).then_inc(self.signs, 1)

    def take(self, dve, n, i):
        nc = self.nc
        dve.wait_ge(self.signs, NQ * n + i + 1)
        for h in range(2):
            half = slice(h * D // 2, (h + 1) * D // 2)
            sign = self.sign[:, i % self.sign_slots, half]
            if i == 0:
                wait(dve, self.dq_ready, n)
                op = nc.vector.tensor_scalar(self.code[:, half], sign, STEPS[0], 0.0, ALU.mult, ALU.max)
            else:
                dve.wait_ge(self.coded, 2 * (NQ * n + i) + h - 1)
                op = nc.vector.scalar_tensor_tensor(out=self.code[:, half], in0=sign, scalar=STEPS[i],
                                                    in1=self.code[:, half], op0=ALU.mult, op1=ALU.max)
            op.then_inc(self.coded, 1)

    def finish(self, dve, n, p):
        dve.wait_ge(self.coded, 2 * NQ * (n + 1))
        top = self.top[:, p, :].unsqueeze(2).broadcast_to([P, NB, QB])
        out = self.dq[:, p % self.dq_slots, :].rearrange("p (b k) -> p b k", k=QB)
        self.nc.vector.scalar_tensor_tensor(out=out, in0=self.code[:, :].rearrange("p (b k) -> p b k", k=QB),
                                            scalar=-1.0, in1=top, op0=ALU.add, op1=ALU.mult).then_inc(self.dq_ready, 1)


class RowStats:

    def __init__(self, nc, ctx, name):
        sb = lambda n, shape: ctx.enter_context(nc.sbuf_tensor(f"{name}_{n}", shape, F32))
        sem = lambda n: ctx.enter_context(nc.semaphore(f"{name}_{n}"))
        self.nc = nc
        self.parts = sb("parts", [P, 2, 6])
        self.mv = sb("mv", [P, 2, 2])
        self.var_eps = sb("var_eps", [P, 2])
        self.rstd = sb("rstd", [P, 2])
        self.eps = sb("eps", [P, 1])
        self.power = sb("power", [P, 1])
        self.eps_ready = sem("eps_ready")
        self.parts_ready = sem("parts_ready")
        self.passed = sem("passed")
        self.mv_ready = sem("mv_ready")
        self.var_ready = sem("var_ready")
        self.rstd_ready = sem("rstd_ready")

    def start(self, dve):
        self.nc.vector.memset(self.power[:, :], -0.5).then_inc(self.eps_ready, 1)
        self.nc.vector.memset(self.eps[:, :], EPS).then_inc(self.eps_ready, 1)

    def moments(self, dve, n, p, halves):
        nc = self.nc
        wait(dve, self.mv_ready, n)
        for h in range(2):
            nc.vector.bn_stats(self.parts[:, h, :], halves[h]).then_inc(self.parts_ready, 1)
        wait_apart(dve, self.parts_ready, 2 * n + 2, self.passed)
        nc.vector.bn_aggr(self.mv[:, p, :], self.parts[:, :, :]).then_inc(self.mv_ready, 1)

    def invert(self, pool, n, p):
        if isinstance(n, int) and n == 0:
            pool.wait_ge(self.eps_ready, 2)
        pool.wait_ge(self.mv_ready, n + 1)
        self.nc.gpsimd.tensor_tensor(self.var_eps[:, p:p + 1], self.mv[:, p, 1:2], self.eps[:, :],
                                     ALU.add).then_inc(self.var_ready, 1)
        pool.wait_ge(self.var_ready, n + 1)
        self.nc.gpsimd.tensor_tensor(self.rstd[:, p:p + 1], self.var_eps[:, p:p + 1], self.power[:, :],
                                     ALU.pow).then_inc(self.rstd_ready, 1)

    def normalise(self, dve, n, p, out, rows):
        dve.wait_ge(self.rstd_ready, n + 1)
        return self.nc.vector.tensor_scalar(out, rows, self.mv[:, p, 0:1], self.rstd[:, p:p + 1],
                                            ALU.subtract, ALU.mult)


def constants(nc, k, slopes, alibi):
    with ExitStack() as ctx:
        sb = lambda n, shape, dt: ctx.enter_context(nc.sbuf_tensor(n, shape, dt))
        sem = lambda n: ctx.enter_context(nc.semaphore(n))
        where = sb("position_int", [HEADS, S], I32)
        position = sb("position", [HEADS, S], F32)
        slope = sb("slope", [HEADS, 1], F32)
        full = sb("alibi_full", [HEADS, S], F32)
        part = sb("alibi_parts", [HEADS, 2, S], F32R)
        zeroed, made, slope_in, stored = sem("c_zeroed"), sem("c_made"), sem("c_slope"), sem("c_stored")
        pos_ready, step = sem("c_pos"), sem("c_step")
        with nc.Block() as block:
            @block.sync
            def _(sp):
                sp.dma_start(slope[:, :], slopes).then_inc(slope_in, 16)
                sp.wait_ge(step, 4)
                for b in range(B):
                    for g in range(HG):
                        src = part[g * G4:(g + 1) * G4, :, :].bitcast(F32)
                        sp.dma_start(alibi[b * HG + g].rearrange("c i t -> i c t"), src).then_inc(stored, 16)
                sp.wait_ge(stored, 16 * GROUPS)

            @block.gpsimd
            def _(pool):
                nc.gpsimd.iota(where[:, :], [[1, S]], base=1 - S, channel_multiplier=0).then_inc(pos_ready, 1)
                for m in (k.ident, k.ident16, k.mask_q, k.mask_k):
                    nc.gpsimd.memset(m[:, :], 0.0).then_inc(zeroed, 1)
                pool.wait_ge(zeroed, 4)
                for m in (k.ident, k.ident16):
                    nc.gpsimd.affine_select(out=m[:, :], in_=m[:, :], compare_op=ALU.not_equal, fill=1.0,
                                            base=0, pattern=[[-1, P]], channel_multiplier=1).then_inc(made, 1)
                nc.gpsimd.affine_select(out=k.mask_q[:, :], in_=k.mask_q[:, :], compare_op=ALU.is_ge, fill=MASKED,
                                        base=0, pattern=[[-1, P]], channel_multiplier=1).then_inc(made, 1)
                nc.gpsimd.affine_select(out=k.mask_k[:, :], in_=k.mask_k[:, :], compare_op=ALU.is_ge, fill=MASKED,
                                        base=0, pattern=[[1, P]], channel_multiplier=-1).then_inc(made, 1)
                pool.wait_ge(made, 4)

            @block.vector
            def _(dve):
                dve.wait_ge(pos_ready, 1)
                nc.vector.tensor_copy(position[:, :], where[:, :]).then_inc(step, 1)
                dve.wait_ge(step, 1)
                dve.wait_ge(slope_in, 16)
                nc.vector.tensor_scalar(full[:, :], position[:, :], slope[:, :], None, ALU.mult).then_inc(step, 1)
                dve.wait_ge(step, 2)
                nc.vector.tensor_copy(part[:, 0, :], full[:, :]).then_inc(step, 1)
                dve.wait_ge(step, 3)
                nc.vector.tensor_tensor(part[:, 1, :], full[:, :], part[:, 0, :].bitcast(F32),
                                        ALU.subtract).then_inc(step, 1)


def normalise(nc, k, name, x, xt_hi, xt_lo):
    with ExitStack() as ctx:
        sb = lambda n, shape, dt: ctx.enter_context(nc.sbuf_tensor(f"{name}_{n}", shape, dt))
        sem = lambda n: ctx.enter_context(nc.semaphore(f"{name}_{n}"))
        rows = sb("rows", [P, 2, D], F32)
        flat = sb("flat", [P, 2, D], F32)
        stats = RowStats(nc, ctx, name)
        loaded = [sem(f"loaded{s}") for s in range(2)]
        flat_ready, turned, hi_ready, lo_ready = sem("flat_ready"), sem("turned"), sem("hi_ready"), sem("lo_ready")
        passed = sem("act_passed")

        def bank(p):
            return k.psum[:, 2 * p:2 * p + 2, :].rearrange("p a b -> p (a b)")

        with nc.Block() as block:
            @block.sync
            def _(sp):
                def body(j):
                    for p in range(2):
                        n = j * 2 + p
                        wait(sp, flat_ready, n - 1)
                        sp.dma_start(rows[:, p, :], x[n]).then_inc(loaded[p], 16)
                tiles(sp, NT // 2, body)

            @block.vector
            def _(dve):
                stats.start(dve)

                def low(n, p):
                    dve.wait_ge(hi_ready, n + 1)
                    cols = bass.ds(n * P, P)
                    nc.vector.tensor_tensor(xt_lo[:, :, cols], bank(p).rearrange("p (k t) -> p k t", t=P),
                                            xt_hi[:, :, cols].bitcast(F32), ALU.subtract).then_inc(lo_ready, 1)

                def body(j):
                    for p in range(2):
                        n = j * 2 + p
                        dve.wait_ge(loaded[p], (j + 1) * 16)
                        wait(dve, flat_ready, n - 1)
                        stats.moments(dve, n, p, [rows[:, p, h * CH:(h + 1) * CH] for h in range(2)])
                        if not (isinstance(n, int) and n == 0):
                            low(n - 1, 1 - p)
                        wait(dve, turned, n - 1)
                        stats.normalise(dve, n, p, flat[:, p, :], rows[:, p, :]).then_inc(flat_ready, 1)
                tiles(dve, NT // 2, body)
                low(NT - 1, 1)

            @block.tensor
            def _(pe):
                def body(j):
                    for p in range(2):
                        n = j * 2 + p
                        pe.wait_ge(flat_ready, n + 1)
                        wait(pe, lo_ready, n - 1)
                        for t in range(KT):
                            op = nc.tensor.transpose(bank(p)[:, t * P:(t + 1) * P], flat[:, p, t * P:(t + 1) * P],
                                                     k.ident[:, :])
                        op.then_inc(turned, 1)
                tiles(pe, NT // 2, body)

            @block.gpsimd
            def _(pool):
                def body(j):
                    for p in range(2):
                        stats.invert(pool, j * 2 + p, p)
                tiles(pool, NT // 2, body)

            @block.scalar
            def _(act):
                def high(n, p):
                    wait_apart(act, turned, n + 1, passed)
                    nc.scalar.activation(xt_hi[:, :, bass.ds(n * P, P)], bank(p).rearrange("p (k t) -> p k t", t=P),
                                         ACT.Copy).then_inc(hi_ready, 1)

                def body(j):
                    for p in range(2):
                        n = j * 2 + p
                        if not (isinstance(n, int) and n == 0):
                            high(n - 1, 1 - p)
                tiles(act, NT // 2, body)
                high(NT - 1, 1)


def qkv(nc, k, wqkv, bqkv, w3, xt_hi, xt_lo, q_hi, q_lo, k_hi, k_lo, v_all, dq3):
    with ExitStack() as ctx:
        sb = lambda n, shape, dt: ctx.enter_context(nc.sbuf_tensor(f"qkv_{n}", shape, dt))
        sem = lambda n: ctx.enter_context(nc.semaphore(f"qkv_{n}"))
        raw = sb("raw", [P, 2, KT, P], F32)
        w_hi = sb("w_hi", [P, 2, KT, P], F32R)
        w_lo = sb("w_lo", [P, 2, KT, P], F32R)
        bias = sb("bias", [P, 3 * KT], F32)
        bias_q = sb("bias_q", [P, KT], F32)
        full = sb("full", [P, 2, CH], F32)
        hi = sb("hi", [P, 2, CH], F32R)
        lo = sb("lo", [P, 2, CH], F32R)
        nf4 = Nf4(nc, ctx, "w3", 2, 5)
        raw_in = [sem(f"raw_in{s}") for s in range(2)]
        bias_in, bias_ready = sem("bias_in"), sem("bias_ready")
        w_hi_ready, w_lo_ready, summed, full_ready = sem("w_hi_ready"), sem("w_lo_ready"), sem("summed"), sem("full_ready")
        hi_ready, lo_ready, passed = sem("hi_ready"), sem("lo_ready"), sem("act_passed")
        stored = [sem(f"stored{s}") for s in range(2)]
        v_stored = [sem(f"v_stored{s}") for s in range(2)]
        dq_stored = [sem(f"dq_stored{s}") for s in range(2)]
        LAST = 3 * KT
        V0 = 2 * KT

        def kinds(eng, body):
            tiles(eng, KT // 2, lambda j: body(j, 0))
            tiles(eng, KT, lambda j: body(j, 1), first=0, start=KT // 2)
            tiles(eng, 3 * KT // 2, lambda j: body(j, 2), last=2, start=KT)

        def known(n, most):
            return not (isinstance(n, int) and n >= most)

        with nc.Block() as block:
            @block.sync
            def _(sp):
                sp.dma_start(bias[:, :], bqkv).then_inc(bias_in, 16)
                for m in range(2):
                    sp.dma_start(raw[:, m], wqkv[m]).then_inc(raw_in[m], 16)
                    nf4.load(sp, m, 0, m, w3[m])

                def body(j, kind):
                    for p in range(2):
                        m = j * 2 + p
                        if known(m, LAST - 2):
                            sp.wait_ge(w_lo_ready, m + 1)
                            sp.dma_start(raw[:, p], wqkv[m + 2]).then_inc(raw_in[p], 16)
                        if not (isinstance(m, int) and (m == 0 or m > FT)):
                            sp.wait_ge(nf4.dq_ready, m)
                            sp.dma_start(dq3[m - 1], nf4.dq[:, 1 - p, :]).then_inc(dq_stored[1 - p], 16)
                        for c in range(NCH):
                            n = m * NCH + c
                            dst = (m - kind * KT) + (c // 2) * HG
                            cols = slice((c % 2) * CH, (c % 2 + 1) * CH)
                            if kind < 2:
                                sp.wait_ge(lo_ready, n + 1)
                                for to, src in (((q_hi, k_hi)[kind], hi), ((q_lo, k_lo)[kind], lo)):
                                    sp.dma_start(to[dst][:, cols], src[:, c % 2, :].bitcast(F32)).then_inc(stored[c % 2], 16)
                            else:
                                sp.wait_ge(full_ready, n + 1)
                                sp.dma_start(v_all[dst][:, cols], full[:, c % 2, :]).then_inc(v_stored[c % 2], 16)
                            if c == 1 and known(m, FT - 2):
                                nf4.load(sp, m + 2, j + 1, p, w3[m + 2])
                kinds(sp, body)
                for s in range(2):
                    sp.wait_ge(stored[s], 16 * 2 * V0 * 2)
                    sp.wait_ge(v_stored[s], 16 * KT * 2)
                    sp.wait_ge(dq_stored[s], 16 * FT // 2)

            @block.scalar
            def _(act):
                def split(m, j, p):
                    act.wait_ge(raw_in[p], 16 * (j + 1))
                    wait(act, summed, NCH * (m - 1))
                    nc.scalar.activation(w_hi[:, p], raw[:, p], ACT.Copy).then_inc(w_hi_ready, 1)

                split(0, 0, 0)

                def body(j, kind):
                    for p in range(2):
                        m = j * 2 + p
                        if known(m, LAST - 1):
                            split(m + 1, j + p, 1 - p)
                        for c in range(NCH):
                            if known(m, FT):
                                for i in range(4 * c, min(4 * c + 4, NQ)):
                                    nf4.make_sign(act, m, p, i)
                            n = m * NCH + c
                            if c == 0 and p == 0:
                                act.wait_ge(bias_ready, 1)
                            if kind < 2:
                                wait(act, lo_ready, n - 1)
                            else:
                                act.wait_ge(lo_ready, V0 * NCH)
                                wait(act, v_stored[c % 2], 16 * ((m - V0) * 2 + c // 2))
                            wait_apart(act, summed, n + 1, passed)
                            col = bias_q[:, bass.ds(m, 1)] if kind == 0 else bias[:, bass.ds(m, 1)]
                            nc.scalar.activation(full[:, c % 2, :], k.psum[:, c, :], ACT.Identity, bias=col,
                                                 scale=SCALE if kind == 0 else 1.0).then_inc(full_ready, 1)
                kinds(act, body)

            @block.tensor
            def _(pe):
                def body(j, kind):
                    for p in range(2):
                        m = j * 2 + p
                        pe.wait_ge(w_lo_ready, m + 1)
                        for c in range(NCH):
                            wait(pe, full_ready, NCH * (m - 1) + c + 1)
                            cols = slice(c * CH, (c + 1) * CH)
                            terms = [(w, x, t) for t in range(KT) for w, x in ((w_hi, xt_hi), (w_hi, xt_lo), (w_lo, xt_hi))]
                            for i, (w, x, t) in enumerate(terms):
                                op = nc.tensor.matmul(k.psum[:, c, :], w[:, p, t, :], x[:, t, cols],
                                                      start=(i == 0), stop=(i == len(terms) - 1))
                            op.then_inc(summed, 1)
                kinds(pe, body)

            @block.vector
            def _(dve):
                nf4.biases(dve)
                dve.wait_ge(bias_in, 16)
                nc.vector.tensor_scalar(bias_q[:, :], bias[:, 0:KT], SCALE, None, ALU.mult).then_inc(bias_ready, 1)

                def split(m, j, p):
                    dve.wait_ge(w_hi_ready, m + 1)
                    nc.vector.tensor_tensor(w_lo[:, p], raw[:, p], w_hi[:, p].bitcast(F32),
                                            ALU.subtract).then_inc(w_lo_ready, 1)

                split(0, 0, 0)
                nf4.prepare(dve, 0, 0, 0)

                def body(j, kind):
                    for p in range(2):
                        m = j * 2 + p
                        if known(m, LAST - 1):
                            split(m + 1, j + p, 1 - p)
                        if known(m, FT - 1):
                            nf4.prepare(dve, m + 1, j + p, 1 - p)
                        for c in range(NCH):
                            if known(m, FT):
                                for i in range(4 * c, min(4 * c + 4, NQ)):
                                    nf4.take(dve, m, i)
                            if kind < 2:
                                n = m * NCH + c
                                dve.wait_ge(full_ready, n + 1)
                                wait(dve, stored[c % 2], 32 * (m * 2 + c // 2))
                                nc.vector.tensor_copy(hi[:, c % 2, :], full[:, c % 2, :]).then_inc(hi_ready, 1)
                                dve.wait_ge(hi_ready, n + 1)
                                nc.vector.tensor_tensor(lo[:, c % 2, :], full[:, c % 2, :],
                                                        hi[:, c % 2, :].bitcast(F32), ALU.subtract).then_inc(lo_ready, 1)
                        if known(m, FT):
                            wait(dve, dq_stored[p], 16 * j)
                            nf4.finish(dve, m, p)
                kinds(dve, body)


def block_rows(step):
    c, t = step
    return max(0, t * P - c * CH)


STEPS2 = [(c, t) for c in range(S // CH) for t in range((c + 1) * CH // P)]
UNITS_HEAD = [(t, a) for t in range(QT) for a in range(0, (t + 1) * P, CH)]
MAX_AT = {u: n for n, u in enumerate(UNITS_HEAD)}


def first_pass_units():
    units = [("v", 0), ("v", 1)]
    later = []
    for i in range(G4):
        for n, u in enumerate(UNITS_HEAD):
            units.append(("s", i, u))
            if n == 3:
                units += later
                later = []
        later = [("m", i, 0), ("m", i, 1)]
    return units + later


UNITS = first_pass_units()
NU = len(UNITS)


def attention(nc, k, q_hi, q_lo, k_hi, k_lo, v_all, alibi, att_hi, att_lo):
    SUM_ROWS, ALL_ROWS = 3 * HD + 2, 3 * HD + 4
    ITEMS = len(STEPS2) * G4
    PROBS = 8
    assert ITEMS % PROBS == 0 and NU % 2 == 0
    with ExitStack() as ctx:
        sb = lambda n, shape, dt: ctx.enter_context(nc.sbuf_tensor(f"heads_{n}", shape, dt))
        sem = lambda n: ctx.enter_context(nc.semaphore(f"heads_{n}"))
        qs = sb("qs", [P, 2, G4, S], F32R)
        ks = sb("ks", [P, 2, G4, S], F32R)
        vt = sb("vt", [P, 2, S], F32)
        v = sb("v", [P, 2, QT, P], F32)
        ones = sb("ones", [P, HD], F32)
        probs = sb("probs", [P, PROBS, CH], F32)
        part_max = sb("part_max", [P, 2, len(UNITS_HEAD)], F32)
        neg_max = sb("neg_max", [P, 2, QT], F32)
        max_rows = sb("max_rows", [P, 2, QT, 4], F32R)
        out_sb = sb("out", [P, 2, CH], F32)
        sum_sb = sb("sum", [P, CH], F32)
        inv = sb("inv", [P, CH], F32)
        full = sb("full", [P, CH], F32)
        hi = sb("hi", [P, 2, CH], F32R)
        lo = sb("lo", [P, 2, CH], F32R)
        loaded = [sem(f"loaded{s}") for s in range(2)]
        stored = [sem(f"stored{s}") for s in range(2)]
        LOADS = 8
        set_up = sem("set_up")
        unit_done, unit_read, turned_rows = sem("unit_done"), sem("unit_read"), sem("turned_rows")
        best, split_hi, split_lo = sem("best"), sem("split_hi"), sem("split_lo")
        scored, exped, used = sem("scored"), sem("exped"), sem("used")
        out_read, inv_ready, full_ready = sem("out_read"), sem("inv_ready"), sem("full_ready")
        hi_ready, lo_ready = sem("hi_ready"), sem("lo_ready")
        NS = len(STEPS2)
        M_UNITS = [u for u in UNITS if u[0] == "m"]
        S2_BANKS = 4
        OUT, SUM = 6, 7

        def unit_bank(n):
            return S2_BANKS + n % 2

        def groups(eng, body):
            def two(j):
                for p in range(2):
                    g = j * 2 + p
                    body(g, j, p, not (isinstance(g, int) and g == GROUPS - 1))
            tiles(eng, GROUPS // 2, two, last=1)

        with nc.Block() as block:
            @block.sync
            def _(sp):
                def load(g, p, uses):
                    wait(sp, scored, ITEMS * (g - 1))
                    for to, rows, src in ((qs, 0, q_hi), (qs, 1, q_hi), (qs, 2, q_lo),
                                          (ks, 0, k_hi), (ks, 1, k_lo), (ks, 2, k_hi)):
                        dst = to[rows * HD:(rows + 1) * HD, p, :, :].bitcast(F32)
                        sp.dma_start(dst, src[g].rearrange("(i r) t -> r i t", r=HD)).then_inc(loaded[p], 16)
                    sp.dma_start(ks[3 * HD:3 * HD + 2, p, :, :].bitcast(F32), alibi[g]).then_inc(loaded[p], 16)
                    sp.dma_start(vt[:, p, :], v_all[g]).then_inc(loaded[p], 16)

                sp.wait_ge(set_up, 3)
                load(0, 0, 0)
                load(1, 1, 0)

                def body(g, j, p, more):
                    for c in range(2):
                        sp.wait_ge(lo_ready, 2 * g + c + 1)
                        for to, src in ((att_hi, hi), (att_lo, lo)):
                            sp.dma_start(to[g, c], src[:, c, :].bitcast(F32)).then_inc(stored[c], 16)
                        if c == 1 and not (isinstance(g, int) and g >= GROUPS - 2):
                            load(g + 2, p, j)
                groups(sp, body)
                for c in range(2):
                    sp.wait_ge(stored[c], 32 * GROUPS)

            @block.tensor
            def _(pe):
                def unit(g, p, n):
                    what = UNITS[n]
                    wait(pe, unit_read, NU * g + n - 1)
                    bank = k.psum[:, unit_bank(n), :]
                    if what[0] == "v":
                        for t in range(4):
                            cols = slice((4 * what[1] + t) * P, (4 * what[1] + t + 1) * P)
                            op = nc.tensor.transpose(bank[:, t * P:(t + 1) * P], vt[:, p, cols], k.ident[:, :])
                    elif what[0] == "m":
                        i = what[1]
                        pe.wait_ge(split_lo, G4 * g + i + 1)
                        for t in range(4):
                            op = nc.tensor.transpose(bank[0:4, t * P:(t + 1) * P],
                                                     max_rows[:, i % 2, 4 * what[2] + t, :].bitcast(F32), k.ident[:, :])
                    else:
                        i, (t, a) = what[1:]
                        width = min(CH, (t + 1) * P - a)
                        last = a + width == (t + 1) * P
                        op = nc.tensor.matmul(bank[:, 0:width], qs[0:SUM_ROWS, p, i, t * P:(t + 1) * P],
                                              ks[0:SUM_ROWS, p, i, a:a + width], start=True, stop=not last)
                        if last:
                            op = nc.tensor.matmul(bank[:, width - P:width], k.ident16[:, :], k.mask_q[:, :],
                                                  start=False, stop=True)
                    op.then_inc(unit_done, 1)

                def scores(g, p, s, i):
                    c, t = STEPS2[s]
                    n = g * ITEMS + s * G4 + i
                    wait(pe, exped, n - S2_BANKS + 1)
                    if s == 0:
                        pe.wait_ge(turned_rows, 2 * (G4 * g + i + 1))
                    skip = block_rows((c, t))
                    bank = k.psum[:, i, 0:CH - skip]
                    diagonal = t * P >= c * CH
                    op = nc.tensor.matmul(bank, ks[0:ALL_ROWS, p, i, t * P:(t + 1) * P],
                                          qs[0:ALL_ROWS, p, i, c * CH + skip:(c + 1) * CH], start=True, stop=not diagonal)
                    if diagonal:
                        op = nc.tensor.matmul(k.psum[:, i, 0:P], k.ident16[:, :], k.mask_k[:, :], start=False, stop=True)
                    op.then_inc(scored, 1)

                def values(g, p, s):
                    c, t = STEPS2[s]
                    if t == 0:
                        wait(pe, out_read, 2 * (2 * g + c))
                    pe.wait_ge(exped, g * ITEMS + (s + 1) * G4)
                    if s == 0:
                        pe.wait_ge(unit_read, NU * g + 2)
                    skip = block_rows((c, t))
                    end = t == (c + 1) * CH // P - 1
                    for to in (OUT, SUM):
                        for i in range(G4):
                            slot = (s * G4 + i) % PROBS
                            lhs = v[:, p, t, i * HD:(i + 1) * HD] if to == OUT else ones[:, :]
                            op = nc.tensor.matmul(k.psum[i * HD:(i + 1) * HD, to, skip:CH], lhs,
                                                  probs[:, slot, 0:CH - skip], start=(t == 0), stop=end)
                    op.then_inc(used, 1)

                pe.wait_ge(set_up, 3)
                pe.wait_ge(loaded[0], 16 * LOADS)
                for n in range(NU):
                    unit(0, 0, n)

                def body(g, j, p, more):
                    n = 0
                    if more:
                        pe.wait_ge(loaded[1 - p], 16 * LOADS * (j + p + 1))
                    for s in range(NS):
                        goal = NU * (s + 1) // NS if more else 0
                        for i in range(G4):
                            scores(g, p, s, i)
                            if n < goal:
                                unit(g + 1, 1 - p, n)
                                n += 1
                        if s:
                            values(g, p, s - 1)
                        while n < goal:
                            unit(g + 1, 1 - p, n)
                            n += 1
                    values(g, p, NS - 1)
                groups(pe, body)

            @block.scalar
            def _(act):
                def take_out(g, c):
                    s_last = sum((cc + 1) * CH // P for cc in range(c + 1))
                    act.wait_ge(used, g * NS + s_last)
                    wait(act, full_ready, 2 * g + c)
                    nc.scalar.activation(out_sb[:, c, :], k.psum[:, OUT, :], ACT.Copy).then_inc(out_read, 1)
                    nc.scalar.activation(sum_sb[:, :], k.psum[:, SUM, :], ACT.Copy).then_inc(out_read, 1)

                def body(g, j, p, more):
                    for s in range(NS):
                        skip = block_rows(STEPS2[s])
                        for i in range(G4):
                            n = g * ITEMS + s * G4 + i
                            act.wait_ge(scored, n + 1)
                            if not (isinstance(g, int) and g == 0 and s < 2):
                                act.wait_ge(used, g * NS + s - 1)
                            nc.scalar.activation(probs[:, (s * G4 + i) % PROBS, 0:CH - skip],
                                                 k.psum[:, i, 0:CH - skip], ACT.Exp).then_inc(exped, 1)
                        if s == CH // P:
                            take_out(g, 0)
                    take_out(g, 1)
                groups(act, body)

            @block.vector
            def _(dve):
                for p in range(2):
                    nc.vector.memset(qs[3 * HD:ALL_ROWS, p, :, :].bitcast(F32), 1.0)
                    nc.vector.memset(ks[3 * HD:ALL_ROWS, p, :, :].bitcast(F32), 1.0).then_inc(set_up, 1)
                nc.vector.memset(max_rows[:, :, :, :].bitcast(F32), 1.0)
                nc.vector.memset(ones[:, :], 1.0).then_inc(set_up, 1)
                dve.wait_ge(set_up, 3)

                def unit(g, p, n):
                    what = UNITS[n]
                    dve.wait_ge(unit_done, NU * g + n + 1)
                    bank = k.psum[:, unit_bank(n), :]
                    if what[0] == "v":
                        wait(dve, used, NS * (g - 1))
                        nc.vector.tensor_copy(v[:, p, 4 * what[1]:4 * what[1] + 4, :].rearrange("p t c -> p (t c)"),
                                              bank).then_inc(unit_read, 1)
                        return
                    i = what[1]
                    if what[0] == "m":
                        cols = slice(what[2] * CH, (what[2] + 1) * CH)
                        nc.vector.tensor_copy(qs[3 * HD:ALL_ROWS, p, i, cols], bank[0:4, :]).then_inc(turned_rows, 1)
                        dve.wait_ge(turned_rows, 2 * (G4 * g + i) + what[2] + 1)
                        dve.sem_inc(unit_read, 1)
                        return
                    t, a = what[2]
                    width = min(CH, (t + 1) * P - a)
                    at = MAX_AT[what[2]]
                    nc.vector.reduce_max(part_max[:, i % 2, at:at + 1], bank[:, 0:width], AX.X,
                                         negate=True).then_inc(unit_read, 1)
                    if what[2] != UNITS_HEAD[-1]:
                        return
                    dve.wait_ge(unit_read, NU * g + n + 1)
                    wait(dve, turned_rows, 2 * (G4 * g + i - 1))
                    one = CH // P
                    parts = part_max[:, i % 2, one:].rearrange("p (t a) -> p t a", a=2)
                    nc.vector.tensor_copy(neg_max[:, i % 2, 0:one], part_max[:, i % 2, 0:one])
                    nc.vector.tensor_tensor(neg_max[:, i % 2, one:], parts[:, :, 0], parts[:, :, 1],
                                            ALU.min).then_inc(best, 1)
                    dve.wait_ge(best, G4 * g + i + 1)
                    nc.vector.tensor_copy(max_rows[:, i % 2, :, 2], neg_max[:, i % 2, :]).then_inc(split_hi, 1)
                    dve.wait_ge(split_hi, G4 * g + i + 1)
                    nc.vector.tensor_tensor(max_rows[:, i % 2, :, 3], neg_max[:, i % 2, :],
                                            max_rows[:, i % 2, :, 2].bitcast(F32), ALU.subtract).then_inc(split_lo, 1)

                def finish(g, j, c):
                    dve.wait_ge(out_read, 2 * (2 * g + c + 1))
                    nc.vector.reciprocal(inv[:, :], sum_sb[:, :]).then_inc(inv_ready, 1)
                    dve.wait_ge(inv_ready, 2 * g + c + 1)
                    wait(dve, lo_ready, 2 * g + c)
                    nc.vector.tensor_tensor(full[:, :], out_sb[:, c, :], inv[:, :], ALU.mult).then_inc(full_ready, 1)
                    dve.wait_ge(full_ready, 2 * g + c + 1)
                    wait(dve, stored[c], 32 * g)
                    nc.vector.tensor_copy(hi[:, c, :], full[:, :]).then_inc(hi_ready, 1)
                    dve.wait_ge(hi_ready, 2 * g + c + 1)
                    nc.vector.tensor_tensor(lo[:, c, :], full[:, :], hi[:, c, :].bitcast(F32),
                                            ALU.subtract).then_inc(lo_ready, 1)

                for n in range(NU):
                    unit(0, 0, n)

                def body(g, j, p, more):
                    half = NU * (CH // P + 2) // NS
                    if more:
                        for n in range(half):
                            unit(g + 1, 1 - p, n)
                    finish(g, j, 0)
                    if more:
                        for n in range(half, NU):
                            unit(g + 1, 1 - p, n)
                    finish(g, j, 1)
                groups(dve, body)


def out_project(nc, k, wout, bout, x, att_hi, att_lo, x2):
    with ExitStack() as ctx:
        sb = lambda n, shape, dt: ctx.enter_context(nc.sbuf_tensor(f"out_{n}", shape, dt))
        sem = lambda n: ctx.enter_context(nc.semaphore(f"out_{n}"))
        raw = sb("raw", [P, 2, D], F32)
        w_hi = sb("w_hi", [P, KT, D], F32R)
        w_lo = sb("w_lo", [P, KT, D], F32R)
        a_hi = sb("a_hi", [P, 2, HG, CH], F32R)
        a_lo = sb("a_lo", [P, 2, HG, CH], F32R)
        bias = sb("bias", [P, D], F32)
        rows = sb("rows", [P, 2, D], F32)
        y = sb("y", [P, 2, D], F32)
        stats = RowStats(nc, ctx, "out")
        raw_in = [sem(f"raw_in{s}") for s in range(2)]
        rows_in = [sem(f"rows_in{s}") for s in range(2)]
        att_in = [sem(f"att_in{s}") for s in range(2)]
        stored = [sem(f"stored{s}") for s in range(2)]
        bias_in = sem("bias_in")
        hi_ready, lo_ready, summed, biased = sem("hi_ready"), sem("lo_ready"), sem("summed"), sem("biased")
        flat_ready, added = sem("flat_ready"), sem("added")
        TILES = CH // P

        def bank(n):
            return k.psum[:, 2 * n:2 * n + 2, :].rearrange("p a b -> p (a b)")

        with nc.Block() as block:
            @block.sync
            def _(sp):
                sp.dma_start(bias[:, :], bout.partition_broadcast(P)).then_inc(bias_in, 16)

                def load_att(u, s):
                    wait(sp, summed, TILES * (u - 1))
                    for to, src in ((a_hi, att_hi), (a_lo, att_lo)):
                        sp.dma_start(to[:, s, :, :].bitcast(F32), src[u]).then_inc(att_in[s], 16)

                for t in range(KT):
                    wait(sp, lo_ready, t - 1)
                    sp.dma_start(raw[:, t % 2, :], wout[t]).then_inc(raw_in[t % 2], 16)
                    if t == 1:
                        load_att(0, 0)
                load_att(1, 1)

                def body(u):
                    for i in range(TILES):
                        n = u * TILES + i
                        wait(sp, added, n - 1)
                        sp.dma_start(rows[:, i % 2, :], x[n]).then_inc(rows_in[i % 2], 16)
                        if not (isinstance(n, int) and n == 0):
                            sp.wait_ge(added, n)
                            sp.dma_start(x2[n - 1], y[:, (i - 1) % 2, :]).then_inc(stored[(i - 1) % 2], 16)
                tiles(sp, 1, body)
                for u in range(1, NCH):
                    if u + 1 < NCH:
                        load_att(u + 1, (u + 1) % 2)
                    body(u)
                sp.wait_ge(added, NT)
                sp.dma_start(x2[NT - 1], y[:, (NT - 1) % 2, :]).then_inc(stored[(NT - 1) % 2], 16)
                for s in range(2):
                    sp.wait_ge(stored[s], 16 * NT // 2)

            @block.scalar
            def _(act):
                for t in range(KT):
                    act.wait_ge(raw_in[t % 2], 16 * (t // 2 + 1))
                    nc.scalar.activation(w_hi[:, t, :], raw[:, t % 2, :], ACT.Copy).then_inc(hi_ready, 1)

            @block.gpsimd
            def _(pool):
                def body(j):
                    for p in range(2):
                        stats.invert(pool, j * 2 + p, p)
                tiles(pool, NT // 2, body)

            @block.tensor
            def _(pe):
                pe.wait_ge(lo_ready, KT)

                def body(u, s, uses):
                    pe.wait_ge(att_in[s], 32 * (uses + 1))
                    for i in range(TILES):
                        n = u * TILES + i
                        wait(pe, biased, 2 * (n - 1))
                        for h in range(2):
                            cols = slice(h * CH, (h + 1) * CH)
                            terms = [(a, w, t) for t in range(KT) for a, w in ((a_hi, w_hi), (a_hi, w_lo), (a_lo, w_hi))]
                            for m, (a, w, t) in enumerate(terms):
                                op = nc.tensor.matmul(k.psum[:, 2 * (i % 2) + h, :], a[:, s, t, i * P:(i + 1) * P],
                                                      w[:, t, cols], start=(m == 0), stop=(m == len(terms) - 1))
                        op.then_inc(summed, 1)
                for u in range(NCH):
                    body(u, u % 2, u // 2)

            @block.vector
            def _(dve):
                stats.start(dve)
                for t in range(KT):
                    dve.wait_ge(hi_ready, t + 1)
                    nc.vector.tensor_tensor(w_lo[:, t, :], raw[:, t % 2, :], w_hi[:, t, :].bitcast(F32),
                                            ALU.subtract).then_inc(lo_ready, 1)
                dve.wait_ge(bias_in, 16)

                def body(j):
                    for p in range(2):
                        n = j * 2 + p
                        dve.wait_ge(summed, n + 1)
                        wait(dve, stored[p], 16 * j)
                        for h in range(2):
                            cols = slice(h * CH, (h + 1) * CH)
                            nc.vector.tensor_tensor(y[:, p, cols], k.psum[:, 2 * p + h, :], bias[:, cols],
                                                    ALU.add).then_inc(biased, 1)
                        dve.wait_ge(biased, 2 * (n + 1))
                        wait(dve, flat_ready, n - 1)
                        stats.moments(dve, n, p, [y[:, p, h * CH:(h + 1) * CH] for h in range(2)])
                        stats.normalise(dve, n, p, y[:, p, :], y[:, p, :]).then_inc(flat_ready, 1)
                        dve.wait_ge(flat_ready, n + 1)
                        dve.wait_ge(rows_in[p], 16 * (j + 1))
                        nc.vector.tensor_tensor(y[:, p, :], y[:, p, :], rows[:, p, :], ALU.add).then_inc(added, 1)
                tiles(dve, NT // 2, body)


def gate_up(nc, k, w12, xt_hi, xt_lo, h_hi, h_lo):
    with ExitStack() as ctx:
        sb = lambda n, shape, dt: ctx.enter_context(nc.sbuf_tensor(f"gu_{n}", shape, dt))
        sem = lambda n: ctx.enter_context(nc.semaphore(f"gu_{n}"))
        w_hi = sb("w_hi", [P, 2, 2, KT, P], F32R)
        w_lo = sb("w_lo", [P, 2, 2, KT, P], F32R)
        act_gate = sb("act_gate", [P, 2, CH], F32)
        full = sb("full", [P, CH], F32)
        hi = sb("hi", [P, 2, CH], F32R)
        lo = sb("lo", [P, 2, CH], F32R)
        nf4 = Nf4(nc, ctx, "w12", 1, 3)
        turned, hi_ready, lo_ready = sem("turned"), sem("w_hi_ready"), sem("w_lo_ready")
        summed, gated, multiplied = sem("summed"), sem("gated"), sem("multiplied")
        h_hi_ready, h_lo_ready = sem("h_hi_ready"), sem("h_lo_ready")
        stored = [sem(f"stored{s}") for s in range(2)]
        GATE, UP, TURN = 0, 2, 4

        def turn_banks(u):
            return k.psum[:, TURN + 2 * u:TURN + 2 * u + 2, :].rearrange("p a b -> p (a b)")

        def last(t):
            return isinstance(t, int) and t >= FT - 1

        def steps(eng, body):
            def two(j):
                for q in range(2):
                    body(j * 2 + q, j, q)
            tiles(eng, FT // 2, two, last=1)

        with nc.Block() as block:
            @block.sync
            def _(sp):
                nf4.load(sp, 0, 0, 0, w12[0])
                nf4.load(sp, 1, 0, 1, w12[1])
                nf4.load(sp, 2, 1, 0, w12[2])
                nf4.load(sp, 3, 1, 1, w12[3])

                def body(t, j, q):
                    for c in range(NCH):
                        sp.wait_ge(h_lo_ready, t * NCH + c + 1)
                        cols = slice(c * CH, (c + 1) * CH)
                        for to, src in ((h_hi, hi), (h_lo, lo)):
                            sp.dma_start(to[t][:, cols], src[:, c % 2, :].bitcast(F32)).then_inc(stored[c % 2], 16)
                        if c in (0, 2) and not (isinstance(t, int) and t >= FT - 2):
                            u = c // 2
                            nf4.load(sp, 2 * t + 4 + u, t + 2, u, w12[2 * t + 4 + u])
                steps(sp, body)
                for s in range(2):
                    sp.wait_ge(stored[s], 32 * 2 * FT)

            def high(act, n, q, u):
                act.wait_ge(turned, n + 1)
                wait(act, summed, 2 * NCH * ((n - u) // 2 - 1) if isinstance(n, int) else 0)
                nc.scalar.activation(w_hi[:, q, u], turn_banks(u).rearrange("p (k h) -> p k h", h=P),
                                     ACT.Copy).then_inc(hi_ready, 1)

            @block.scalar
            def _(act):
                for u in range(2):
                    for i in range(NQ):
                        nf4.make_sign(act, u, u, i)
                for u in range(2):
                    high(act, u, 0, u)

                def body(t, j, q):
                    for c in range(NCH):
                        n = t * NCH + c
                        u = c // 2
                        if not last(t):
                            for i in (range(0, 8) if c % 2 == 0 else range(8, NQ)):
                                nf4.make_sign(act, 2 * t + 2 + u, u, i)
                        act.wait_ge(summed, 2 * n + 1)
                        wait(act, multiplied, n - 1)
                        nc.scalar.activation(act_gate[:, c % 2, :], k.psum[:, GATE + c % 2, :], ACT.Silu).then_inc(gated, 1)
                    if not last(t):
                        for u in range(2):
                            act.wait_ge(turned, 2 * t + 2 + u + 1)
                            wait(act, summed, 2 * NCH * t)
                            nc.scalar.activation(w_hi[:, 1 - q, u], turn_banks(u).rearrange("p (k h) -> p k h", h=P),
                                                 ACT.Copy).then_inc(hi_ready, 1)
                steps(act, body)

            @block.tensor
            def _(pe):
                def turn(n, u):
                    pe.wait_ge(nf4.dq_ready, n + 1)
                    wait(pe, lo_ready, n - 1)
                    for t in range(KT):
                        op = nc.tensor.transpose(turn_banks(u)[:, t * P:(t + 1) * P], nf4.dq[:, 0, t * P:(t + 1) * P],
                                                 k.ident[:, :])
                    op.then_inc(turned, 1)

                turn(0, 0)
                turn(1, 1)

                def body(t, j, q):
                    pe.wait_ge(lo_ready, 2 * t + 2)
                    for c in range(NCH):
                        cols = slice(c * CH, (c + 1) * CH)
                        n = t * NCH + c
                        for u, to, free in ((0, GATE, gated), (1, UP, multiplied)):
                            wait(pe, free, n - 1)
                            terms = [(w, x, m) for m in range(KT)
                                     for w, x in ((w_hi, xt_hi), (w_hi, xt_lo), (w_lo, xt_hi))]
                            for i, (w, x, m) in enumerate(terms):
                                op = nc.tensor.matmul(k.psum[:, to + c % 2, :], w[:, q, u, m, :], x[:, m, cols],
                                                      start=(i == 0), stop=(i == len(terms) - 1))
                            op.then_inc(summed, 1)
                        if c == 2 and not last(t):
                            turn(2 * t + 2, 0)
                    if not last(t):
                        turn(2 * t + 3, 1)
                steps(pe, body)

            @block.vector
            def _(dve):
                nf4.biases(dve)

                def low(n, q, u):
                    dve.wait_ge(hi_ready, n + 1)
                    nc.vector.tensor_tensor(w_lo[:, q, u], turn_banks(u).rearrange("p (k h) -> p k h", h=P),
                                            w_hi[:, q, u].bitcast(F32), ALU.subtract).then_inc(lo_ready, 1)

                def finish(n, u):
                    wait(dve, turned, n)
                    nf4.finish(dve, n, u)

                nf4.prepare(dve, 0, 0, 0)
                nf4.prepare(dve, 1, 0, 1)
                for n in range(2):
                    for i in range(NQ):
                        nf4.take(dve, n, i)
                    finish(n, n)
                    nf4.prepare(dve, n + 2, 1, n)
                for u in range(2):
                    low(u, 0, u)

                def product(t, q, c):
                    n = t * NCH + c
                    dve.wait_ge(summed, 2 * (n + 1))
                    dve.wait_ge(gated, n + 1)
                    wait(dve, h_lo_ready, n)
                    nc.vector.tensor_tensor(full[:, :], act_gate[:, c % 2, :], k.psum[:, UP + c % 2, :],
                                            ALU.mult).then_inc(multiplied, 1)
                    dve.wait_ge(multiplied, n + 1)
                    wait(dve, stored[c % 2], 32 * (t * 2 + c // 2))
                    nc.vector.tensor_copy(hi[:, c % 2, :], full[:, :]).then_inc(h_hi_ready, 1)
                    dve.wait_ge(h_hi_ready, n + 1)
                    nc.vector.tensor_tensor(lo[:, c % 2, :], full[:, :], hi[:, c % 2, :].bitcast(F32),
                                            ALU.subtract).then_inc(h_lo_ready, 1)

                def body(t, j, q):
                    for c in range(NCH):
                        u = c // 2
                        if not last(t):
                            for i in (range(0, 8) if c % 2 == 0 else range(8, NQ)):
                                nf4.take(dve, 2 * t + 2 + u, i)
                            if c % 2:
                                finish(2 * t + 2 + u, u)
                        product(t, q, c)
                        if c % 2 and not (isinstance(t, int) and t >= FT - 2):
                            nf4.prepare(dve, 2 * t + 4 + u, t + 2, u)
                    if not last(t):
                        for u in range(2):
                            low(2 * t + 2 + u, 1 - q, u)
                steps(dve, body)


def down(nc, k, dq3, h_hi, h_lo, x2, partial, out):
    HALF = FT // 2
    with ExitStack() as ctx:
        sb = lambda n, shape, dt: ctx.enter_context(nc.sbuf_tensor(f"down_{n}", shape, dt))
        sem = lambda n: ctx.enter_context(nc.semaphore(f"down_{n}"))
        w_hi = sb("w_hi", [P, HALF, D], F32R)
        w_lo = sb("w_lo", [P, HALF, D], F32R)
        dq = sb("dq", [P, 2, D], F32)
        a_hi = sb("a_hi", [P, 2, HALF, P], F32R)
        a_lo = sb("a_lo", [P, 2, HALF, P], F32R)
        rows = sb("rows", [P, 2, D], F32)
        before = sb("before", [P, 2, D], F32)
        y = sb("y", [P, 2, D], F32)
        stats = RowStats(nc, ctx, "down")
        dq_in = [sem(f"dq_in{s}") for s in range(2)]
        a_in = [sem(f"a_in{s}") for s in range(2)]
        rows_in = [sem(f"rows_in{s}") for s in range(2)]
        stored = [sem(f"stored{s}") for s in range(2)]
        kept = [sem(f"kept{s}") for s in range(2)]
        turned, hi_ready, lo_ready, summed = sem("turned"), sem("hi_ready"), sem("lo_ready"), sem("summed")
        taken, flat_ready, added = sem("taken"), sem("flat_ready"), sem("added")

        def acc_bank(p):
            return k.psum[:, 2 * p:2 * p + 2, :].rearrange("p a b -> p (a b)")

        def turn_bank(p):
            return k.psum[:, 4 + 2 * p:6 + 2 * p, :].rearrange("p a b -> p (a b)")

        with nc.Block() as block:
            @block.sync
            def _(sp):
                def load(m, n, j, p):
                    done = m * NT + n
                    wait(sp, summed, done - 1)
                    for to, src in ((a_hi, h_hi), (a_lo, h_lo)):
                        cols = bass.ds(n * P, P)
                        sp.dma_start(to[:, p].bitcast(F32),
                                     src[m * HALF:(m + 1) * HALF, :, cols].rearrange("t p c -> p t c")).then_inc(a_in[p], 16)

                def weights(m):
                    for t in range(HALF):
                        c = m * HALF + t
                        wait(sp, turned, c - 1)
                        sp.dma_start(dq[:, c % 2, :], dq3[c]).then_inc(dq_in[c % 2], 16)

                load(0, 0, 0, 0)
                weights(0)

                def first(j):
                    for p in range(2):
                        n = j * 2 + p
                        if not (isinstance(n, int) and n == NT - 1):
                            load(0, n + 1, j + p, 1 - p)
                        sp.wait_ge(taken, n + 1)
                        sp.dma_start(partial[n], y[:, p, :]).then_inc(kept[p], 16)
                tiles(sp, NT // 2, first, last=1)
                load(1, 0, 0, 0)
                weights(1)
                for s in range(2):
                    sp.wait_ge(kept[s], 16 * NT // 2)

                def rest(n, j, p):
                    wait(sp, added, n - 1)
                    sp.dma_start(before[:, p, :], partial[n]).then_inc(rows_in[p], 16)
                    sp.dma_start(rows[:, p, :], x2[n]).then_inc(rows_in[p], 16)
                rest(0, 0, 0)

                def second(j):
                    for p in range(2):
                        n = j * 2 + p
                        if not (isinstance(n, int) and n == NT - 1):
                            load(1, n + 1, j + p, 1 - p)
                            rest(n + 1, j + p, 1 - p)
                        sp.wait_ge(added, n + 1)
                        sp.dma_start(out[n], y[:, p, :]).then_inc(stored[p], 16)
                tiles(sp, NT // 2, second, last=1)
                for s in range(2):
                    sp.wait_ge(stored[s], 16 * NT // 2)

            @block.scalar
            def _(act):
                def weights(m):
                    wait(act, summed, m * NT)
                    for t in range(HALF):
                        c = m * HALF + t
                        act.wait_ge(turned, c + 1)
                        nc.scalar.activation(w_hi[:, t, :], turn_bank(c % 2), ACT.Copy).then_inc(hi_ready, 1)
                weights(0)

                def first(j):
                    for p in range(2):
                        n = j * 2 + p
                        act.wait_ge(summed, n + 1)
                        wait(act, kept[p], 16 * j)
                        nc.scalar.activation(y[:, p, :], acc_bank(p), ACT.Copy).then_inc(taken, 1)
                tiles(act, NT // 2, first)
                weights(1)

            @block.gpsimd
            def _(pool):
                def body(j):
                    for p in range(2):
                        stats.invert(pool, j * 2 + p, p)
                tiles(pool, NT // 2, body)

            @block.tensor
            def _(pe):
                def weights(m):
                    for t in range(HALF):
                        c = m * HALF + t
                        pe.wait_ge(dq_in[c % 2], 16 * (c // 2 + 1))
                        wait(pe, lo_ready, c - 1)
                        for b in range(KT):
                            op = nc.tensor.transpose(turn_bank(c % 2)[:, b * P:(b + 1) * P],
                                                     dq[:, c % 2, b * P:(b + 1) * P], k.ident[:, :])
                        op.then_inc(turned, 1)
                    pe.wait_ge(lo_ready, (m + 1) * HALF)

                def half(m):
                    def body(j):
                        for p in range(2):
                            n = j * 2 + p
                            pe.wait_ge(a_in[p], 32 * (m * NT // 2 + j + 1))
                            wait(pe, taken, m * NT + n - 1)
                            for h in range(2):
                                cols = slice(h * CH, (h + 1) * CH)
                                terms = [(a, w, t) for t in range(HALF)
                                         for a, w in ((a_hi, w_hi), (a_hi, w_lo), (a_lo, w_hi))]
                                for i, (a, w, t) in enumerate(terms):
                                    op = nc.tensor.matmul(k.psum[:, 2 * p + h, :], a[:, p, t, :], w[:, t, cols],
                                                          start=(i == 0), stop=(i == len(terms) - 1))
                            op.then_inc(summed, 1)
                    tiles(pe, NT // 2, body)
                weights(0)
                half(0)
                weights(1)
                half(1)

            @block.vector
            def _(dve):
                stats.start(dve)

                def weights(m):
                    for t in range(HALF):
                        c = m * HALF + t
                        dve.wait_ge(hi_ready, c + 1)
                        nc.vector.tensor_tensor(w_lo[:, t, :], turn_bank(c % 2), w_hi[:, t, :].bitcast(F32),
                                                ALU.subtract).then_inc(lo_ready, 1)
                weights(0)
                weights(1)
                for s in range(2):
                    dve.wait_ge(kept[s], 16 * NT // 2)

                def body(j):
                    for p in range(2):
                        n = j * 2 + p
                        dve.wait_ge(summed, NT + n + 1)
                        dve.wait_ge(rows_in[p], 32 * (j + 1))
                        wait(dve, stored[p], 16 * j)
                        nc.vector.tensor_tensor(y[:, p, :], acc_bank(p), before[:, p, :], ALU.add).then_inc(taken, 1)
                        dve.wait_ge(taken, NT + n + 1)
                        wait(dve, flat_ready, n - 1)
                        stats.moments(dve, n, p, [y[:, p, h * CH:(h + 1) * CH] for h in range(2)])
                        stats.normalise(dve, n, p, y[:, p, :], y[:, p, :]).then_inc(flat_ready, 1)
                        dve.wait_ge(flat_ready, n + 1)
                        nc.vector.tensor_tensor(y[:, p, :], y[:, p, :], rows[:, p, :], ALU.add).then_inc(added, 1)
                tiles(dve, NT // 2, body)


class Shared:
    pass


SCRATCH = "Internal"


def block_kernel(nc, x, wqkv, bqkv, wout, bout, w12, w3, slopes, out, phases=None):
    scratch = lambda name, shape: nc.dram_tensor(name, shape, F32, kind=SCRATCH).ap()
    q_hi, q_lo, k_hi, k_lo, v_all = (scratch(n, (GROUPS, P, S)) for n in ("q_hi", "q_lo", "k_hi", "k_lo", "v_all"))
    alibi = scratch("alibi", (GROUPS, 2, G4, S))
    att_hi, att_lo = (scratch(n, (GROUPS, S // CH, P, CH)) for n in ("att_hi", "att_lo"))
    x2, partial = scratch("x2", (NT, P, D)), scratch("partial", (NT, P, D))
    dq3 = scratch("dq3", (FT, P, D))
    h_hi, h_lo = scratch("h_hi", (FT, P, TOK)), scratch("h_lo", (FT, P, TOK))
    with ExitStack() as ctx:
        k = Shared()
        k.psum = ctx.enter_context(nc.psum_tensor("psum", [P, 8, CH], F32))
        k.ident = ctx.enter_context(nc.sbuf_tensor("ident", [P, P], F32))
        k.ident16 = ctx.enter_context(nc.sbuf_tensor("ident16", [P, P], BF16))
        k.mask_q = ctx.enter_context(nc.sbuf_tensor("mask_q", [P, P], BF16))
        k.mask_k = ctx.enter_context(nc.sbuf_tensor("mask_k", [P, P], BF16))
        constants(nc, k, slopes, alibi)
        with ExitStack() as part:
            xt_hi = part.enter_context(nc.sbuf_tensor("xt_hi", [P, KT, TOK], F32R))
            xt_lo = part.enter_context(nc.sbuf_tensor("xt_lo", [P, KT, TOK], F32R))
            normalise(nc, k, "ln1", x, xt_hi, xt_lo)
            qkv(nc, k, wqkv, bqkv, w3, xt_hi, xt_lo, q_hi, q_lo, k_hi, k_lo, v_all, dq3)
        if phases and phases < 2:
            return
        attention(nc, k, q_hi, q_lo, k_hi, k_lo, v_all, alibi, att_hi, att_lo)
        chunked = [[a[b * HG:(b + 1) * HG, c].rearrange("g p t -> p g t") for b in range(B) for c in range(S // CH)]
                   for a in (att_hi, att_lo)]
        if phases and phases < 3:
            return
        out_project(nc, k, wout, bout, x, chunked[0], chunked[1], x2)
        if phases and phases < 4:
            return
        with ExitStack() as part:
            xt_hi = part.enter_context(nc.sbuf_tensor("xt2_hi", [P, KT, TOK], F32R))
            xt_lo = part.enter_context(nc.sbuf_tensor("xt2_lo", [P, KT, TOK], F32R))
            normalise(nc, k, "ln2", x2, xt_hi, xt_lo)
            gate_up(nc, k, w12, xt_hi, xt_lo, h_hi, h_lo)
        if phases and phases < 5:
            return
        down(nc, k, dq3, h_hi, h_lo, x2, partial, out)


def kernel(**inputs):
    import numpy as np
    import concourse.bacc as bacc
    from concourse.bass_utils import run_bass_kernel_spmd

    get = lambda n: np.asarray(inputs[n])
    pad = FT * P - F
    tiled = {
        "x": get("L0_attn_x").reshape(NT, P, D),
        "wqkv": get("L0_attn_w_qkv").reshape(3 * KT, P, KT, P).transpose(0, 3, 2, 1),
        "bqkv": get("L0_attn_b_qkv").reshape(3 * KT, P).T,
        "wout": get("L0_attn_w_out").T.reshape(KT, P, D),
        "bout": get("L0_attn_b_out"),
        "w12": np.stack([np.pad(get(n), ((0, pad), (0, 0))).reshape(FT, P, D) for n in ("L0_ffn_w1", "L0_ffn_w2")],
                        axis=1).reshape(2 * FT, P, D),
        "w3": np.pad(get("L0_ffn_w3"), ((0, 0), (0, pad))).reshape(KT, P, FT, P).transpose(2, 1, 0, 3).reshape(FT, P, D),
        "slopes": (np.float32(1.0) / np.power(np.float32(2.0), np.arange(1, HEADS + 1, dtype=np.float32)
                                              * np.float32(8.0 / HEADS))).reshape(HEADS, 1).astype(np.float32),
    }
    nc = bacc.Bacc("TRN2", target_bir_lowering=False, num_devices=1)
    arrays, args = {}, []
    for name, a in tiled.items():
        a = np.ascontiguousarray(a)
        arrays[f"in_{name}"] = a
        args.append(nc.dram_tensor(f"in_{name}", a.shape, mybir.dt.from_np(a.dtype), kind="ExternalInput").ap())
    out = nc.dram_tensor("result_rows", (NT, P, D), F32, kind="ExternalOutput").ap()
    block_kernel(nc, *args, out)
    r = run_bass_kernel_spmd(nc, [arrays], core_ids=[0])
    return r.results[0]["result_rows"].reshape(B, S, D)
```

```python
import concourse.bass as bass
from concourse import mybir
from contextlib import ExitStack

F32 = mybir.dt.float32
F32R = mybir.dt.float32r
BF16 = mybir.dt.bfloat16
I32 = mybir.dt.int32
ALU = mybir.AluOpType
ACT = mybir.ActivationFunctionType
AX = mybir.AxisListType

P = 128
B, S, D = 2, 1024, 1024
HEADS, HD = 32, 32
F = 2752
TOK = B * S
KT = D // P
FT = -(-F // P)
NT = TOK // P
CH = 512
NCH = TOK // CH
FAST = 256
G4 = P // HD
HG = HEADS // G4
GROUPS = B * HG
QT = S // P
SCALE = HD ** -0.5
EPS = 1e-5
MASKED = -1e30
QB = 64
NB = D // QB

CODE = [-1.0, -0.6961928009986877, -0.5250730514526367, -0.39491748809814453, -0.28444138169288635,
        -0.18477343022823334, -0.09105003625154495, 0.0, 0.07958029955625534, 0.16093020141124725,
        0.24611230194568634, 0.33791524171829224, 0.44070982933044434, 0.5626170039176941,
        0.7229568362236023, 1.0]


def nf4_steps():
    import numpy as np
    code = np.array(CODE, np.float32)
    bounds = (code[:-1] + code[1:]) * np.float32(0.5)
    return [float(b) for b in bounds], [float(c + np.float32(1.0)) for c in code[1:]]


BOUNDS, STEPS = nf4_steps()
NQ = len(BOUNDS)


def wait(eng, sem, value):
    if isinstance(value, int) and value <= 0:
        return
    eng.wait_ge(sem, value)


def wait_apart(eng, sem, value, passed):
    eng.wait_ge(sem, value)
    eng.sem_inc(passed, 1)


def tiles(eng, n, body, first=1, last=0, start=0):
    for j in range(start, start + first):
        body(j)
    if n - last > start + first:
        with eng.Fori(start + first, n - last) as j:
            body(j)
    for j in range(n - last, n):
        body(j)


class Nf4:

    def __init__(self, nc, ctx, name, dq_slots, sign_slots):
        sb = lambda n, shape, dt: ctx.enter_context(nc.sbuf_tensor(f"{name}_{n}", shape, dt))
        sem = lambda n: ctx.enter_context(nc.semaphore(f"{name}_{n}"))
        self.nc = nc
        self.raw = sb("raw", [P, 2, D], F32)
        self.code = sb("code", [P, D], F32)
        self.dq_slots = dq_slots
        self.dq = sb("dq", [P, dq_slots, D], F32)
        assert NQ % sign_slots == 0
        self.sign_slots = sign_slots
        self.sign = sb("sign", [P, sign_slots, D], BF16)
        self.top = sb("top", [P, 2, NB], F32)
        self.safe = sb("safe", [P, 2, NB], F32)
        self.inv = sb("inv", [P, 2, NB], F32)
        self.bias = sb("bias", [P, NQ], F32)
        self.bias_ready = sem("bias_ready")
        self.loaded = [sem(f"loaded{s}") for s in range(2)]
        self.top_ready = sem("top_ready")
        self.safe_ready = sem("safe_ready")
        self.inv_ready = sem("inv_ready")
        self.scaled = sem("scaled")
        self.signs = sem("signs")
        self.coded = sem("coded")
        self.dq_ready = sem("dq_ready")

    def load(self, sp, n, j, p, src):
        wait(sp, self.signs, NQ * (n - 1))
        sp.dma_start(self.raw[:, p, :], src).then_inc(self.loaded[p], 16)

    def biases(self, dve):
        for i in range(NQ):
            self.nc.vector.memset(self.bias[:, i:i + 1], -BOUNDS[i]).then_inc(self.bias_ready, 1)

    def prepare(self, dve, n, j, p):
        nc = self.nc
        blocks = self.raw[:, p, :].rearrange("p (b k) -> p b k", k=QB)
        dve.wait_ge(self.loaded[p], 16 * (j + 1))
        wait(dve, self.dq_ready, n - 1)
        nc.vector.reduce_max(self.top[:, p, :], blocks, AX.X, apply_absolute_value=True).then_inc(self.top_ready, 1)
        dve.wait_ge(self.top_ready, n + 1)
        nc.vector.scalar_tensor_tensor(out=self.safe[:, p, :], in0=self.top[:, p, :], scalar=0.0,
                                       in1=self.top[:, p, :], op0=ALU.is_equal, op1=ALU.add).then_inc(self.safe_ready, 1)
        dve.wait_ge(self.safe_ready, n + 1)
        nc.vector.reciprocal(self.inv[:, p, :], self.safe[:, p, :]).then_inc(self.inv_ready, 1)
        dve.wait_ge(self.inv_ready, n + 1)
        inv = self.inv[:, p, :].unsqueeze(2).broadcast_to([P, NB, QB])
        nc.vector.tensor_tensor(blocks, blocks, inv, ALU.mult).then_inc(self.scaled, 1)

    def make_sign(self, act, n, p, i):
        if i == 0:
            act.wait_ge(self.scaled, n + 1)
            act.wait_ge(self.bias_ready, NQ)
        wait(act, self.coded, 2 * (NQ * n + i - self.sign_slots + 1))
        self.nc.scalar.activation(self.sign[:, i % self.sign_slots, :], self.raw[:, p, :], ACT.Sign,
                                  bias=self.bias[:, i:i + 1]).then_inc(self.signs, 1)

    def take(self, dve, n, i):
        nc = self.nc
        dve.wait_ge(self.signs, NQ * n + i + 1)
        for h in range(2):
            half = slice(h * D // 2, (h + 1) * D // 2)
            sign = self.sign[:, i % self.sign_slots, half]
            if i == 0:
                wait(dve, self.dq_ready, n)
                op = nc.vector.tensor_scalar(self.code[:, half], sign, STEPS[0], 0.0, ALU.mult, ALU.max)
            else:
                dve.wait_ge(self.coded, 2 * (NQ * n + i) + h - 1)
                op = nc.vector.scalar_tensor_tensor(out=self.code[:, half], in0=sign, scalar=STEPS[i],
                                                    in1=self.code[:, half], op0=ALU.mult, op1=ALU.max)
            op.then_inc(self.coded, 1)

    def finish(self, dve, n, p):
        dve.wait_ge(self.coded, 2 * NQ * (n + 1))
        top = self.top[:, p, :].unsqueeze(2).broadcast_to([P, NB, QB])
        out = self.dq[:, p % self.dq_slots, :].rearrange("p (b k) -> p b k", k=QB)
        self.nc.vector.scalar_tensor_tensor(out=out, in0=self.code[:, :].rearrange("p (b k) -> p b k", k=QB),
                                            scalar=-1.0, in1=top, op0=ALU.add, op1=ALU.mult).then_inc(self.dq_ready, 1)


class RowStats:

    def __init__(self, nc, ctx, name):
        sb = lambda n, shape: ctx.enter_context(nc.sbuf_tensor(f"{name}_{n}", shape, F32))
        sem = lambda n: ctx.enter_context(nc.semaphore(f"{name}_{n}"))
        self.nc = nc
        self.parts = sb("parts", [P, 2, 6])
        self.mv = sb("mv", [P, 2, 2])
        self.var_eps = sb("var_eps", [P, 2])
        self.rstd = sb("rstd", [P, 2])
        self.eps = sb("eps", [P, 1])
        self.power = sb("power", [P, 1])
        self.eps_ready = sem("eps_ready")
        self.parts_ready = sem("parts_ready")
        self.passed = sem("passed")
        self.mv_ready = sem("mv_ready")
        self.var_ready = sem("var_ready")
        self.rstd_ready = sem("rstd_ready")

    def start(self, dve):
        self.nc.vector.memset(self.power[:, :], -0.5).then_inc(self.eps_ready, 1)
        self.nc.vector.memset(self.eps[:, :], EPS).then_inc(self.eps_ready, 1)

    def moments(self, dve, n, p, halves):
        nc = self.nc
        wait(dve, self.mv_ready, n)
        for h in range(2):
            nc.vector.bn_stats(self.parts[:, h, :], halves[h]).then_inc(self.parts_ready, 1)
        wait_apart(dve, self.parts_ready, 2 * n + 2, self.passed)
        nc.vector.bn_aggr(self.mv[:, p, :], self.parts[:, :, :]).then_inc(self.mv_ready, 1)

    def invert(self, pool, n, p):
        if isinstance(n, int) and n == 0:
            pool.wait_ge(self.eps_ready, 2)
        pool.wait_ge(self.mv_ready, n + 1)
        self.nc.gpsimd.tensor_tensor(self.var_eps[:, p:p + 1], self.mv[:, p, 1:2], self.eps[:, :],
                                     ALU.add).then_inc(self.var_ready, 1)
        pool.wait_ge(self.var_ready, n + 1)
        self.nc.gpsimd.tensor_tensor(self.rstd[:, p:p + 1], self.var_eps[:, p:p + 1], self.power[:, :],
                                     ALU.pow).then_inc(self.rstd_ready, 1)

    def normalise(self, dve, n, p, out, rows):
        dve.wait_ge(self.rstd_ready, n + 1)
        return self.nc.vector.tensor_scalar(out, rows, self.mv[:, p, 0:1], self.rstd[:, p:p + 1],
                                            ALU.subtract, ALU.mult)


def constants(nc, k, slopes, alibi):
    with ExitStack() as ctx:
        sb = lambda n, shape, dt: ctx.enter_context(nc.sbuf_tensor(n, shape, dt))
        sem = lambda n: ctx.enter_context(nc.semaphore(n))
        where = sb("position_int", [HEADS, S], I32)
        position = sb("position", [HEADS, S], F32)
        slope = sb("slope", [HEADS, 1], F32)
        full = sb("alibi_full", [HEADS, S], F32)
        part = sb("alibi_parts", [HEADS, 2, S], F32R)
        zeroed, made, slope_in, stored = sem("c_zeroed"), sem("c_made"), sem("c_slope"), sem("c_stored")
        pos_ready, step = sem("c_pos"), sem("c_step")
        with nc.Block() as block:
            @block.sync
            def _(sp):
                sp.dma_start(slope[:, :], slopes).then_inc(slope_in, 16)
                sp.wait_ge(step, 4)
                for b in range(B):
                    for g in range(HG):
                        src = part[g * G4:(g + 1) * G4, :, :].bitcast(F32)
                        sp.dma_start(alibi[b * HG + g].rearrange("c i t -> i c t"), src).then_inc(stored, 16)
                sp.wait_ge(stored, 16 * GROUPS)

            @block.gpsimd
            def _(pool):
                nc.gpsimd.iota(where[:, :], [[1, S]], base=1 - S, channel_multiplier=0).then_inc(pos_ready, 1)
                for m in (k.ident, k.ident16, k.mask_q, k.mask_k):
                    nc.gpsimd.memset(m[:, :], 0.0).then_inc(zeroed, 1)
                pool.wait_ge(zeroed, 4)
                for m in (k.ident, k.ident16):
                    nc.gpsimd.affine_select(out=m[:, :], in_=m[:, :], compare_op=ALU.not_equal, fill=1.0,
                                            base=0, pattern=[[-1, P]], channel_multiplier=1).then_inc(made, 1)
                nc.gpsimd.affine_select(out=k.mask_q[:, :], in_=k.mask_q[:, :], compare_op=ALU.is_ge, fill=MASKED,
                                        base=0, pattern=[[-1, P]], channel_multiplier=1).then_inc(made, 1)
                nc.gpsimd.affine_select(out=k.mask_k[:, :], in_=k.mask_k[:, :], compare_op=ALU.is_ge, fill=MASKED,
                                        base=0, pattern=[[1, P]], channel_multiplier=-1).then_inc(made, 1)
                pool.wait_ge(made, 4)

            @block.vector
            def _(dve):
                dve.wait_ge(pos_ready, 1)
                nc.vector.tensor_copy(position[:, :], where[:, :]).then_inc(step, 1)
                dve.wait_ge(step, 1)
                dve.wait_ge(slope_in, 16)
                nc.vector.tensor_scalar(full[:, :], position[:, :], slope[:, :], None, ALU.mult).then_inc(step, 1)
                dve.wait_ge(step, 2)
                nc.vector.tensor_copy(part[:, 0, :], full[:, :]).then_inc(step, 1)
                dve.wait_ge(step, 3)
                nc.vector.tensor_tensor(part[:, 1, :], full[:, :], part[:, 0, :].bitcast(F32),
                                        ALU.subtract).then_inc(step, 1)


def normalise(nc, k, name, x, xt_hi, xt_lo):
    with ExitStack() as ctx:
        sb = lambda n, shape, dt: ctx.enter_context(nc.sbuf_tensor(f"{name}_{n}", shape, dt))
        sem = lambda n: ctx.enter_context(nc.semaphore(f"{name}_{n}"))
        SLOTS = 4
        rows = sb("rows", [P, SLOTS, D], F32)
        flat = sb("flat", [P, 2, D], F32)
        stats = RowStats(nc, ctx, name)
        loaded = [sem(f"loaded{s}") for s in range(SLOTS)]
        flat_ready, turned, hi_ready, lo_ready = sem("flat_ready"), sem("turned"), sem("hi_ready"), sem("lo_ready")
        passed = sem("act_passed")

        def bank(p):
            return k.psum[:, 2 * p:2 * p + 2, :].rearrange("p a b -> p (a b)")

        with nc.Block() as block:
            @block.sync
            def _(sp):
                def body(j):
                    for p in range(SLOTS):
                        n = j * SLOTS + p
                        wait(sp, flat_ready, n - SLOTS + 1)
                        sp.dma_start(rows[:, p, :], x[n]).then_inc(loaded[p], 16)
                tiles(sp, NT // SLOTS, body)

            @block.vector
            def _(dve):
                stats.start(dve)

                def low(n, p):
                    dve.wait_ge(hi_ready, n + 1)
                    cols = bass.ds(n * P, P)
                    nc.vector.tensor_tensor(xt_lo[:, :, cols], bank(p).rearrange("p (k t) -> p k t", t=P),
                                            xt_hi[:, :, cols].bitcast(F32), ALU.subtract).then_inc(lo_ready, 1)

                def moments(n, j, s):
                    dve.wait_ge(loaded[s], (j + 1) * 16)
                    wait(dve, flat_ready, n - 1)
                    stats.moments(dve, n, s % 2, [rows[:, s, h * CH:(h + 1) * CH] for h in range(2)])

                moments(0, 0, 0)

                def body(j):
                    for s in range(SLOTS):
                        n = j * SLOTS + s
                        wait(dve, turned, n - 1)
                        stats.normalise(dve, n, s % 2, flat[:, s % 2, :], rows[:, s, :]).then_inc(flat_ready, 1)
                        if not (isinstance(n, int) and n == NT - 1):
                            moments(n + 1, j + (s + 1) // SLOTS, (s + 1) % SLOTS)
                        if not (isinstance(n, int) and n == 0):
                            low(n - 1, 1 - s % 2)
                tiles(dve, NT // SLOTS, body, last=1)
                low(NT - 1, 1)

            @block.tensor
            def _(pe):
                def body(j):
                    for p in range(2):
                        n = j * 2 + p
                        pe.wait_ge(flat_ready, n + 1)
                        wait(pe, lo_ready, n - 1)
                        for t in range(KT):
                            op = nc.tensor.transpose(bank(p)[:, t * P:(t + 1) * P], flat[:, p, t * P:(t + 1) * P],
                                                     k.ident[:, :])
                        op.then_inc(turned, 1)
                tiles(pe, NT // 2, body)

            @block.gpsimd
            def _(pool):
                def body(j):
                    for p in range(2):
                        stats.invert(pool, j * 2 + p, p)
                tiles(pool, NT // 2, body)

            @block.scalar
            def _(act):
                def high(n, p):
                    wait_apart(act, turned, n + 1, passed)
                    nc.scalar.activation(xt_hi[:, :, bass.ds(n * P, P)], bank(p).rearrange("p (k t) -> p k t", t=P),
                                         ACT.Copy).then_inc(hi_ready, 1)

                def body(j):
                    for p in range(2):
                        n = j * 2 + p
                        if not (isinstance(n, int) and n == 0):
                            high(n - 1, 1 - p)
                tiles(act, NT // 2, body)
                high(NT - 1, 1)


def qkv(nc, k, wqkv, bqkv, w3, xt_hi, xt_lo, q_hi, q_lo, k_hi, k_lo, v_all, dq3):
    with ExitStack() as ctx:
        sb = lambda n, shape, dt: ctx.enter_context(nc.sbuf_tensor(f"qkv_{n}", shape, dt))
        sem = lambda n: ctx.enter_context(nc.semaphore(f"qkv_{n}"))
        raw = sb("raw", [P, 2, KT, P], F32)
        w_hi = sb("w_hi", [P, 2, KT, P], F32R)
        w_lo = sb("w_lo", [P, 2, KT, P], F32R)
        bias = sb("bias", [P, 3 * KT], F32)
        bias_q = sb("bias_q", [P, KT], F32)
        full = sb("full", [P, 2, CH], F32)
        hi = sb("hi", [P, 2, CH], F32R)
        lo = sb("lo", [P, 2, CH], F32R)
        nf4 = Nf4(nc, ctx, "w3", 2, 5)
        raw_in = [sem(f"raw_in{s}") for s in range(2)]
        bias_in, bias_ready = sem("bias_in"), sem("bias_ready")
        w_hi_ready, w_lo_ready, summed, full_ready = sem("w_hi_ready"), sem("w_lo_ready"), sem("summed"), sem("full_ready")
        hi_ready, lo_ready, passed = sem("hi_ready"), sem("lo_ready"), sem("act_passed")
        stored = [sem(f"stored{s}") for s in range(2)]
        v_stored = [sem(f"v_stored{s}") for s in range(2)]
        dq_stored = [sem(f"dq_stored{s}") for s in range(2)]
        LAST = 3 * KT
        V0 = 2 * KT

        def kinds(eng, body):
            tiles(eng, KT // 2, lambda j: body(j, 0))
            tiles(eng, KT, lambda j: body(j, 1), first=0, start=KT // 2)
            tiles(eng, 3 * KT // 2, lambda j: body(j, 2), last=2, start=KT)

        def known(n, most):
            return not (isinstance(n, int) and n >= most)

        with nc.Block() as block:
            @block.sync
            def _(sp):
                sp.dma_start(bias[:, :], bqkv).then_inc(bias_in, 16)
                for m in range(2):
                    sp.dma_start(raw[:, m], wqkv[m]).then_inc(raw_in[m], 16)
                    nf4.load(sp, m, 0, m, w3[m])

                def body(j, kind):
                    for p in range(2):
                        m = j * 2 + p
                        if known(m, LAST - 2):
                            sp.wait_ge(w_lo_ready, m + 1)
                            sp.dma_start(raw[:, p], wqkv[m + 2]).then_inc(raw_in[p], 16)
                        if not (isinstance(m, int) and (m == 0 or m > FT)):
                            sp.wait_ge(nf4.dq_ready, m)
                            sp.dma_start(dq3[m - 1], nf4.dq[:, 1 - p, :]).then_inc(dq_stored[1 - p], 16)
                        for c in range(NCH):
                            n = m * NCH + c
                            dst = (m - kind * KT) + (c // 2) * HG
                            cols = slice((c % 2) * CH, (c % 2 + 1) * CH)
                            if kind < 2:
                                sp.wait_ge(lo_ready, n + 1)
                                for to, src in (((q_hi, k_hi)[kind], hi), ((q_lo, k_lo)[kind], lo)):
                                    sp.dma_start(to[dst][:, cols], src[:, c % 2, :].bitcast(F32)).then_inc(stored[c % 2], 16)
                            else:
                                sp.wait_ge(full_ready, n + 1)
                                sp.dma_start(v_all[dst][:, cols], full[:, c % 2, :]).then_inc(v_stored[c % 2], 16)
                            if c == 1 and known(m, FT - 2):
                                nf4.load(sp, m + 2, j + 1, p, w3[m + 2])
                kinds(sp, body)
                for s in range(2):
                    sp.wait_ge(stored[s], 16 * 2 * V0 * 2)
                    sp.wait_ge(v_stored[s], 16 * KT * 2)
                    sp.wait_ge(dq_stored[s], 16 * FT // 2)

            @block.scalar
            def _(act):
                def split(m, j, p):
                    act.wait_ge(raw_in[p], 16 * (j + 1))
                    wait(act, summed, NCH * (m - 1))
                    nc.scalar.activation(w_hi[:, p], raw[:, p], ACT.Copy).then_inc(w_hi_ready, 1)

                split(0, 0, 0)

                def body(j, kind):
                    for p in range(2):
                        m = j * 2 + p
                        if known(m, LAST - 1):
                            split(m + 1, j + p, 1 - p)
                        for c in range(NCH):
                            if known(m, FT):
                                for i in range(4 * c, min(4 * c + 4, NQ)):
                                    nf4.make_sign(act, m, p, i)
                            n = m * NCH + c
                            if c == 0 and p == 0:
                                act.wait_ge(bias_ready, 1)
                            if kind < 2:
                                wait(act, lo_ready, n - 1)
                            else:
                                act.wait_ge(lo_ready, V0 * NCH)
                                wait(act, v_stored[c % 2], 16 * ((m - V0) * 2 + c // 2))
                            wait_apart(act, summed, n + 1, passed)
                            col = bias_q[:, bass.ds(m, 1)] if kind == 0 else bias[:, bass.ds(m, 1)]
                            nc.scalar.activation(full[:, c % 2, :], k.psum[:, c, :], ACT.Identity, bias=col,
                                                 scale=SCALE if kind == 0 else 1.0).then_inc(full_ready, 1)
                kinds(act, body)

            @block.tensor
            def _(pe):
                def body(j, kind):
                    for p in range(2):
                        m = j * 2 + p
                        pe.wait_ge(w_lo_ready, m + 1)
                        for c in range(NCH):
                            wait(pe, full_ready, NCH * (m - 1) + c + 1)
                            cols = slice(c * CH, (c + 1) * CH)
                            terms = [(w, x, t) for t in range(KT) for w, x in ((w_hi, xt_hi), (w_hi, xt_lo), (w_lo, xt_hi))]
                            for i, (w, x, t) in enumerate(terms):
                                op = nc.tensor.matmul(k.psum[:, c, :], w[:, p, t, :], x[:, t, cols],
                                                      start=(i == 0), stop=(i == len(terms) - 1))
                            op.then_inc(summed, 1)
                kinds(pe, body)

            @block.vector
            def _(dve):
                nf4.biases(dve)
                dve.wait_ge(bias_in, 16)
                nc.vector.tensor_scalar(bias_q[:, :], bias[:, 0:KT], SCALE, None, ALU.mult).then_inc(bias_ready, 1)

                def split(m, j, p):
                    dve.wait_ge(w_hi_ready, m + 1)
                    nc.vector.tensor_tensor(w_lo[:, p], raw[:, p], w_hi[:, p].bitcast(F32),
                                            ALU.subtract).then_inc(w_lo_ready, 1)

                split(0, 0, 0)
                nf4.prepare(dve, 0, 0, 0)

                def body(j, kind):
                    for p in range(2):
                        m = j * 2 + p
                        if known(m, LAST - 1):
                            split(m + 1, j + p, 1 - p)
                        if known(m, FT - 1):
                            nf4.prepare(dve, m + 1, j + p, 1 - p)
                        for c in range(NCH):
                            if known(m, FT):
                                for i in range(4 * c, min(4 * c + 4, NQ)):
                                    nf4.take(dve, m, i)
                            if kind < 2:
                                n = m * NCH + c
                                dve.wait_ge(full_ready, n + 1)
                                wait(dve, stored[c % 2], 32 * (m * 2 + c // 2))
                                nc.vector.tensor_copy(hi[:, c % 2, :], full[:, c % 2, :]).then_inc(hi_ready, 1)
                                dve.wait_ge(hi_ready, n + 1)
                                nc.vector.tensor_tensor(lo[:, c % 2, :], full[:, c % 2, :],
                                                        hi[:, c % 2, :].bitcast(F32), ALU.subtract).then_inc(lo_ready, 1)
                        if known(m, FT):
                            wait(dve, dq_stored[p], 16 * j)
                            nf4.finish(dve, m, p)
                kinds(dve, body)


def block_rows(step):
    c, t = step
    return max(0, t * P - c * CH)


STEPS2 = [(c, t) for c in range(S // CH) for t in range((c + 1) * CH // P)]
UNITS_HEAD = [(t, a) for t in range(QT) for a in range(0, (t + 1) * P, CH)]
MAX_AT = {u: n for n, u in enumerate(UNITS_HEAD)}


def first_pass_units():
    units = [("v", 0), ("v", 1)]
    later = []
    for i in range(G4):
        for n, u in enumerate(UNITS_HEAD):
            units.append(("s", i, u))
            if n == 3:
                units += later
                later = []
        later = [("m", i, 0), ("m", i, 1)]
    return units + later


UNITS = first_pass_units()
NU = len(UNITS)
NS = len(STEPS2)
TURN_UNITS = [sum(u[0] != "s" for u in UNITS[:n + 1]) for n in range(NU)]
SCORE_UNITS = [n + 1 - TURN_UNITS[n] + sum(u[0] == "s" and u[2] == UNITS_HEAD[-1] for u in UNITS[:n])
               for n in range(NU)]
FINISH = 6
SQ = 32


def schedule():
    events, n = [], 0
    pieces = [(1, k) for k in range(FINISH)], [(0, k) for k in range(FINISH)]
    for s in range(NS):
        goal = min(NU, NU * (s + 1) // NS + 1)
        for i in range(G4):
            events.append(("scores", s, i))
            if i != 1 and n < goal:
                events.append(("unit", n))
                n += 1
        if s == 0:
            turn = [("values", -1, 0), ("values", -1, 1), ("take", 1)]
        else:
            turn = [("values", s - 1, 0), ("values", s - 1, 1)]
            if s == CH // P:
                turn.append(("take", 0))
        for e in turn:
            events.append(e)
            if e[0] == "values" and n < goal:
                events.append(("unit", n))
                n += 1
            which = pieces[0] if s <= CH // P else pieces[1]
            if e[0] == "values" and s > 0 and s != CH // P + 1 and which:
                events.append(("finish",) + which.pop(0))
        while n < goal:
            events.append(("unit", n))
            n += 1
    assert not pieces[0] and not pieces[1] and n == NU, pieces
    return events


def attention(nc, k, q_hi, q_lo, k_hi, k_lo, v_all, alibi, att_hi, att_lo):
    SUM_ROWS, ALL_ROWS = 3 * HD + 2, 3 * HD + 4
    ITEMS = NS * G4
    PROBS = 8
    SLOTS = 3
    assert ITEMS % PROBS == 0 and NU % 2 == 0
    EVENTS = schedule()
    with ExitStack() as ctx:
        sb = lambda n, shape, dt: ctx.enter_context(nc.sbuf_tensor(f"heads_{n}", shape, dt))
        sem = lambda n: ctx.enter_context(nc.semaphore(f"heads_{n}"))
        qs = sb("qs", [P, SLOTS, G4, S], F32R)
        ks = sb("ks", [P, SLOTS, G4, S], F32R)
        vt = sb("vt", [P, SLOTS, S], F32)
        v = sb("v", [P, SLOTS, QT, P], F32)
        ones = sb("ones", [P, HD], F32)
        probs = sb("probs", [P, PROBS, CH], F32)
        part_max = sb("part_max", [P, 2, len(UNITS_HEAD)], F32)
        neg_max = sb("neg_max", [P, 2, QT], F32)
        max_rows = sb("max_rows", [P, 2, QT, 4], F32R)
        out_sb = sb("out", [P, 2, CH], F32)
        sum_sb = sb("sum", [P, 2, CH], F32)
        turned = sb("turned", [P, CH], F32)
        inv_few = sb("inv_few", [P, CH // SQ], F32)
        inv = sb("inv", [P, CH], F32)
        full = sb("full", [P, CH], F32)
        hi = sb("hi", [P, 2, CH], F32R)
        lo = sb("lo", [P, 2, CH], F32R)
        loaded = [sem(f"loaded{s}") for s in range(SLOTS)]
        stored = [sem(f"stored{s}") for s in range(2)]
        LOADS = 8
        set_up, ks_set = sem("set_up"), sem("ks_set")
        unit_done, max_read, turn_read = sem("unit_done"), sem("max_read"), sem("turn_read")
        split_hi, split_lo = sem("split_hi"), sem("split_lo")
        scored, exped, used = sem("scored"), sem("exped"), sem("used")
        out_read, inv_ready, full_ready = sem("out_read"), sem("inv_ready"), sem("full_ready")
        hi_ready, lo_ready = sem("hi_ready"), sem("lo_ready")
        turned_ready, inverted = sem("turned_ready"), sem("inverted")
        S2_BANKS = 4
        OUT, SUM = 6, 7
        NSC, NTU = G4 * (len(UNITS_HEAD) + 1), TURN_UNITS[-1]

        def unit_bank(n):
            return S2_BANKS + n % 2

        def groups(eng, body):
            def three(j):
                for p in range(SLOTS):
                    body(j * SLOTS + p, j, p, True)
            tiles(eng, GROUPS // SLOTS, three, last=1)
            assert GROUPS % SLOTS == 1
            body(GROUPS - 1, GROUPS // SLOTS, 0, False)

        def first(g):
            return isinstance(g, int) and g == 0

        with nc.Block() as block:
            @block.sync
            def _(sp):
                def load(g, p):
                    wait(sp, scored, ITEMS * (g - SLOTS + 1))
                    for to, rows, src in ((qs, 0, q_hi), (qs, 1, q_hi), (qs, 2, q_lo),
                                          (ks, 0, k_hi), (ks, 1, k_lo), (ks, 2, k_hi)):
                        dst = to[rows * HD:(rows + 1) * HD, p, :, :].bitcast(F32)
                        sp.dma_start(dst, src[g].rearrange("(i r) t -> r i t", r=HD)).then_inc(loaded[p], 16)
                    sp.dma_start(vt[:, p, :], v_all[g]).then_inc(loaded[p], 16)
                    if isinstance(g, int) and g < SLOTS:
                        sp.wait_ge(ks_set, g + 1)
                    sp.dma_start(ks[3 * HD:3 * HD + 2, p, :, :].bitcast(F32), alibi[g]).then_inc(loaded[p], 16)

                def store(g, c):
                    sp.wait_ge(lo_ready, 2 * g + c + 1)
                    for to, src in ((att_hi, hi), (att_lo, lo)):
                        sp.dma_start(to[g, c], src[:, c, :].bitcast(F32)).then_inc(stored[c], 16)

                load(0, 0)
                load(1, 1)

                def body(g, j, p, more):
                    if not (isinstance(g, int) and g >= GROUPS - 2):
                        load(g + 2, (p + 2) % SLOTS)
                    if not first(g):
                        store(g - 1, 1)
                    store(g, 0)
                groups(sp, body)
                store(GROUPS - 1, 1)
                for c in range(2):
                    sp.wait_ge(stored[c], 32 * GROUPS)

            @block.tensor
            def _(pe):
                def unit(g, p, n):
                    what = UNITS[n]
                    if n >= 2:
                        before = (max_read, NSC * g + SCORE_UNITS[n - 2]) if UNITS[n - 2][0] == "s" else \
                                 (turn_read, NTU * g + TURN_UNITS[n - 2])
                    else:
                        assert UNITS[NU - 2][0] == UNITS[NU - 1][0] == "m"
                        before = (turn_read, NTU * (g - 1) + TURN_UNITS[NU - 2 + n])
                    if not (first(g) and n < 2):
                        pe.wait_ge(*before)
                    bank = k.psum[:, unit_bank(n), :]
                    if what[0] == "v":
                        for t in range(4):
                            cols = slice((4 * what[1] + t) * P, (4 * what[1] + t + 1) * P)
                            op = nc.tensor.transpose(bank[:, t * P:(t + 1) * P], vt[:, p, cols], k.ident[:, :])
                    elif what[0] == "m":
                        i = what[1]
                        pe.wait_ge(split_lo, G4 * g + i + 1)
                        for t in range(4):
                            op = nc.tensor.transpose(bank[0:4, t * P:(t + 1) * P],
                                                     max_rows[:, i % 2, 4 * what[2] + t, :].bitcast(F32), k.ident[:, :])
                    else:
                        i, (t, a) = what[1:]
                        width = min(CH, (t + 1) * P - a)
                        last = a + width == (t + 1) * P
                        wide = max(width, FAST)
                        op = nc.tensor.matmul(bank[:, 0:wide], qs[0:SUM_ROWS, p, i, t * P:(t + 1) * P],
                                              ks[0:SUM_ROWS, p, i, a:a + wide], start=True, stop=not last)
                        if last:
                            op = nc.tensor.matmul(bank[:, width - P:width], k.ident16[:, :], k.mask_q[:, :],
                                                  start=False, stop=True)
                    op.then_inc(unit_done, 1)

                def scores(g, p, s, i):
                    c, t = STEPS2[s]
                    n = g * ITEMS + s * G4 + i
                    wait(pe, exped, n - S2_BANKS + 1)
                    if s == 0:
                        pe.wait_ge(turn_read, NTU * g + TURN_UNITS[UNITS.index(("m", i, 1))])
                    skip = block_rows((c, t))
                    wide = min(skip, CH - FAST)
                    diagonal = t * P >= c * CH
                    op = nc.tensor.matmul(k.psum[:, i, wide:CH], ks[0:ALL_ROWS, p, i, t * P:(t + 1) * P],
                                          qs[0:ALL_ROWS, p, i, c * CH + wide:(c + 1) * CH], start=True, stop=not diagonal)
                    if diagonal:
                        op = nc.tensor.matmul(k.psum[:, i, skip:skip + P], k.ident16[:, :], k.mask_k[:, :],
                                              start=False, stop=True)
                    op.then_inc(scored, 1)

                def values(g, p, s, what):
                    c, t = STEPS2[s]
                    if what == 0:
                        if t == 0:
                            wait(pe, out_read, 2 * (2 * g + c))
                        pe.wait_ge(exped, g * ITEMS + (s + 1) * G4)
                    skip = block_rows((c, t))
                    end = t == (c + 1) * CH // P - 1
                    to = (OUT, SUM)[what]
                    for i in range(G4):
                        lhs = v[:, p, t, i * HD:(i + 1) * HD] if to == OUT else ones[:, :]
                        op = nc.tensor.matmul(k.psum[i * HD:(i + 1) * HD, to, skip:CH], lhs,
                                              probs[:, (s * G4 + i) % PROBS, skip:CH], start=(t == 0), stop=end)
                    if what:
                        op.then_inc(used, 1)

                pe.wait_ge(set_up, SLOTS + 1)
                pe.wait_ge(loaded[0], 16 * LOADS)
                for n in range(NU):
                    unit(0, 0, n)

                def body(g, j, p, more):
                    if more:
                        pe.wait_ge(loaded[(p + 1) % SLOTS], 16 * LOADS * (j + (p + 1) // SLOTS + 1))
                    for e in EVENTS:
                        if e[0] == "scores":
                            scores(g, p, e[1], e[2])
                        elif e[0] == "unit" and more:
                            unit(g + 1, (p + 1) % SLOTS, e[1])
                        elif e[0] == "values" and e[1] >= 0:
                            values(g, p, e[1], e[2])
                        elif e[0] == "values" and not first(g):
                            values(g - 1, (p - 1) % SLOTS, NS - 1, e[2])
                groups(pe, body)
                for what in range(2):
                    values(GROUPS - 1, 0, NS - 1, what)

            @block.scalar
            def _(act):
                def take_out(g, c):
                    act.wait_ge(used, g * NS + sum((cc + 1) * CH // P for cc in range(c + 1)))
                    wait(act, full_ready, 2 * g + c - 1)
                    nc.scalar.activation(out_sb[:, c, :], k.psum[:, OUT, :], ACT.Copy).then_inc(out_read, 1)
                    nc.scalar.activation(sum_sb[:, c, :], k.psum[:, SUM, :], ACT.Copy).then_inc(out_read, 1)

                def unit(g, p, n):
                    what = UNITS[n]
                    bank = k.psum[:, unit_bank(n), :]
                    if what[0] == "s":
                        return
                    act.wait_ge(unit_done, NU * g + n + 1)
                    if what[0] == "v":
                        wait(act, used, NS * (g - SLOTS + 1))
                        out = v[:, p, 4 * what[1]:4 * what[1] + 4, :].rearrange("p t c -> p (t c)")
                        nc.scalar.activation(out, bank, ACT.Copy).then_inc(turn_read, 1)
                    else:
                        out = qs[3 * HD:ALL_ROWS, p, what[1], what[2] * CH:(what[2] + 1) * CH]
                        nc.scalar.activation(out, bank[0:4, :], ACT.Copy).then_inc(turn_read, 1)

                def exp(g, s, i):
                    skip = block_rows(STEPS2[s])
                    act.wait_ge(scored, g * ITEMS + s * G4 + i + 1)
                    if not (first(g) and s < 2):
                        act.wait_ge(used, g * NS + s - 1)
                    nc.scalar.activation(probs[:, (s * G4 + i) % PROBS, skip:CH], k.psum[:, i, skip:CH],
                                         ACT.Exp).then_inc(exped, 1)

                for n in range(NU):
                    unit(0, 0, n)

                def body(g, j, p, more):
                    for e in EVENTS:
                        if e[0] == "scores":
                            exp(g, e[1], e[2])
                        elif e[0] == "unit" and more:
                            unit(g + 1, (p + 1) % SLOTS, e[1])
                        elif e == ("take", 0):
                            take_out(g, 0)
                        elif e == ("take", 1) and not first(g):
                            take_out(g - 1, 1)
                groups(act, body)
                take_out(GROUPS - 1, 1)

            @block.gpsimd
            def _(pool):
                for p in range(SLOTS):
                    nc.gpsimd.memset(ks[3 * HD:ALL_ROWS, p, :, :].bitcast(F32), 1.0).then_inc(ks_set, 1)

            @block.vector
            def _(dve):
                for p in range(SLOTS):
                    nc.vector.memset(qs[3 * HD:ALL_ROWS, p, :, :].bitcast(F32), 1.0).then_inc(set_up, 1)
                nc.vector.memset(max_rows[:, :, :, :].bitcast(F32), 1.0)
                nc.vector.memset(ones[:, :], 1.0).then_inc(set_up, 1)
                dve.wait_ge(set_up, SLOTS + 1)

                def unit(g, n):
                    what = UNITS[n]
                    if what[0] != "s":
                        return
                    i, (t, a) = what[1:]
                    dve.wait_ge(unit_done, NU * g + n + 1)
                    width = min(CH, (t + 1) * P - a)
                    at = MAX_AT[what[2]]
                    nc.vector.reduce_max(part_max[:, i % 2, at:at + 1], k.psum[:, unit_bank(n), 0:width], AX.X,
                                         negate=True).then_inc(max_read, 1)
                    if what[2] != UNITS_HEAD[-1]:
                        return
                    dve.wait_ge(max_read, NSC * g + SCORE_UNITS[n])
                    if i >= 2:
                        dve.wait_ge(turn_read, NTU * g + TURN_UNITS[UNITS.index(("m", i - 2, 1))])
                    elif not first(g):
                        dve.wait_ge(turn_read, NTU * (g - 1) + TURN_UNITS[UNITS.index(("m", i + 2, 1))])
                    one = CH // P
                    parts = part_max[:, i % 2, one:].rearrange("p (t a) -> p t a", a=2)
                    nc.vector.tensor_copy(neg_max[:, i % 2, 0:one], part_max[:, i % 2, 0:one])
                    nc.vector.tensor_tensor(neg_max[:, i % 2, one:], parts[:, :, 0], parts[:, :, 1],
                                            ALU.min).then_inc(max_read, 1)
                    dve.wait_ge(max_read, NSC * g + SCORE_UNITS[n] + 1)
                    nc.vector.tensor_copy(max_rows[:, i % 2, :, 2], neg_max[:, i % 2, :]).then_inc(split_hi, 1)
                    dve.wait_ge(split_hi, G4 * g + i + 1)
                    nc.vector.tensor_tensor(max_rows[:, i % 2, :, 3], neg_max[:, i % 2, :],
                                            max_rows[:, i % 2, :, 2].bitcast(F32), ALU.subtract).then_inc(split_lo, 1)

                def finish(g, c, piece):
                    n = 2 * g + c
                    squares = lambda tensor: tensor.rearrange("p (b k) -> p b k", k=SQ)
                    if piece == 0:
                        dve.wait_ge(out_read, 2 * (n + 1))
                        wait(dve, inverted, n)
                        nc.vector.transpose(turned[:, :], sum_sb[:, c, :]).then_inc(turned_ready, 1)
                    elif piece == 1:
                        dve.wait_ge(turned_ready, n + 1)
                        wait(dve, inv_ready, n)
                        nc.vector.reciprocal(inv_few[:, :], squares(turned[:, :])[:, :, 0]).then_inc(inverted, 1)
                    elif piece == 2:
                        dve.wait_ge(inverted, n + 1)
                        wait(dve, full_ready, n)
                        spread = inv_few[:, :].unsqueeze(2).broadcast_to([P, CH // SQ, SQ])
                        nc.vector.transpose(squares(inv[:, :]), spread).then_inc(inv_ready, 1)
                    elif piece == 3:
                        dve.wait_ge(inv_ready, n + 1)
                        wait(dve, lo_ready, n)
                        nc.vector.tensor_tensor(full[:, :], out_sb[:, c, :], inv[:, :], ALU.mult).then_inc(full_ready, 1)
                    elif piece == 4:
                        dve.wait_ge(full_ready, n + 1)
                        wait(dve, stored[c], 32 * g)
                        nc.vector.tensor_copy(hi[:, c, :], full[:, :]).then_inc(hi_ready, 1)
                    else:
                        dve.wait_ge(hi_ready, n + 1)
                        nc.vector.tensor_tensor(lo[:, c, :], full[:, :], hi[:, c, :].bitcast(F32),
                                                ALU.subtract).then_inc(lo_ready, 1)

                for n in range(NU):
                    unit(0, n)

                def body(g, j, p, more):
                    for e in EVENTS:
                        if e[0] == "unit" and more:
                            unit(g + 1, e[1])
                        elif e[0] == "finish" and e[1] == 0:
                            finish(g, 0, e[2])
                        elif e[0] == "finish" and not first(g):
                            finish(g - 1, 1, e[2])
                groups(dve, body)
                for piece in range(FINISH):
                    finish(GROUPS - 1, 1, piece)


def out_project(nc, k, wout, bout, x, att_hi, att_lo, x2):
    with ExitStack() as ctx:
        sb = lambda n, shape, dt: ctx.enter_context(nc.sbuf_tensor(f"out_{n}", shape, dt))
        sem = lambda n: ctx.enter_context(nc.semaphore(f"out_{n}"))
        raw = sb("raw", [P, 2, D], F32)
        w_hi = sb("w_hi", [P, KT, D], F32R)
        w_lo = sb("w_lo", [P, KT, D], F32R)
        a_hi = sb("a_hi", [P, 2, HG, CH], F32R)
        a_lo = sb("a_lo", [P, 2, HG, CH], F32R)
        bias = sb("bias", [P, D], F32)
        rows = sb("rows", [P, 2, D], F32)
        y = sb("y", [P, 2, D], F32)
        stats = RowStats(nc, ctx, "out")
        raw_in = [sem(f"raw_in{s}") for s in range(2)]
        rows_in = [sem(f"rows_in{s}") for s in range(2)]
        att_in = [sem(f"att_in{s}") for s in range(2)]
        att_first = [sem(f"att_first{t}") for t in range(KT)]
        stored = [sem(f"stored{s}") for s in range(2)]
        bias_in = sem("bias_in")
        hi_ready, lo_ready, summed, biased = sem("hi_ready"), sem("lo_ready"), sem("summed"), sem("biased")
        flat_ready, added = sem("flat_ready"), sem("added")
        TILES = CH // P

        with nc.Block() as block:
            @block.sync
            def _(sp):
                sp.dma_start(bias[:, :], bout.partition_broadcast(P)).then_inc(bias_in, 16)

                def load_att(u, s):
                    wait(sp, summed, TILES * (u - 1))
                    for to, src in ((a_hi, att_hi), (a_lo, att_lo)):
                        sp.dma_start(to[:, s, :, :].bitcast(F32), src[u]).then_inc(att_in[s], 16)

                for t in range(KT):
                    wait(sp, lo_ready, t - 1)
                    sp.dma_start(raw[:, t % 2, :], wout[t]).then_inc(raw_in[t % 2], 16)
                    for to, src in ((a_hi, att_hi), (a_lo, att_lo)):
                        sp.dma_start(to[:, 0, t, :].bitcast(F32), src[0][:, t, :]).then_inc(att_first[t], 16)
                load_att(1, 1)

                def body(u):
                    for i in range(TILES):
                        n = u * TILES + i
                        wait(sp, added, n - 1)
                        sp.dma_start(rows[:, i % 2, :], x[n]).then_inc(rows_in[i % 2], 16)
                        if not (isinstance(n, int) and n == 0):
                            sp.wait_ge(added, n)
                            sp.dma_start(x2[n - 1], y[:, (i - 1) % 2, :]).then_inc(stored[(i - 1) % 2], 16)
                tiles(sp, 1, body)
                for u in range(1, NCH):
                    if u + 1 < NCH:
                        load_att(u + 1, (u + 1) % 2)
                    body(u)
                sp.wait_ge(added, NT)
                sp.dma_start(x2[NT - 1], y[:, (NT - 1) % 2, :]).then_inc(stored[(NT - 1) % 2], 16)
                for s in range(2):
                    sp.wait_ge(stored[s], 16 * NT // 2)

            @block.scalar
            def _(act):
                for t in range(KT):
                    act.wait_ge(raw_in[t % 2], 16 * (t // 2 + 1))
                    nc.scalar.activation(w_hi[:, t, :], raw[:, t % 2, :], ACT.Copy).then_inc(hi_ready, 1)

            @block.gpsimd
            def _(pool):
                def body(j):
                    for p in range(2):
                        stats.invert(pool, j * 2 + p, p)
                tiles(pool, NT // 2, body)

            @block.tensor
            def _(pe):
                def products(u, s, i, t):
                    for h in range(2):
                        for m, (a, w) in enumerate(((a_hi, w_hi), (a_hi, w_lo), (a_lo, w_hi))):
                            op = nc.tensor.matmul(k.psum[:, 2 * i + h, :], a[:, s, t, i * P:(i + 1) * P],
                                                  w[:, t, h * CH:(h + 1) * CH], start=(t == 0 and m == 0),
                                                  stop=(t == KT - 1 and m == 2))
                    if t == KT - 1:
                        op.then_inc(summed, 1)

                for t in range(KT):
                    pe.wait_ge(att_first[t], 32)
                    pe.wait_ge(lo_ready, t + 1)
                    for i in range(TILES):
                        products(0, 0, i, t)

                for u in range(1, NCH):
                    pe.wait_ge(att_in[u % 2], 32 * ((u + 1) // 2))
                    for i in range(TILES):
                        pe.wait_ge(biased, 2 * ((u - 1) * TILES + i + 1))
                        for t in range(KT):
                            products(u, u % 2, i, t)

            @block.vector
            def _(dve):
                stats.start(dve)
                for t in range(KT):
                    dve.wait_ge(hi_ready, t + 1)
                    nc.vector.tensor_tensor(w_lo[:, t, :], raw[:, t % 2, :], w_hi[:, t, :].bitcast(F32),
                                            ALU.subtract).then_inc(lo_ready, 1)
                dve.wait_ge(bias_in, 16)

                def body(u):
                    for i in range(TILES):
                        n = u * TILES + i
                        p = i % 2
                        dve.wait_ge(summed, n + 1)
                        wait(dve, stored[p], 16 * (u * TILES // 2 + i // 2))
                        for h in range(2):
                            cols = slice(h * CH, (h + 1) * CH)
                            nc.vector.tensor_tensor(y[:, p, cols], k.psum[:, 2 * i + h, :], bias[:, cols],
                                                    ALU.add).then_inc(biased, 1)
                        dve.wait_ge(biased, 2 * (n + 1))
                        wait(dve, flat_ready, n - 1)
                        stats.moments(dve, n, p, [y[:, p, h * CH:(h + 1) * CH] for h in range(2)])
                        stats.normalise(dve, n, p, y[:, p, :], y[:, p, :]).then_inc(flat_ready, 1)
                        dve.wait_ge(flat_ready, n + 1)
                        dve.wait_ge(rows_in[p], 16 * (u * TILES // 2 + i // 2 + 1))
                        nc.vector.tensor_tensor(y[:, p, :], y[:, p, :], rows[:, p, :], ALU.add).then_inc(added, 1)
                tiles(dve, NCH, body)


VECTOR_PLAN = {2: [("low", 1)], 6: [("product", -1)], 8: [("prepare", 1)], 9: [("rest", -1)],
               11: [("product", 0)], 14: [("rest", 0), ("finish", 0)], 18: [("product", 1)],
               22: [("rest", 1), ("low", 0), ("prepare", 0)], 24: [("product", 2)],
               27: [("rest", 2)], 29: [("finish", 1)]}
SCALAR_PLAN = {2: [("high", 1)], 9: [("part", -1)], 11: [("gate", 0)], 14: [("part", 0)], 17: [("gate", 1)],
               21: [("part", 1)], 22: [("high", 0)], 26: [("gate", 2)], 27: [("part", 2)], 29: [("gate", 3)]}


def gate_up(nc, k, w12, xt_hi, xt_lo, h_hi, h_lo):
    with ExitStack() as ctx:
        sb = lambda n, shape, dt: ctx.enter_context(nc.sbuf_tensor(f"gu_{n}", shape, dt))
        sem = lambda n: ctx.enter_context(nc.semaphore(f"gu_{n}"))
        w_hi = sb("w_hi", [P, 2, 2, KT, P], F32R)
        w_lo = sb("w_lo", [P, 2, 2, KT, P], F32R)
        act_gate = sb("act_gate", [P, 2, CH], F32)
        full = sb("full", [P, 2, CH], F32)
        hi = sb("hi", [P, 2, CH], F32R)
        lo = sb("lo", [P, 2, CH], F32R)
        nf4 = Nf4(nc, ctx, "w12", 1, 3)
        turned, hi_ready, lo_ready = sem("turned"), sem("w_hi_ready"), sem("w_lo_ready")
        summed, gated, multiplied = sem("summed"), sem("gated"), sem("multiplied")
        h_hi_ready, h_lo_ready = sem("h_hi_ready"), sem("h_lo_ready")
        stored = [sem(f"stored{s}") for s in range(2)]
        GATE, UP, TURN = 0, 2, 4

        def turn_banks(u):
            return k.psum[:, TURN + 2 * u:TURN + 2 * u + 2, :].rearrange("p a b -> p (a b)")

        def first(t):
            return isinstance(t, int) and t == 0

        def last(t):
            return isinstance(t, int) and t >= FT - 1

        def steps(eng, body):
            def two(j):
                for q in range(2):
                    body(j * 2 + q, j, q)
            tiles(eng, FT // 2, two, last=1)

        with nc.Block() as block:
            @block.sync
            def _(sp):
                nf4.load(sp, 0, 0, 0, w12[0])
                nf4.load(sp, 1, 0, 1, w12[1])
                nf4.load(sp, 2, 1, 0, w12[2])
                nf4.load(sp, 3, 1, 1, w12[3])

                def store(t, c):
                    sp.wait_ge(h_lo_ready, t * NCH + c + 1)
                    cols = slice(c * CH, (c + 1) * CH)
                    for to, src in ((h_hi, hi), (h_lo, lo)):
                        sp.dma_start(to[t][:, cols], src[:, c % 2, :].bitcast(F32)).then_inc(stored[c % 2], 16)

                def body(t, j, q):
                    more = not (isinstance(t, int) and t >= FT - 2)
                    if not first(t):
                        store(t - 1, NCH - 1)
                    if more:
                        nf4.load(sp, 2 * t + 4, t + 2, 0, w12[2 * t + 4])
                    for c in range(NCH - 1):
                        store(t, c)
                    if more:
                        nf4.load(sp, 2 * t + 5, t + 2, 1, w12[2 * t + 5])
                steps(sp, body)
                store(FT - 1, NCH - 1)
                for s in range(2):
                    sp.wait_ge(stored[s], 32 * 2 * FT)

            @block.scalar
            def _(act):
                def high(n, t, q, u):
                    act.wait_ge(turned, n + 1)
                    wait(act, summed, 2 * NCH * (t - 1))
                    nc.scalar.activation(w_hi[:, q, u], turn_banks(u).rearrange("p (k h) -> p k h", h=P),
                                         ACT.Copy).then_inc(hi_ready, 1)

                def gate(t, c):
                    act.wait_ge(summed, 2 * (NCH * t + c) + 1)
                    wait(act, multiplied, NCH * t + c - 1)
                    nc.scalar.activation(act_gate[:, c % 2, :], k.psum[:, GATE + c % 2, :], ACT.Silu).then_inc(gated, 1)

                def part(t, c):
                    act.wait_ge(multiplied, NCH * t + c + 1)
                    wait(act, stored[c % 2], 32 * (2 * t + c // 2))
                    nc.scalar.activation(hi[:, c % 2, :], full[:, c % 2, :], ACT.Copy).then_inc(h_hi_ready, 1)

                for u in range(2):
                    for i in range(NQ):
                        nf4.make_sign(act, u, u, i)
                high(0, 0, 0, 0)

                def body(t, j, q):
                    for m in range(2 * NQ):
                        if not last(t):
                            nf4.make_sign(act, 2 * t + 2 + m // NQ, m // NQ, m % NQ)
                        for what, c in SCALAR_PLAN.get(m, ()):
                            if what == "gate":
                                gate(t, c)
                            elif what == "part" and c >= 0:
                                part(t, c)
                            elif what == "part" and not first(t):
                                part(t - 1, NCH - 1)
                            elif what == "high" and c == 1:
                                high(2 * t + 1, t, q, 1)
                            elif what == "high" and not last(t):
                                high(2 * t + 2, t + 1, 1 - q, 0)
                steps(act, body)
                part(FT - 1, NCH - 1)

            @block.tensor
            def _(pe):
                def turn(n, u):
                    pe.wait_ge(nf4.dq_ready, n + 1)
                    wait(pe, lo_ready, n - 1)
                    for t in range(KT):
                        op = nc.tensor.transpose(turn_banks(u)[:, t * P:(t + 1) * P], nf4.dq[:, 0, t * P:(t + 1) * P],
                                                 k.ident[:, :])
                    op.then_inc(turned, 1)

                turn(0, 0)
                turn(1, 1)

                def body(t, j, q):
                    for c in range(NCH):
                        cols = slice(c * CH, (c + 1) * CH)
                        n = t * NCH + c
                        for u, to, free in ((0, GATE, gated), (1, UP, multiplied)):
                            if c == 0:
                                pe.wait_ge(lo_ready, 2 * t + u + 1)
                            wait(pe, free, n - 1)
                            terms = [(w, x, m) for m in range(KT)
                                     for w, x in ((w_hi, xt_hi), (w_hi, xt_lo), (w_lo, xt_hi))]
                            for i, (w, x, m) in enumerate(terms):
                                op = nc.tensor.matmul(k.psum[:, to + c % 2, :], w[:, q, u, m, :], x[:, m, cols],
                                                      start=(i == 0), stop=(i == len(terms) - 1))
                            op.then_inc(summed, 1)
                            if (c, u) == (1, 1) and not last(t):
                                turn(2 * t + 2, 0)
                            if (c, u) == (3, 0) and not last(t):
                                turn(2 * t + 3, 1)
                steps(pe, body)

            @block.vector
            def _(dve):
                nf4.biases(dve)

                def low(n, q, u):
                    dve.wait_ge(hi_ready, n + 1)
                    nc.vector.tensor_tensor(w_lo[:, q, u], turn_banks(u).rearrange("p (k h) -> p k h", h=P),
                                            w_hi[:, q, u].bitcast(F32), ALU.subtract).then_inc(lo_ready, 1)

                def finish(n, u):
                    wait(dve, turned, n)
                    nf4.finish(dve, n, u)

                nf4.prepare(dve, 0, 0, 0)
                nf4.prepare(dve, 1, 0, 1)
                for n in range(2):
                    for i in range(NQ):
                        nf4.take(dve, n, i)
                    finish(n, n)
                nf4.prepare(dve, 2, 1, 0)
                low(0, 0, 0)

                def product(t, c):
                    n = t * NCH + c
                    dve.wait_ge(summed, 2 * (n + 1))
                    dve.wait_ge(gated, n + 1)
                    wait(dve, h_lo_ready, n - 1)
                    nc.vector.tensor_tensor(full[:, c % 2, :], act_gate[:, c % 2, :], k.psum[:, UP + c % 2, :],
                                            ALU.mult).then_inc(multiplied, 1)

                def rest(t, c):
                    dve.wait_ge(h_hi_ready, t * NCH + c + 1)
                    nc.vector.tensor_tensor(lo[:, c % 2, :], full[:, c % 2, :], hi[:, c % 2, :].bitcast(F32),
                                            ALU.subtract).then_inc(h_lo_ready, 1)

                def body(t, j, q):
                    for m in range(2 * NQ):
                        if not last(t):
                            nf4.take(dve, 2 * t + 2 + m // NQ, m % NQ)
                        for what, c in VECTOR_PLAN.get(m, ()):
                            if what in ("product", "rest"):
                                do = product if what == "product" else rest
                                if c >= 0:
                                    do(t, c)
                                elif not first(t):
                                    do(t - 1, NCH - 1)
                            elif what == "low" and c == 1:
                                low(2 * t + 1, q, 1)
                            elif last(t):
                                pass
                            elif what == "low":
                                low(2 * t + 2, 1 - q, 0)
                            elif what == "finish":
                                finish(2 * t + 2 + c, c)
                            elif c == 1:
                                nf4.prepare(dve, 2 * t + 3, t + 1, 1)
                            elif not (isinstance(t, int) and t >= FT - 2):
                                nf4.prepare(dve, 2 * t + 4, t + 2, 0)
                steps(dve, body)
                product(FT - 1, NCH - 1)
                rest(FT - 1, NCH - 1)


def down(nc, k, dq3, h_hi, h_lo, x2, partial, out):
    HALF = FT // 2
    with ExitStack() as ctx:
        sb = lambda n, shape, dt: ctx.enter_context(nc.sbuf_tensor(f"down_{n}", shape, dt))
        sem = lambda n: ctx.enter_context(nc.semaphore(f"down_{n}"))
        w_hi = sb("w_hi", [P, HALF, D], F32R)
        w_lo = sb("w_lo", [P, HALF, D], F32R)
        dq = sb("dq", [P, 2, D], F32)
        a_hi = sb("a_hi", [P, 2, HALF, P], F32R)
        a_lo = sb("a_lo", [P, 2, HALF, P], F32R)
        rows = sb("rows", [P, 2, D], F32)
        before = sb("before", [P, 2, D], F32)
        y = sb("y", [P, 2, D], F32)
        stats = RowStats(nc, ctx, "down")
        dq_in = [sem(f"dq_in{s}") for s in range(2)]
        a_in = [sem(f"a_in{s}") for s in range(2)]
        rows_in = [sem(f"rows_in{s}") for s in range(2)]
        stored = [sem(f"stored{s}") for s in range(2)]
        kept = [sem(f"kept{s}") for s in range(2)]
        turned, hi_ready, lo_ready, summed = sem("turned"), sem("hi_ready"), sem("lo_ready"), sem("summed")
        taken, flat_ready, added = sem("taken"), sem("flat_ready"), sem("added")

        def acc_bank(p):
            return k.psum[:, 2 * p:2 * p + 2, :].rearrange("p a b -> p (a b)")

        def turn_bank(p):
            return k.psum[:, 4 + 2 * p:6 + 2 * p, :].rearrange("p a b -> p (a b)")

        with nc.Block() as block:
            @block.sync
            def _(sp):
                def load(m, n, j, p):
                    wait(sp, summed, m * NT + n - 1)
                    for to, src in ((a_hi, h_hi), (a_lo, h_lo)):
                        cols = bass.ds(n * P, P)
                        sp.dma_start(to[:, p].bitcast(F32),
                                     src[m * HALF:(m + 1) * HALF, :, cols].rearrange("t p c -> p t c")).then_inc(a_in[p], 16)

                def weights(m):
                    for t in range(HALF):
                        c = m * HALF + t
                        wait(sp, turned, c - 1)
                        sp.dma_start(dq[:, c % 2, :], dq3[c]).then_inc(dq_in[c % 2], 16)

                load(0, 0, 0, 0)
                load(0, 1, 0, 1)
                weights(0)

                def first(j):
                    for p in range(2):
                        n = j * 2 + p
                        if not (isinstance(n, int) and n >= NT - 2):
                            load(0, n + 2, j + 1, p)
                        sp.wait_ge(taken, n + 1)
                        sp.dma_start(partial[n], y[:, p, :]).then_inc(kept[p], 16)
                tiles(sp, NT // 2, first, last=1)
                load(1, 0, 0, 0)
                load(1, 1, 0, 1)
                weights(1)
                for s in range(2):
                    sp.wait_ge(kept[s], 16 * NT // 2)

                def rest(n, j, p):
                    wait(sp, added, n - 1)
                    sp.dma_start(before[:, p, :], partial[n]).then_inc(rows_in[p], 16)
                    sp.dma_start(rows[:, p, :], x2[n]).then_inc(rows_in[p], 16)
                rest(0, 0, 0)

                def second(j):
                    for p in range(2):
                        n = j * 2 + p
                        if not (isinstance(n, int) and n == NT - 1):
                            rest(n + 1, j + p, 1 - p)
                        if not (isinstance(n, int) and n >= NT - 2):
                            load(1, n + 2, j + 1, p)
                        sp.wait_ge(added, n + 1)
                        sp.dma_start(out[n], y[:, p, :]).then_inc(stored[p], 16)
                tiles(sp, NT // 2, second, last=1)
                for s in range(2):
                    sp.wait_ge(stored[s], 16 * NT // 2)

            @block.scalar
            def _(act):
                def weights(m):
                    wait(act, summed, m * NT)
                    for t in range(HALF):
                        c = m * HALF + t
                        act.wait_ge(turned, c + 1)
                        nc.scalar.activation(w_hi[:, t, :], turn_bank(c % 2), ACT.Copy).then_inc(hi_ready, 1)
                weights(0)

                def first(j):
                    for p in range(2):
                        n = j * 2 + p
                        act.wait_ge(summed, n + 1)
                        wait(act, kept[p], 16 * j)
                        nc.scalar.activation(y[:, p, :], acc_bank(p), ACT.Copy).then_inc(taken, 1)
                tiles(act, NT // 2, first)
                weights(1)

            @block.gpsimd
            def _(pool):
                def body(j):
                    for p in range(2):
                        stats.invert(pool, j * 2 + p, p)
                tiles(pool, NT // 2, body)

            @block.tensor
            def _(pe):
                def turn(c):
                    pe.wait_ge(dq_in[c % 2], 16 * (c // 2 + 1))
                    wait(pe, lo_ready, c - 1)
                    for b in range(KT):
                        op = nc.tensor.transpose(turn_bank(c % 2)[:, b * P:(b + 1) * P],
                                                 dq[:, c % 2, b * P:(b + 1) * P], k.ident[:, :])
                    op.then_inc(turned, 1)

                def products(p, h, t):
                    for i, (a, w) in enumerate(((a_hi, w_hi), (a_hi, w_lo), (a_lo, w_hi))):
                        op = nc.tensor.matmul(k.psum[:, 2 * p + h, :], a[:, p, t, :], w[:, t, h * CH:(h + 1) * CH],
                                              start=(t == 0 and i == 0), stop=(t == HALF - 1 and i == 2))
                    if t == HALF - 1 and h == 1:
                        op.then_inc(summed, 1)

                def half(m):
                    for c in range(m * HALF, m * HALF + 2):
                        turn(c)
                    for p in range(2):
                        pe.wait_ge(a_in[p], 32 * (m * NT // 2 + 1))
                        wait(pe, taken, m * NT + p - 1)
                    for t in range(HALF):
                        pe.wait_ge(lo_ready, m * HALF + t + 1)
                        for p in range(2):
                            for h in range(2):
                                products(p, h, t)
                        if t + 2 < HALF:
                            turn(m * HALF + t + 2)

                    def body(j):
                        for p in range(2):
                            pe.wait_ge(a_in[p], 32 * (m * NT // 2 + j + 1))
                            pe.wait_ge(taken, m * NT + 2 * j + p - 1)
                            for h in range(2):
                                for t in range(HALF):
                                    products(p, h, t)
                    with pe.Fori(1, NT // 2) as j:
                        body(j)
                half(0)
                half(1)

            @block.vector
            def _(dve):
                stats.start(dve)

                def weights(m):
                    for t in range(HALF):
                        c = m * HALF + t
                        dve.wait_ge(hi_ready, c + 1)
                        nc.vector.tensor_tensor(w_lo[:, t, :], turn_bank(c % 2), w_hi[:, t, :].bitcast(F32),
                                                ALU.subtract).then_inc(lo_ready, 1)
                weights(0)
                weights(1)
                for s in range(2):
                    dve.wait_ge(kept[s], 16 * NT // 2)

                def body(j):
                    for p in range(2):
                        n = j * 2 + p
                        dve.wait_ge(summed, NT + n + 1)
                        dve.wait_ge(rows_in[p], 32 * (j + 1))
                        wait(dve, stored[p], 16 * j)
                        nc.vector.tensor_tensor(y[:, p, :], acc_bank(p), before[:, p, :], ALU.add).then_inc(taken, 1)
                        dve.wait_ge(taken, NT + n + 1)
                        wait(dve, flat_ready, n - 1)
                        stats.moments(dve, n, p, [y[:, p, h * CH:(h + 1) * CH] for h in range(2)])
                        stats.normalise(dve, n, p, y[:, p, :], y[:, p, :]).then_inc(flat_ready, 1)
                        dve.wait_ge(flat_ready, n + 1)
                        nc.vector.tensor_tensor(y[:, p, :], y[:, p, :], rows[:, p, :], ALU.add).then_inc(added, 1)
                tiles(dve, NT // 2, body)


class Shared:
    pass


SCRATCH = "Internal"


def block_kernel(nc, x, wqkv, bqkv, wout, bout, w12, w3, slopes, out, phases=None):
    scratch = lambda name, shape: nc.dram_tensor(name, shape, F32, kind=SCRATCH).ap()
    q_hi, q_lo, k_hi, k_lo, v_all = (scratch(n, (GROUPS, P, S)) for n in ("q_hi", "q_lo", "k_hi", "k_lo", "v_all"))
    alibi = scratch("alibi", (GROUPS, 2, G4, S))
    att_hi, att_lo = (scratch(n, (GROUPS, S // CH, P, CH)) for n in ("att_hi", "att_lo"))
    x2, partial = scratch("x2", (NT, P, D)), scratch("partial", (NT, P, D))
    dq3 = scratch("dq3", (FT, P, D))
    h_hi, h_lo = scratch("h_hi", (FT, P, TOK)), scratch("h_lo", (FT, P, TOK))
    with ExitStack() as ctx:
        k = Shared()
        k.psum = ctx.enter_context(nc.psum_tensor("psum", [P, 8, CH], F32))
        k.ident = ctx.enter_context(nc.sbuf_tensor("ident", [P, P], F32))
        k.ident16 = ctx.enter_context(nc.sbuf_tensor("ident16", [P, P], BF16))
        k.mask_q = ctx.enter_context(nc.sbuf_tensor("mask_q", [P, P], BF16))
        k.mask_k = ctx.enter_context(nc.sbuf_tensor("mask_k", [P, P], BF16))
        constants(nc, k, slopes, alibi)
        with ExitStack() as part:
            xt_hi = part.enter_context(nc.sbuf_tensor("xt_hi", [P, KT, TOK], F32R))
            xt_lo = part.enter_context(nc.sbuf_tensor("xt_lo", [P, KT, TOK], F32R))
            normalise(nc, k, "ln1", x, xt_hi, xt_lo)
            qkv(nc, k, wqkv, bqkv, w3, xt_hi, xt_lo, q_hi, q_lo, k_hi, k_lo, v_all, dq3)
        if phases and phases < 2:
            return
        attention(nc, k, q_hi, q_lo, k_hi, k_lo, v_all, alibi, att_hi, att_lo)
        chunked = [[a[b * HG:(b + 1) * HG, c].rearrange("g p t -> p g t") for b in range(B) for c in range(S // CH)]
                   for a in (att_hi, att_lo)]
        if phases and phases < 3:
            return
        out_project(nc, k, wout, bout, x, chunked[0], chunked[1], x2)
        if phases and phases < 4:
            return
        with ExitStack() as part:
            xt_hi = part.enter_context(nc.sbuf_tensor("xt2_hi", [P, KT, TOK], F32R))
            xt_lo = part.enter_context(nc.sbuf_tensor("xt2_lo", [P, KT, TOK], F32R))
            normalise(nc, k, "ln2", x2, xt_hi, xt_lo)
            gate_up(nc, k, w12, xt_hi, xt_lo, h_hi, h_lo)
        if phases and phases < 5:
            return
        down(nc, k, dq3, h_hi, h_lo, x2, partial, out)


def kernel(**inputs):
    import numpy as np
    import concourse.bacc as bacc
    from concourse.bass_utils import run_bass_kernel_spmd

    get = lambda n: np.asarray(inputs[n])
    pad = FT * P - F
    tiled = {
        "x": get("L0_attn_x").reshape(NT, P, D),
        "wqkv": get("L0_attn_w_qkv").reshape(3 * KT, P, KT, P).transpose(0, 3, 2, 1),
        "bqkv": get("L0_attn_b_qkv").reshape(3 * KT, P).T,
        "wout": get("L0_attn_w_out").T.reshape(KT, P, D),
        "bout": get("L0_attn_b_out"),
        "w12": np.stack([np.pad(get(n), ((0, pad), (0, 0))).reshape(FT, P, D) for n in ("L0_ffn_w1", "L0_ffn_w2")],
                        axis=1).reshape(2 * FT, P, D),
        "w3": np.pad(get("L0_ffn_w3"), ((0, 0), (0, pad))).reshape(KT, P, FT, P).transpose(2, 1, 0, 3).reshape(FT, P, D),
        "slopes": (np.float32(1.0) / np.power(np.float32(2.0), np.arange(1, HEADS + 1, dtype=np.float32)
                                              * np.float32(8.0 / HEADS))).reshape(HEADS, 1).astype(np.float32),
    }
    nc = bacc.Bacc("TRN2", target_bir_lowering=False, num_devices=1)
    arrays, args = {}, []
    for name, a in tiled.items():
        a = np.ascontiguousarray(a)
        arrays[f"in_{name}"] = a
        args.append(nc.dram_tensor(f"in_{name}", a.shape, mybir.dt.from_np(a.dtype), kind="ExternalInput").ap())
    out = nc.dram_tensor("result_rows", (NT, P, D), F32, kind="ExternalOutput").ap()
    block_kernel(nc, *args, out)
    r = run_bass_kernel_spmd(nc, [arrays], core_ids=[0])
    return r.results[0]["result_rows"].reshape(B, S, D)
```

```python
import concourse.bass as bass
from concourse import mybir
from contextlib import ExitStack

F32 = mybir.dt.float32
F32R = mybir.dt.float32r
BF16 = mybir.dt.bfloat16
I32 = mybir.dt.int32
ALU = mybir.AluOpType
ACT = mybir.ActivationFunctionType
AX = mybir.AxisListType

P = 128
B, S, D = 2, 1024, 1024
HEADS, HD = 32, 32
F = 2752
TOK = B * S
KT = D // P
FT = -(-F // P)
NT = TOK // P
CH = 512
NCH = TOK // CH
FAST = 256
G4 = P // HD
HG = HEADS // G4
GROUPS = B * HG
QT = S // P
SCALE = HD ** -0.5
EPS = 1e-5
MASKED = -1e30
QB = 64
NB = D // QB

CODE = [-1.0, -0.6961928009986877, -0.5250730514526367, -0.39491748809814453, -0.28444138169288635,
        -0.18477343022823334, -0.09105003625154495, 0.0, 0.07958029955625534, 0.16093020141124725,
        0.24611230194568634, 0.33791524171829224, 0.44070982933044434, 0.5626170039176941,
        0.7229568362236023, 1.0]


def nf4_steps():
    import numpy as np
    code = np.array(CODE, np.float32)
    bounds = (code[:-1] + code[1:]) * np.float32(0.5)
    return [float(b) for b in bounds], [float(c + np.float32(1.0)) for c in code[1:]]


BOUNDS, STEPS = nf4_steps()
NQ = len(BOUNDS)


def wait(eng, sem, value):
    if isinstance(value, int) and value <= 0:
        return
    eng.wait_ge(sem, value)


def wait_apart(eng, sem, value, passed):
    eng.wait_ge(sem, value)
    eng.sem_inc(passed, 1)


def tiles(eng, n, body, first=1, last=0, start=0):
    for j in range(start, start + first):
        body(j)
    if n - last > start + first:
        with eng.Fori(start + first, n - last) as j:
            body(j)
    for j in range(n - last, n):
        body(j)


class Nf4:

    def __init__(self, nc, k, ctx, name, dq_slots, sign_slots, raw_slots=2):
        sb = lambda n, shape, dt: ctx.enter_context(nc.sbuf_tensor(f"{name}_{n}", shape, dt))
        sem = lambda n: ctx.enter_context(nc.semaphore(f"{name}_{n}"))
        self.nc = nc
        self.raw_slots = raw_slots
        self.raw = sb("raw", [P, raw_slots, D], F32)
        self.code = sb("code", [P, raw_slots, D], F32)
        self.dq_slots = dq_slots
        self.dq = sb("dq", [P, dq_slots, D], F32)
        assert NQ % sign_slots == 0
        self.sign_slots = sign_slots
        self.sign = sb("sign", [P, sign_slots, D], BF16)
        self.top = sb("top", [P, raw_slots, NB], F32)
        self.safe = sb("safe", [P, raw_slots, NB], F32)
        self.inv = sb("inv", [P, raw_slots, NB], F32)
        self.bias = k.bounds
        self.loaded = [sem(f"loaded{s}") for s in range(raw_slots)]
        self.steps = sem("steps")
        self.scaled = sem("scaled")
        self.signs = sem("signs")
        self.started = sem("started")
        self.coded = sem("coded")
        self.dq_ready = sem("dq_ready")

    def load(self, sp, n, j, p, src):
        wait(sp, self.signs, NQ * (n + 1 - self.raw_slots))
        sp.dma_start(self.raw[:, p, :], src).then_inc(self.loaded[p], 16)

    def prepare(self, dve, n, j, p):
        nc = self.nc
        blocks = self.raw[:, p, :].rearrange("p (b k) -> p b k", k=QB)
        dve.wait_ge(self.loaded[p], 16 * (j + 1))
        wait(dve, self.dq_ready, n + 1 - self.raw_slots)
        nc.vector.reduce_max(self.top[:, p, :], blocks, AX.X, apply_absolute_value=True).then_inc(self.steps, 1)
        dve.wait_ge(self.steps, 3 * n + 1)
        nc.vector.scalar_tensor_tensor(out=self.safe[:, p, :], in0=self.top[:, p, :], scalar=0.0,
                                       in1=self.top[:, p, :], op0=ALU.is_equal, op1=ALU.add).then_inc(self.steps, 1)
        dve.wait_ge(self.steps, 3 * n + 2)
        nc.vector.reciprocal(self.inv[:, p, :], self.safe[:, p, :]).then_inc(self.steps, 1)
        dve.wait_ge(self.steps, 3 * n + 3)
        inv = self.inv[:, p, :].unsqueeze(2).broadcast_to([P, NB, QB])
        nc.vector.tensor_tensor(blocks, blocks, inv, ALU.mult).then_inc(self.scaled, 1)

    def make_sign(self, act, n, p, i):
        if i == 0:
            act.wait_ge(self.scaled, n + 1)
        former = i - self.sign_slots
        if former == 0:
            act.wait_ge(self.started, n + 1)
        else:
            wait(act, self.coded, 2 * ((NQ - 1) * n + former + (former < 0)))
        self.nc.scalar.activation(self.sign[:, i % self.sign_slots, :], self.raw[:, p, :], ACT.Sign,
                                  bias=self.bias[:, i:i + 1]).then_inc(self.signs, 1)
        if i == 0:
            act.wait_ge(self.signs, NQ * n + 1)
            wait(act, self.dq_ready, n + 1 - self.raw_slots)
            self.nc.scalar.activation(self.code[:, p, :], self.sign[:, 0, :], ACT.Relu,
                                      scale=STEPS[0]).then_inc(self.started, 1)

    def take(self, dve, n, p, i):
        nc = self.nc
        if i == 0:
            return
        dve.wait_ge(self.signs, NQ * n + i + 1)
        if i == 1:
            dve.wait_ge(self.started, n + 1)
        for h in range(2):
            half = slice(h * D // 2, (h + 1) * D // 2)
            if i > 1:
                dve.wait_ge(self.coded, 2 * ((NQ - 1) * n + i - 1) + h - 1)
            nc.vector.scalar_tensor_tensor(out=self.code[:, p, half], in0=self.sign[:, i % self.sign_slots, half],
                                           scalar=STEPS[i], in1=self.code[:, p, half], op0=ALU.mult,
                                           op1=ALU.max).then_inc(self.coded, 1)

    def finish(self, dve, n, p):
        dve.wait_ge(self.coded, 2 * (NQ - 1) * (n + 1))
        top = self.top[:, p, :].unsqueeze(2).broadcast_to([P, NB, QB])
        out = self.dq[:, p % self.dq_slots, :].rearrange("p (b k) -> p b k", k=QB)
        self.nc.vector.scalar_tensor_tensor(out=out, in0=self.code[:, p, :].rearrange("p (b k) -> p b k", k=QB),
                                            scalar=-1.0, in1=top, op0=ALU.add, op1=ALU.mult).then_inc(self.dq_ready, 1)


class RowStats:

    def __init__(self, nc, k, ctx, name):
        sb = lambda n, shape: ctx.enter_context(nc.sbuf_tensor(f"{name}_{n}", shape, F32))
        sem = lambda n: ctx.enter_context(nc.semaphore(f"{name}_{n}"))
        self.nc = nc
        self.parts = sb("parts", [P, 2, 6])
        self.mv = sb("mv", [P, 2, 2])
        self.var_eps = sb("var_eps", [P, 2])
        self.rstd = sb("rstd", [P, 2])
        self.eps, self.power, self.passed = k.eps, k.power, k.passed
        self.parts_ready = sem("parts_ready")
        self.mv_ready = sem("mv_ready")
        self.inverted = sem("inverted")

    def moments(self, dve, n, p, halves):
        nc = self.nc
        wait(dve, self.mv_ready, n)
        for h in range(2):
            nc.vector.bn_stats(self.parts[:, h, :], halves[h]).then_inc(self.parts_ready, 1)
        wait_apart(dve, self.parts_ready, 2 * n + 2, self.passed)
        nc.vector.bn_aggr(self.mv[:, p, :], self.parts[:, :, :]).then_inc(self.mv_ready, 1)

    def invert(self, pool, n, p):
        pool.wait_ge(self.mv_ready, n + 1)
        self.nc.gpsimd.tensor_tensor(self.var_eps[:, p:p + 1], self.mv[:, p, 1:2], self.eps[:, :],
                                     ALU.add).then_inc(self.inverted, 1)
        pool.wait_ge(self.inverted, 2 * n + 1)
        self.nc.gpsimd.tensor_tensor(self.rstd[:, p:p + 1], self.var_eps[:, p:p + 1], self.power[:, :],
                                     ALU.pow).then_inc(self.inverted, 1)

    def normalise(self, dve, n, p, out, rows):
        dve.wait_ge(self.inverted, 2 * n + 2)
        return self.nc.vector.tensor_scalar(out, rows, self.mv[:, p, 0:1], self.rstd[:, p:p + 1],
                                            ALU.subtract, ALU.mult)


def constants(nc, k, slopes, alibi):
    with ExitStack() as ctx:
        sb = lambda n, shape, dt: ctx.enter_context(nc.sbuf_tensor(n, shape, dt))
        sem = lambda n: ctx.enter_context(nc.semaphore(n))
        where = sb("position_int", [HEADS, S], I32)
        position = sb("position", [HEADS, S], F32)
        slope = sb("slope", [HEADS, 1], F32)
        full = sb("alibi_full", [HEADS, S], F32)
        part = sb("alibi_parts", [HEADS, 2, S], F32R)
        made, slope_in, stored = sem("c_made"), sem("c_slope"), sem("c_stored")
        pos_ready, step = sem("c_pos"), sem("c_step")
        with nc.Block() as block:
            @block.sync
            def _(sp):
                sp.dma_start(slope[:, :], slopes).then_inc(slope_in, 16)
                sp.wait_ge(step, 4)
                for b in range(B):
                    for g in range(HG):
                        src = part[g * G4:(g + 1) * G4, :, :].bitcast(F32)
                        sp.dma_start(alibi[b * HG + g].rearrange("c i t -> i c t"), src).then_inc(stored, 16)
                sp.wait_ge(stored, 16 * GROUPS)

            @block.gpsimd
            def _(pool):
                nc.gpsimd.iota(where[:, :], [[1, S]], base=1 - S, channel_multiplier=0).then_inc(pos_ready, 1)
                for m in (k.ident, k.ident16, k.mask_q, k.mask_k):
                    nc.gpsimd.memset(m[:, :], 0.0).then_inc(made, 1)
                pool.wait_ge(made, 4)
                for m in (k.ident, k.ident16):
                    nc.gpsimd.affine_select(out=m[:, :], in_=m[:, :], compare_op=ALU.not_equal, fill=1.0,
                                            base=0, pattern=[[-1, P]], channel_multiplier=1).then_inc(made, 1)
                nc.gpsimd.affine_select(out=k.mask_q[:, :], in_=k.mask_q[:, :], compare_op=ALU.is_ge, fill=MASKED,
                                        base=0, pattern=[[-1, P]], channel_multiplier=1).then_inc(made, 1)
                nc.gpsimd.affine_select(out=k.mask_k[:, :], in_=k.mask_k[:, :], compare_op=ALU.is_ge, fill=MASKED,
                                        base=0, pattern=[[1, P]], channel_multiplier=-1).then_inc(made, 1)
                pool.wait_ge(made, 8)

            @block.vector
            def _(dve):
                nc.vector.memset(k.eps[:, :], EPS)
                nc.vector.memset(k.power[:, :], -0.5)
                for i in range(NQ):
                    nc.vector.memset(k.bounds[:, i:i + 1], -BOUNDS[i])
                dve.wait_ge(pos_ready, 1)
                nc.vector.tensor_copy(position[:, :], where[:, :]).then_inc(step, 1)
                dve.wait_ge(step, 1)
                dve.wait_ge(slope_in, 16)
                nc.vector.tensor_scalar(full[:, :], position[:, :], slope[:, :], None, ALU.mult).then_inc(step, 1)
                dve.wait_ge(step, 2)
                nc.vector.tensor_copy(part[:, 0, :], full[:, :]).then_inc(step, 1)
                dve.wait_ge(step, 3)
                nc.vector.tensor_tensor(part[:, 1, :], full[:, :], part[:, 0, :].bitcast(F32),
                                        ALU.subtract).then_inc(step, 1)


def normalise(nc, k, name, x, xt_hi, xt_lo):
    with ExitStack() as ctx:
        sb = lambda n, shape, dt: ctx.enter_context(nc.sbuf_tensor(f"{name}_{n}", shape, dt))
        sem = lambda n: ctx.enter_context(nc.semaphore(f"{name}_{n}"))
        SLOTS = 4
        rows = sb("rows", [P, SLOTS, D], F32)
        flat = sb("flat", [P, 2, D], F32)
        stats = RowStats(nc, k, ctx, name)
        loaded = [sem(f"loaded{s}") for s in range(SLOTS)]
        flat_ready, turned, hi_ready, lo_ready = sem("flat_ready"), sem("turned"), sem("hi_ready"), sem("lo_ready")

        def bank(p):
            return k.psum[:, 2 * p:2 * p + 2, :].rearrange("p a b -> p (a b)")

        with nc.Block() as block:
            @block.sync
            def _(sp):
                def body(j):
                    for p in range(SLOTS):
                        n = j * SLOTS + p
                        wait(sp, flat_ready, n - SLOTS + 1)
                        sp.dma_start(rows[:, p, :], x[n]).then_inc(loaded[p], 16)
                tiles(sp, NT // SLOTS, body)

            @block.vector
            def _(dve):

                def low(n, p):
                    dve.wait_ge(hi_ready, n + 1)
                    cols = bass.ds(n * P, P)
                    nc.vector.tensor_tensor(xt_lo[:, :, cols], bank(p).rearrange("p (k t) -> p k t", t=P),
                                            xt_hi[:, :, cols].bitcast(F32), ALU.subtract).then_inc(lo_ready, 1)

                def moments(n, j, s):
                    dve.wait_ge(loaded[s], (j + 1) * 16)
                    wait(dve, flat_ready, n - 1)
                    stats.moments(dve, n, s % 2, [rows[:, s, h * CH:(h + 1) * CH] for h in range(2)])

                moments(0, 0, 0)

                def body(j):
                    for s in range(SLOTS):
                        n = j * SLOTS + s
                        wait(dve, turned, n - 1)
                        stats.normalise(dve, n, s % 2, flat[:, s % 2, :], rows[:, s, :]).then_inc(flat_ready, 1)
                        if not (isinstance(n, int) and n == NT - 1):
                            moments(n + 1, j + (s + 1) // SLOTS, (s + 1) % SLOTS)
                        if not (isinstance(n, int) and n == 0):
                            low(n - 1, 1 - s % 2)
                tiles(dve, NT // SLOTS, body, last=1)
                low(NT - 1, 1)

            @block.tensor
            def _(pe):
                def body(j):
                    for p in range(2):
                        n = j * 2 + p
                        pe.wait_ge(flat_ready, n + 1)
                        wait(pe, lo_ready, n - 1)
                        for t in range(KT):
                            op = nc.tensor.transpose(bank(p)[:, t * P:(t + 1) * P], flat[:, p, t * P:(t + 1) * P],
                                                     k.ident[:, :])
                        op.then_inc(turned, 1)
                tiles(pe, NT // 2, body)

            @block.gpsimd
            def _(pool):
                def body(j):
                    for p in range(2):
                        stats.invert(pool, j * 2 + p, p)
                tiles(pool, NT // 2, body)

            @block.scalar
            def _(act):
                def high(n, p):
                    wait_apart(act, turned, n + 1, k.passed)
                    nc.scalar.activation(xt_hi[:, :, bass.ds(n * P, P)], bank(p).rearrange("p (k t) -> p k t", t=P),
                                         ACT.Copy).then_inc(hi_ready, 1)

                def body(j):
                    for p in range(2):
                        n = j * 2 + p
                        if not (isinstance(n, int) and n == 0):
                            high(n - 1, 1 - p)
                tiles(act, NT // 2, body)
                high(NT - 1, 1)


NF4_HERE = 3 * KT // 2
SHARES = [range(NQ * max(s - 1, 0) // 6, NQ * min(s, 6) // 6) for s in range(2 * NCH)]


def qkv(nc, k, wqkv, bqkv, w3, xt_hi, xt_lo, q_hi, q_lo, k_hi, k_lo, v_all, dq3):
    with ExitStack() as ctx:
        sb = lambda n, shape, dt: ctx.enter_context(nc.sbuf_tensor(f"qkv_{n}", shape, dt))
        sem = lambda n: ctx.enter_context(nc.semaphore(f"qkv_{n}"))
        raw = sb("raw", [P, 2, KT, P], F32)
        w_hi = sb("w_hi", [P, 2, KT, P], F32R)
        w_lo = sb("w_lo", [P, 2, KT, P], F32R)
        bias = sb("bias", [P, 3 * KT], F32)
        bias_q = sb("bias_q", [P, KT], F32)
        full = sb("full", [P, 2, CH], F32)
        hi = sb("hi", [P, 2, CH], F32R)
        lo = sb("lo", [P, 2, CH], F32R)
        nf4 = Nf4(nc, k, ctx, "w3", 1, 5, raw_slots=1)
        raw_in = [sem(f"raw_in{s}") for s in range(2)]
        bias_in, bias_ready = sem("bias_in"), sem("bias_ready")
        w_hi_ready, w_lo_ready, summed, full_ready = sem("w_hi_ready"), sem("w_lo_ready"), sem("summed"), sem("full_ready")
        hi_ready, lo_ready = sem("hi_ready"), sem("lo_ready")
        stored = [sem(f"stored{s}") for s in range(2)]
        v_stored = [sem(f"v_stored{s}") for s in range(2)]
        dq_stored = sem("dq_stored")
        LAST = 3 * KT
        V0 = 2 * KT

        def kinds(eng, body):
            tiles(eng, KT // 2, lambda j: body(j, 0))
            tiles(eng, KT, lambda j: body(j, 1), first=0, start=KT // 2)
            tiles(eng, 3 * KT // 2, lambda j: body(j, 2), last=1, start=KT)

        def known(n, most):
            return not (isinstance(n, int) and n >= most)

        with nc.Block() as block:
            @block.sync
            def _(sp):
                sp.dma_start(bias[:, :], bqkv).then_inc(bias_in, 16)
                for m in range(2):
                    sp.dma_start(raw[:, m], wqkv[m]).then_inc(raw_in[m], 16)
                nf4.load(sp, 0, 0, 0, w3[0])

                def store_dq(n):
                    sp.wait_ge(nf4.dq_ready, n + 1)
                    sp.dma_start(dq3[n], nf4.dq[:, 0, :]).then_inc(dq_stored, 16)

                def body(j, kind):
                    for p in range(2):
                        m = j * 2 + p
                        if known(m, LAST - 2):
                            sp.wait_ge(w_lo_ready, m + 1)
                            sp.dma_start(raw[:, p], wqkv[m + 2]).then_inc(raw_in[p], 16)
                        if p == 0 and not (isinstance(j, int) and j == 0):
                            store_dq(j - 1)
                        for c in range(NCH):
                            n = m * NCH + c
                            dst = (m - kind * KT) + (c // 2) * HG
                            cols = slice((c % 2) * CH, (c % 2 + 1) * CH)
                            if kind < 2:
                                sp.wait_ge(lo_ready, n + 1)
                                for to, src in (((q_hi, k_hi)[kind], hi), ((q_lo, k_lo)[kind], lo)):
                                    sp.dma_start(to[dst][:, cols], src[:, c % 2, :].bitcast(F32)).then_inc(stored[c % 2], 16)
                            else:
                                sp.wait_ge(full_ready, n + 1)
                                sp.dma_start(v_all[dst][:, cols], full[:, c % 2, :]).then_inc(v_stored[c % 2], 16)
                            if (p, c) == (1, 2) and known(j, NF4_HERE - 1):
                                nf4.load(sp, j + 1, j + 1, 0, w3[j + 1])
                kinds(sp, body)
                store_dq(NF4_HERE - 1)
                for s in range(2):
                    sp.wait_ge(stored[s], 16 * 2 * V0 * 2)
                    sp.wait_ge(v_stored[s], 16 * KT * 2)
                sp.wait_ge(dq_stored, 16 * NF4_HERE)

            @block.scalar
            def _(act):
                def split(m, j, p):
                    act.wait_ge(raw_in[p], 16 * (j + 1))
                    wait(act, summed, NCH * (m - 1))
                    nc.scalar.activation(w_hi[:, p], raw[:, p], ACT.Copy).then_inc(w_hi_ready, 1)

                split(0, 0, 0)

                def body(j, kind):
                    for p in range(2):
                        m = j * 2 + p
                        if known(m, LAST - 1):
                            split(m + 1, j + p, 1 - p)
                        for c in range(NCH):
                            for i in SHARES[p * NCH + c]:
                                nf4.make_sign(act, j, 0, i)
                            n = m * NCH + c
                            if c == 0 and p == 0:
                                act.wait_ge(bias_ready, 1)
                            if kind < 2:
                                wait(act, lo_ready, n - 1)
                            else:
                                act.wait_ge(lo_ready, V0 * NCH)
                                wait(act, v_stored[c % 2], 16 * ((m - V0) * 2 + c // 2))
                            wait_apart(act, summed, n + 1, k.passed)
                            col = bias_q[:, bass.ds(m, 1)] if kind == 0 else bias[:, bass.ds(m, 1)]
                            nc.scalar.activation(full[:, c % 2, :], k.psum[:, c, :], ACT.Identity, bias=col,
                                                 scale=SCALE if kind == 0 else 1.0).then_inc(full_ready, 1)
                kinds(act, body)

            @block.tensor
            def _(pe):
                def body(j, kind):
                    for p in range(2):
                        m = j * 2 + p
                        pe.wait_ge(w_lo_ready, m + 1)
                        for c in range(NCH):
                            wait(pe, full_ready, NCH * (m - 1) + c + 1)
                            cols = slice(c * CH, (c + 1) * CH)
                            terms = [(w, x, t) for t in range(KT) for w, x in ((w_hi, xt_hi), (w_hi, xt_lo), (w_lo, xt_hi))]
                            for i, (w, x, t) in enumerate(terms):
                                op = nc.tensor.matmul(k.psum[:, c, :], w[:, p, t, :], x[:, t, cols],
                                                      start=(i == 0), stop=(i == len(terms) - 1))
                            op.then_inc(summed, 1)
                kinds(pe, body)

            @block.vector
            def _(dve):
                dve.wait_ge(bias_in, 16)
                nc.vector.tensor_scalar(bias_q[:, :], bias[:, 0:KT], SCALE, None, ALU.mult).then_inc(bias_ready, 1)

                def split(m, j, p):
                    dve.wait_ge(w_hi_ready, m + 1)
                    nc.vector.tensor_tensor(w_lo[:, p], raw[:, p], w_hi[:, p].bitcast(F32),
                                            ALU.subtract).then_inc(w_lo_ready, 1)

                split(0, 0, 0)
                nf4.prepare(dve, 0, 0, 0)

                def body(j, kind):
                    for p in range(2):
                        m = j * 2 + p
                        if known(m, LAST - 1):
                            split(m + 1, j + p, 1 - p)
                        for c in range(NCH):
                            for i in SHARES[p * NCH + c]:
                                nf4.take(dve, j, 0, i)
                            if kind < 2:
                                n = m * NCH + c
                                dve.wait_ge(full_ready, n + 1)
                                wait(dve, stored[c % 2], 32 * (m * 2 + c // 2))
                                nc.vector.tensor_copy(hi[:, c % 2, :], full[:, c % 2, :]).then_inc(hi_ready, 1)
                                dve.wait_ge(hi_ready, n + 1)
                                nc.vector.tensor_tensor(lo[:, c % 2, :], full[:, c % 2, :],
                                                        hi[:, c % 2, :].bitcast(F32), ALU.subtract).then_inc(lo_ready, 1)
                            if (p, c) == (1, 2):
                                wait(dve, dq_stored, 16 * j)
                                nf4.finish(dve, j, 0)
                    if known(j, NF4_HERE - 1):
                        nf4.prepare(dve, j + 1, j + 1, 0)
                kinds(dve, body)


def block_rows(step):
    c, t = step
    return max(0, t * P - c * CH)


STEPS2 = [(c, t) for c in range(S // CH) for t in range((c + 1) * CH // P)]
UNITS_HEAD = [(t, a) for t in range(QT) for a in range(0, (t + 1) * P, CH)]
MAX_AT = {u: n for n, u in enumerate(UNITS_HEAD)}


def first_pass_units():
    units = [("v", 0), ("v", 1)]
    later = []
    for i in range(G4):
        for n, u in enumerate(UNITS_HEAD):
            units.append(("s", i, u))
            if n == 3:
                units += later
                later = []
        later = [("m", i, 0), ("m", i, 1)]
    return units + later


UNITS = first_pass_units()
NU = len(UNITS)
NS = len(STEPS2)
TURN_UNITS = [sum(u[0] != "s" for u in UNITS[:n + 1]) for n in range(NU)]
SCORE_UNITS = [n + 1 - TURN_UNITS[n] + sum(u[0] == "s" and u[2] == UNITS_HEAD[-1] for u in UNITS[:n])
               for n in range(NU)]
FINISH = 6
SQ = 32


def schedule():
    events, n = [], 0
    pieces = [(1, k) for k in range(FINISH)], [(0, k) for k in range(FINISH)]
    for s in range(NS):
        ready = lambda n: not (s == NS - 1 and UNITS[n][0] == "m")
        goal = min(NU, NU * (s + 1) // NS + 1)
        for i in range(G4):
            events.append(("scores", s, i))
            if i != 1 and n < goal and ready(n):
                events.append(("unit", n))
                n += 1
        if s == 0:
            turn = [("values", -1, 0), ("values", -1, 1), ("take", 1)]
        else:
            turn = [("values", s - 1, 0), ("values", s - 1, 1)]
            if s == CH // P:
                turn.append(("take", 0))
        for e in turn:
            events.append(e)
            if e[0] == "values" and n < goal and ready(n):
                events.append(("unit", n))
                n += 1
            which = pieces[0] if s <= CH // P else pieces[1]
            if e[0] == "values" and s > 0 and s != CH // P + 1 and which:
                events.append(("finish",) + which.pop(0))
        while n < goal:
            events.append(("unit", n))
            n += 1
    assert not pieces[0] and not pieces[1] and n == NU, pieces
    return events


def attention(nc, k, q_hi, q_lo, k_hi, k_lo, v_all, alibi, att_hi, att_lo):
    SUM_ROWS, ALL_ROWS = 3 * HD + 2, 3 * HD + 4
    ITEMS = NS * G4
    PROBS = 8
    SLOTS = 3
    assert ITEMS % PROBS == 0 and NU % 2 == 0
    EVENTS = schedule()
    with ExitStack() as ctx:
        sb = lambda n, shape, dt: ctx.enter_context(nc.sbuf_tensor(f"heads_{n}", shape, dt))
        sem = lambda n: ctx.enter_context(nc.semaphore(f"heads_{n}"))
        qs = sb("qs", [P, SLOTS, G4, S], F32R)
        ks = sb("ks", [P, SLOTS, G4, S], F32R)
        vt = sb("vt", [P, SLOTS, S], F32)
        v = sb("v", [P, SLOTS, QT, P], F32)
        ones = sb("ones", [P, HD], F32)
        probs = sb("probs", [P, PROBS, CH], F32)
        part_max = sb("part_max", [P, 2, len(UNITS_HEAD)], F32)
        neg_max = sb("neg_max", [P, 2, QT], F32)
        max_rows = sb("max_rows", [P, 2, QT, 4], F32R)
        out_sb = sb("out", [P, 2, CH], F32)
        sum_sb = sb("sum", [P, 2, CH], F32)
        turned = sb("turned", [P, CH], F32)
        inv_few = sb("inv_few", [P, CH // SQ], F32)
        inv = sb("inv", [P, CH], F32)
        full = sb("full", [P, CH], F32)
        hi = sb("hi", [P, 2, CH], F32R)
        lo = sb("lo", [P, 2, CH], F32R)
        loaded = [sem(f"loaded{s}") for s in range(SLOTS)]
        stored = [sem(f"stored{s}") for s in range(2)]
        first_loaded = sem("first_loaded")
        LOADS = 8
        set_up, ks_set = sem("set_up"), sem("ks_set")
        unit_done, max_read, turn_read = sem("unit_done"), sem("max_read"), sem("turn_read")
        split_hi, split_lo = sem("split_hi"), sem("split_lo")
        scored, exped, used = sem("scored"), sem("exped"), sem("used")
        out_read, inv_ready, full_ready = sem("out_read"), sem("inv_ready"), sem("full_ready")
        hi_ready, lo_ready = sem("hi_ready"), sem("lo_ready")
        turned_ready, inverted = sem("turned_ready"), sem("inverted")
        S2_BANKS = 4
        OUT, SUM = 6, 7
        NSC, NTU = G4 * (len(UNITS_HEAD) + 1), TURN_UNITS[-1]

        def unit_bank(n):
            return S2_BANKS + n % 2

        def groups(eng, body):
            def three(j):
                for p in range(SLOTS):
                    body(j * SLOTS + p, j, p, True)
            tiles(eng, GROUPS // SLOTS, three, last=1)
            assert GROUPS % SLOTS == 1
            body(GROUPS - 1, GROUPS // SLOTS, 0, False)

        def first(g):
            return isinstance(g, int) and g == 0

        with nc.Block() as block:
            @block.sync
            def _(sp):
                def load(g, p):
                    wait(sp, scored, ITEMS * (g - SLOTS + 1))
                    for to, rows, src in ((qs, 0, q_hi), (qs, 1, q_hi), (qs, 2, q_lo),
                                          (ks, 0, k_hi), (ks, 1, k_lo), (ks, 2, k_hi)):
                        dst = to[rows * HD:(rows + 1) * HD, p, :, :].bitcast(F32)
                        sp.dma_start(dst, src[g].rearrange("(i r) t -> r i t", r=HD)).then_inc(loaded[p], 16)
                    sp.dma_start(vt[:, p, :], v_all[g]).then_inc(loaded[p], 16)
                    if isinstance(g, int) and g < SLOTS:
                        sp.wait_ge(ks_set, g + 1)
                    sp.dma_start(ks[3 * HD:3 * HD + 2, p, :, :].bitcast(F32), alibi[g]).then_inc(loaded[p], 16)

                def store(g, c):
                    sp.wait_ge(lo_ready, 2 * g + c + 1)
                    for to, src in ((att_hi, hi), (att_lo, lo)):
                        sp.dma_start(to[g, c], src[:, c, :].bitcast(F32)).then_inc(stored[c], 16)

                sp.dma_start(vt[:, 0, :], v_all[0]).then_inc(first_loaded, 16)
                for heads, sem_in in ((slice(0, 1), first_loaded), (slice(1, G4), loaded[0])):
                    for to, rows, src in ((qs, 0, q_hi), (qs, 1, q_hi), (qs, 2, q_lo),
                                          (ks, 0, k_hi), (ks, 1, k_lo), (ks, 2, k_hi)):
                        dst = to[rows * HD:(rows + 1) * HD, 0, heads, :].bitcast(F32)
                        sp.dma_start(dst, src[0].rearrange("(i r) t -> r i t", r=HD)[:, heads, :]).then_inc(sem_in, 16)
                    if heads.start == 0:
                        sp.wait_ge(ks_set, 1)
                        sp.dma_start(ks[3 * HD:3 * HD + 2, 0, :, :].bitcast(F32), alibi[0]).then_inc(first_loaded, 16)
                load(1, 1)

                def body(g, j, p, more):
                    if not (isinstance(g, int) and g >= GROUPS - 2):
                        load(g + 2, (p + 2) % SLOTS)
                    if not first(g):
                        store(g - 1, 1)
                    store(g, 0)
                groups(sp, body)
                store(GROUPS - 1, 1)
                for c in range(2):
                    sp.wait_ge(stored[c], 32 * GROUPS)

            @block.tensor
            def _(pe):
                def unit(g, p, n):
                    what = UNITS[n]
                    if n >= 2:
                        before = (max_read, NSC * g + SCORE_UNITS[n - 2]) if UNITS[n - 2][0] == "s" else \
                                 (turn_read, NTU * g + TURN_UNITS[n - 2])
                    else:
                        assert UNITS[NU - 2][0] == UNITS[NU - 1][0] == "m"
                        before = (turn_read, NTU * (g - 1) + TURN_UNITS[NU - 2 + n])
                    if not (first(g) and n < 2):
                        pe.wait_ge(*before)
                    bank = k.psum[:, unit_bank(n), :]
                    if what[0] == "v":
                        for t in range(4):
                            cols = slice((4 * what[1] + t) * P, (4 * what[1] + t + 1) * P)
                            op = nc.tensor.transpose(bank[:, t * P:(t + 1) * P], vt[:, p, cols], k.ident[:, :])
                    elif what[0] == "m":
                        i = what[1]
                        pe.wait_ge(split_lo, G4 * g + i + 1)
                        for t in range(4):
                            op = nc.tensor.transpose(bank[0:4, t * P:(t + 1) * P],
                                                     max_rows[:, i % 2, 4 * what[2] + t, :].bitcast(F32), k.ident[:, :])
                    else:
                        i, (t, a) = what[1:]
                        width = min(CH, (t + 1) * P - a)
                        last = a + width == (t + 1) * P
                        wide = max(width, FAST)
                        op = nc.tensor.matmul(bank[:, 0:wide], qs[0:SUM_ROWS, p, i, t * P:(t + 1) * P],
                                              ks[0:SUM_ROWS, p, i, a:a + wide], start=True, stop=not last)
                        if last:
                            op = nc.tensor.matmul(bank[:, width - P:width], k.ident16[:, :], k.mask_q[:, :],
                                                  start=False, stop=True)
                    op.then_inc(unit_done, 1)

                def scores(g, p, s, i):
                    c, t = STEPS2[s]
                    n = g * ITEMS + s * G4 + i
                    wait(pe, exped, n - S2_BANKS + 1)
                    if s == 0:
                        pe.wait_ge(turn_read, NTU * g + TURN_UNITS[UNITS.index(("m", i, 1))])
                    skip = block_rows((c, t))
                    wide = min(skip, CH - FAST)
                    diagonal = t * P >= c * CH
                    op = nc.tensor.matmul(k.psum[:, i, wide:CH], ks[0:ALL_ROWS, p, i, t * P:(t + 1) * P],
                                          qs[0:ALL_ROWS, p, i, c * CH + wide:(c + 1) * CH], start=True, stop=not diagonal)
                    if diagonal:
                        op = nc.tensor.matmul(k.psum[:, i, skip:skip + P], k.ident16[:, :], k.mask_k[:, :],
                                              start=False, stop=True)
                    op.then_inc(scored, 1)

                def values(g, p, s, what):
                    c, t = STEPS2[s]
                    if what == 0:
                        if t == 0:
                            wait(pe, out_read, 2 * (2 * g + c))
                        pe.wait_ge(exped, g * ITEMS + (s + 1) * G4)
                    skip = block_rows((c, t))
                    end = t == (c + 1) * CH // P - 1
                    to = (OUT, SUM)[what]
                    for i in range(G4):
                        lhs = v[:, p, t, i * HD:(i + 1) * HD] if to == OUT else ones[:, :]
                        op = nc.tensor.matmul(k.psum[i * HD:(i + 1) * HD, to, skip:CH], lhs,
                                              probs[:, (s * G4 + i) % PROBS, skip:CH], start=(t == 0), stop=end)
                    if what:
                        op.then_inc(used, 1)

                pe.wait_ge(set_up, SLOTS + 1)
                pe.wait_ge(first_loaded, 16 * LOADS)
                for n in range(NU):
                    if n == UNITS.index(("s", 1, UNITS_HEAD[0])):
                        pe.wait_ge(loaded[0], 16 * (LOADS - 2))
                    unit(0, 0, n)

                def body(g, j, p, more):
                    if more:
                        to = (p + 1) % SLOTS
                        count = LOADS * (j + (p + 1) // SLOTS + 1) - (2 if to == 0 else 0)
                        pe.wait_ge(loaded[to], 16 * count)
                    for e in EVENTS:
                        if e[0] == "scores":
                            scores(g, p, e[1], e[2])
                        elif e[0] == "unit" and more:
                            unit(g + 1, (p + 1) % SLOTS, e[1])
                        elif e[0] == "values" and e[1] >= 0:
                            values(g, p, e[1], e[2])
                        elif e[0] == "values" and not first(g):
                            values(g - 1, (p - 1) % SLOTS, NS - 1, e[2])
                groups(pe, body)
                for what in range(2):
                    values(GROUPS - 1, 0, NS - 1, what)

            @block.scalar
            def _(act):
                def take_out(g, c):
                    act.wait_ge(used, g * NS + sum((cc + 1) * CH // P for cc in range(c + 1)))
                    wait(act, full_ready, 2 * g + c - 1)
                    nc.scalar.activation(out_sb[:, c, :], k.psum[:, OUT, :], ACT.Copy).then_inc(out_read, 1)
                    nc.scalar.activation(sum_sb[:, c, :], k.psum[:, SUM, :], ACT.Copy).then_inc(out_read, 1)

                def unit(g, p, n):
                    what = UNITS[n]
                    bank = k.psum[:, unit_bank(n), :]
                    if what[0] == "s":
                        return
                    act.wait_ge(unit_done, NU * g + n + 1)
                    if what[0] == "v":
                        wait(act, used, NS * (g - SLOTS + 1))
                        out = v[:, p, 4 * what[1]:4 * what[1] + 4, :].rearrange("p t c -> p (t c)")
                        nc.scalar.activation(out, bank, ACT.Copy).then_inc(turn_read, 1)
                    else:
                        out = qs[3 * HD:ALL_ROWS, p, what[1], what[2] * CH:(what[2] + 1) * CH]
                        nc.scalar.activation(out, bank[0:4, :], ACT.Copy).then_inc(turn_read, 1)

                def exp(g, s, i):
                    skip = block_rows(STEPS2[s])
                    act.wait_ge(scored, g * ITEMS + s * G4 + i + 1)
                    if not (first(g) and s < 2):
                        act.wait_ge(used, g * NS + s - 1)
                    nc.scalar.activation(probs[:, (s * G4 + i) % PROBS, skip:CH], k.psum[:, i, skip:CH],
                                         ACT.Exp).then_inc(exped, 1)

                for n in range(NU):
                    unit(0, 0, n)

                def body(g, j, p, more):
                    for e in EVENTS:
                        if e[0] == "scores":
                            exp(g, e[1], e[2])
                        elif e[0] == "unit" and more:
                            unit(g + 1, (p + 1) % SLOTS, e[1])
                        elif e == ("take", 0):
                            take_out(g, 0)
                        elif e == ("take", 1) and not first(g):
                            take_out(g - 1, 1)
                groups(act, body)
                take_out(GROUPS - 1, 1)

            @block.gpsimd
            def _(pool):
                for p in range(SLOTS):
                    nc.gpsimd.memset(ks[3 * HD:ALL_ROWS, p, :, :].bitcast(F32), 1.0).then_inc(ks_set, 1)

            @block.vector
            def _(dve):
                for p in range(SLOTS):
                    nc.vector.memset(qs[3 * HD:ALL_ROWS, p, :, :].bitcast(F32), 1.0).then_inc(set_up, 1)
                nc.vector.memset(max_rows[:, :, :, :].bitcast(F32), 1.0)
                nc.vector.memset(ones[:, :], 1.0).then_inc(set_up, 1)
                dve.wait_ge(set_up, SLOTS + 1)

                def unit(g, n):
                    what = UNITS[n]
                    if what[0] != "s":
                        return
                    i, (t, a) = what[1:]
                    dve.wait_ge(unit_done, NU * g + n + 1)
                    width = min(CH, (t + 1) * P - a)
                    at = MAX_AT[what[2]]
                    nc.vector.reduce_max(part_max[:, i % 2, at:at + 1], k.psum[:, unit_bank(n), 0:width], AX.X,
                                         negate=True).then_inc(max_read, 1)
                    if what[2] != UNITS_HEAD[-1]:
                        return
                    dve.wait_ge(max_read, NSC * g + SCORE_UNITS[n])
                    if i >= 2:
                        dve.wait_ge(turn_read, NTU * g + TURN_UNITS[UNITS.index(("m", i - 2, 1))])
                    elif not first(g):
                        dve.wait_ge(turn_read, NTU * (g - 1) + TURN_UNITS[UNITS.index(("m", i + 2, 1))])
                    one = CH // P
                    parts = part_max[:, i % 2, one:].rearrange("p (t a) -> p t a", a=2)
                    nc.vector.tensor_copy(neg_max[:, i % 2, 0:one], part_max[:, i % 2, 0:one])
                    nc.vector.tensor_tensor(neg_max[:, i % 2, one:], parts[:, :, 0], parts[:, :, 1],
                                            ALU.min).then_inc(max_read, 1)
                    dve.wait_ge(max_read, NSC * g + SCORE_UNITS[n] + 1)
                    nc.vector.tensor_copy(max_rows[:, i % 2, :, 2], neg_max[:, i % 2, :]).then_inc(split_hi, 1)
                    dve.wait_ge(split_hi, G4 * g + i + 1)
                    nc.vector.tensor_tensor(max_rows[:, i % 2, :, 3], neg_max[:, i % 2, :],
                                            max_rows[:, i % 2, :, 2].bitcast(F32), ALU.subtract).then_inc(split_lo, 1)

                def finish(g, c, piece):
                    n = 2 * g + c
                    squares = lambda tensor: tensor.rearrange("p (b k) -> p b k", k=SQ)
                    if piece == 0:
                        dve.wait_ge(out_read, 2 * (n + 1))
                        wait(dve, inverted, n)
                        nc.vector.transpose(turned[:, :], sum_sb[:, c, :]).then_inc(turned_ready, 1)
                    elif piece == 1:
                        dve.wait_ge(turned_ready, n + 1)
                        wait(dve, inv_ready, n)
                        nc.vector.reciprocal(inv_few[:, :], squares(turned[:, :])[:, :, 0]).then_inc(inverted, 1)
                    elif piece == 2:
                        dve.wait_ge(inverted, n + 1)
                        wait(dve, full_ready, n)
                        spread = inv_few[:, :].unsqueeze(2).broadcast_to([P, CH // SQ, SQ])
                        nc.vector.transpose(squares(inv[:, :]), spread).then_inc(inv_ready, 1)
                    elif piece == 3:
                        dve.wait_ge(inv_ready, n + 1)
                        wait(dve, lo_ready, n)
                        nc.vector.tensor_tensor(full[:, :], out_sb[:, c, :], inv[:, :], ALU.mult).then_inc(full_ready, 1)
                    elif piece == 4:
                        dve.wait_ge(full_ready, n + 1)
                        wait(dve, stored[c], 32 * g)
                        nc.vector.tensor_copy(hi[:, c, :], full[:, :]).then_inc(hi_ready, 1)
                    else:
                        dve.wait_ge(hi_ready, n + 1)
                        nc.vector.tensor_tensor(lo[:, c, :], full[:, :], hi[:, c, :].bitcast(F32),
                                                ALU.subtract).then_inc(lo_ready, 1)

                for n in range(NU):
                    unit(0, n)

                def body(g, j, p, more):
                    for e in EVENTS:
                        if e[0] == "unit" and more:
                            unit(g + 1, e[1])
                        elif e[0] == "finish" and e[1] == 0:
                            finish(g, 0, e[2])
                        elif e[0] == "finish" and not first(g):
                            finish(g - 1, 1, e[2])
                groups(dve, body)
                for piece in range(FINISH):
                    finish(GROUPS - 1, 1, piece)


def out_project(nc, k, wout, bout, x, w12, att_hi, att_lo, x2, dq12):
    with ExitStack() as ctx:
        sb = lambda n, shape, dt: ctx.enter_context(nc.sbuf_tensor(f"out_{n}", shape, dt))
        sem = lambda n: ctx.enter_context(nc.semaphore(f"out_{n}"))
        raw = sb("raw", [P, 2, D], F32)
        w_hi = sb("w_hi", [P, KT, D], F32R)
        w_lo = sb("w_lo", [P, KT, D], F32R)
        a_hi = sb("a_hi", [P, 2, HG, CH], F32R)
        a_lo = sb("a_lo", [P, 2, HG, CH], F32R)
        bias = sb("bias", [P, D], F32)
        rows = sb("rows", [P, 2, D], F32)
        y = sb("y", [P, 2, D], F32)
        stats = RowStats(nc, k, ctx, "out")
        nf4 = Nf4(nc, k, ctx, "w12_first", 1, 5, raw_slots=1)
        dq_stored = sem("dq_stored")
        raw_in = [sem(f"raw_in{s}") for s in range(2)]
        rows_in = [sem(f"rows_in{s}") for s in range(2)]
        att_in = [sem(f"att_in{s}") for s in range(2)]
        att_first = [sem(f"att_first{t}") for t in range(KT)]
        stored = [sem(f"stored{s}") for s in range(2)]
        bias_in = sem("bias_in")
        hi_ready, lo_ready, summed, biased = sem("hi_ready"), sem("lo_ready"), sem("summed"), sem("biased")
        flat_ready, added = sem("flat_ready"), sem("added")
        TILES = CH // P

        with nc.Block() as block:
            @block.sync
            def _(sp):
                sp.dma_start(bias[:, :], bout.partition_broadcast(P)).then_inc(bias_in, 16)

                def load_att(u, s):
                    wait(sp, summed, TILES * (u - 1))
                    for to, src in ((a_hi, att_hi), (a_lo, att_lo)):
                        sp.dma_start(to[:, s, :, :].bitcast(F32), src[u]).then_inc(att_in[s], 16)

                for t in range(KT):
                    wait(sp, lo_ready, t - 1)
                    sp.dma_start(raw[:, t % 2, :], wout[t]).then_inc(raw_in[t % 2], 16)
                    for to, src in ((a_hi, att_hi), (a_lo, att_lo)):
                        sp.dma_start(to[:, 0, t, :].bitcast(F32), src[0][:, t, :]).then_inc(att_first[t], 16)
                load_att(1, 1)

                def body(u):
                    for i in range(TILES):
                        n = u * TILES + i
                        wait(sp, added, n - 1)
                        sp.dma_start(rows[:, i % 2, :], x[n]).then_inc(rows_in[i % 2], 16)
                        if not (isinstance(n, int) and n == 0):
                            sp.wait_ge(added, n)
                            sp.dma_start(x2[n - 1], y[:, (i - 1) % 2, :]).then_inc(stored[(i - 1) % 2], 16)
                tiles(sp, 1, body)
                for u in range(1, NCH):
                    if u + 1 < NCH:
                        load_att(u + 1, (u + 1) % 2)
                    body(u)
                sp.wait_ge(added, NT)
                sp.dma_start(x2[NT - 1], y[:, (NT - 1) % 2, :]).then_inc(stored[(NT - 1) % 2], 16)
                for s in range(2):
                    sp.wait_ge(stored[s], 16 * NT // 2)

            @block.scalar
            def _(act):
                for t in range(KT):
                    act.wait_ge(raw_in[t % 2], 16 * (t // 2 + 1))
                    nc.scalar.activation(w_hi[:, t, :], raw[:, t % 2, :], ACT.Copy).then_inc(hi_ready, 1)
                for n in range(2):
                    nf4.load(act, n, n, 0, w12[n])
                    for i in range(NQ):
                        nf4.make_sign(act, n, 0, i)
                    act.wait_ge(nf4.dq_ready, n + 1)
                    act.dma_start(dq12[n], nf4.dq[:, 0, :]).then_inc(dq_stored, 16)
                act.wait_ge(dq_stored, 32)

            @block.gpsimd
            def _(pool):
                def body(j):
                    for p in range(2):
                        stats.invert(pool, j * 2 + p, p)
                tiles(pool, NT // 2, body)

            @block.tensor
            def _(pe):
                def products(u, s, i, t):
                    for h in range(2):
                        for m, (a, w) in enumerate(((a_hi, w_hi), (a_hi, w_lo), (a_lo, w_hi))):
                            op = nc.tensor.matmul(k.psum[:, 2 * i + h, :], a[:, s, t, i * P:(i + 1) * P],
                                                  w[:, t, h * CH:(h + 1) * CH], start=(t == 0 and m == 0),
                                                  stop=(t == KT - 1 and m == 2))
                    if t == KT - 1:
                        op.then_inc(summed, 1)

                for t in range(KT):
                    pe.wait_ge(att_first[t], 32)
                    pe.wait_ge(lo_ready, t + 1)
                    for i in range(TILES):
                        products(0, 0, i, t)

                for u in range(1, NCH):
                    pe.wait_ge(att_in[u % 2], 32 * ((u + 1) // 2))
                    for i in range(TILES):
                        pe.wait_ge(biased, 2 * ((u - 1) * TILES + i + 1))
                        for t in range(KT):
                            products(u, u % 2, i, t)

            @block.vector
            def _(dve):
                for t in range(KT):
                    dve.wait_ge(hi_ready, t + 1)
                    nc.vector.tensor_tensor(w_lo[:, t, :], raw[:, t % 2, :], w_hi[:, t, :].bitcast(F32),
                                            ALU.subtract).then_inc(lo_ready, 1)
                dve.wait_ge(bias_in, 16)

                def body(v):
                    nf4.prepare(dve, v, v, 0)
                    for i in range(2 * TILES):
                        n = v * 2 * TILES + i
                        p = i % 2
                        dve.wait_ge(summed, n + 1)
                        wait(dve, stored[p], 16 * (v * TILES + i // 2))
                        for h in range(2):
                            cols = slice(h * CH, (h + 1) * CH)
                            nc.vector.tensor_tensor(y[:, p, cols], k.psum[:, 2 * (i % TILES) + h, :], bias[:, cols],
                                                    ALU.add).then_inc(biased, 1)
                        dve.wait_ge(biased, 2 * (n + 1))
                        wait(dve, flat_ready, n - 1)
                        stats.moments(dve, n, p, [y[:, p, h * CH:(h + 1) * CH] for h in range(2)])
                        for m in range(i * NQ // (2 * TILES), (i + 1) * NQ // (2 * TILES)):
                            nf4.take(dve, v, 0, m)
                        stats.normalise(dve, n, p, y[:, p, :], y[:, p, :]).then_inc(flat_ready, 1)
                        dve.wait_ge(flat_ready, n + 1)
                        dve.wait_ge(rows_in[p], 16 * (v * TILES + i // 2 + 1))
                        nc.vector.tensor_tensor(y[:, p, :], y[:, p, :], rows[:, p, :], ALU.add).then_inc(added, 1)
                    wait(dve, dq_stored, 16 * v)
                    nf4.finish(dve, v, 0)
                for v in range(2):
                    body(v)


VECTOR_PLAN = {4: [("low", 1)], 7: [("product", -1)], 9: [("prepare", 1)], 10: [("rest", -1)],
               13: [("product", 0)], 14: [("finish", 0)], 16: [("rest", 0)], 20: [("product", 1)],
               22: [("low", 0), ("prepare", 0)], 23: [("rest", 1)], 26: [("product", 2)], 
               29: [("finish", 1), ("rest", 2)]}
SCALAR_PLAN = {3: [("high", 1)], 10: [("part", -1)], 11: [("gate", 0)], 16: [("part", 0)], 18: [("gate", 1)],
               22: [("high", 0)], 23: [("part", 1)], 26: [("gate", 2)], 29: [("part", 2), ("gate", 3)]}


def gate_up(nc, k, w12, dq12, xt_hi, xt_lo, h_hi, h_lo):
    with ExitStack() as ctx:
        sb = lambda n, shape, dt: ctx.enter_context(nc.sbuf_tensor(f"gu_{n}", shape, dt))
        sem = lambda n: ctx.enter_context(nc.semaphore(f"gu_{n}"))
        w_hi = sb("w_hi", [P, 2, 2, KT, P], F32R)
        w_lo = sb("w_lo", [P, 2, 2, KT, P], F32R)
        act_gate = sb("act_gate", [P, 2, CH], F32)
        full = sb("full", [P, 2, CH], F32)
        hi = sb("hi", [P, 2, CH], F32R)
        lo = sb("lo", [P, 2, CH], F32R)
        nf4 = Nf4(nc, k, ctx, "w12", 1, 3)
        turned, hi_ready, lo_ready = sem("turned"), sem("w_hi_ready"), sem("w_lo_ready")
        summed, gated, multiplied = sem("summed"), sem("gated"), sem("multiplied")
        h_hi_ready, h_lo_ready = sem("h_hi_ready"), sem("h_lo_ready")
        stored = [sem(f"stored{s}") for s in range(2)]
        first_in = [sem(f"first_in{s}") for s in range(2)]
        GATE, UP, TURN = 0, 2, 4

        def turn_banks(u):
            return k.psum[:, TURN + 2 * u:TURN + 2 * u + 2, :].rearrange("p a b -> p (a b)")

        def first(t):
            return isinstance(t, int) and t == 0

        def last(t):
            return isinstance(t, int) and t >= FT - 1

        def steps(eng, body):
            def two(j):
                for q in range(2):
                    body(j * 2 + q, j, q)
            tiles(eng, FT // 2, two, last=1)

        with nc.Block() as block:
            @block.sync
            def _(sp):
                for n, to in enumerate((nf4.dq[:, 0, :], nf4.code[:, 1, :])):
                    sp.dma_start(to, dq12[n]).then_inc(first_in[n], 16)
                    nf4.load(sp, n, 0, n, w12[n + 2])

                def store(t, c):
                    sp.wait_ge(h_lo_ready, t * NCH + c + 1)
                    cols = slice(c * CH, (c + 1) * CH)
                    for to, src in ((h_hi, hi), (h_lo, lo)):
                        sp.dma_start(to[t][:, cols], src[:, c % 2, :].bitcast(F32)).then_inc(stored[c % 2], 16)

                def body(t, j, q):
                    more = not (isinstance(t, int) and t >= FT - 2)
                    if not first(t):
                        store(t - 1, NCH - 1)
                    if more:
                        nf4.load(sp, 2 * t + 2, t + 1, 0, w12[2 * t + 4])
                    for c in range(NCH - 1):
                        store(t, c)
                    if more:
                        nf4.load(sp, 2 * t + 3, t + 1, 1, w12[2 * t + 5])
                steps(sp, body)
                store(FT - 1, NCH - 1)
                for s in range(2):
                    sp.wait_ge(stored[s], 32 * 2 * FT)

            @block.scalar
            def _(act):
                def high(n, t, q, u):
                    act.wait_ge(turned, n + 1)
                    wait(act, summed, 2 * NCH * (t - 1))
                    nc.scalar.activation(w_hi[:, q, u], turn_banks(u).rearrange("p (k h) -> p k h", h=P),
                                         ACT.Copy).then_inc(hi_ready, 1)

                def gate(t, c):
                    act.wait_ge(summed, 2 * (NCH * t + c) + 1)
                    wait(act, multiplied, NCH * t + c - 1)
                    nc.scalar.activation(act_gate[:, c % 2, :], k.psum[:, GATE + c % 2, :], ACT.Silu).then_inc(gated, 1)

                def part(t, c):
                    act.wait_ge(multiplied, NCH * t + c + 1)
                    wait(act, stored[c % 2], 32 * (2 * t + c // 2))
                    nc.scalar.activation(hi[:, c % 2, :], full[:, c % 2, :], ACT.Copy).then_inc(h_hi_ready, 1)

                high(0, 0, 0, 0)
                act.wait_ge(turned, 2)

                def body(t, j, q):
                    for m in range(2 * NQ):
                        if not last(t):
                            nf4.make_sign(act, 2 * t + m // NQ, m // NQ, m % NQ)
                        for what, c in SCALAR_PLAN.get(m, ()):
                            if what == "gate":
                                gate(t, c)
                            elif what == "part" and c >= 0:
                                part(t, c)
                            elif what == "part" and not first(t):
                                part(t - 1, NCH - 1)
                            elif what == "high" and c == 1:
                                high(2 * t + 1, t, q, 1)
                            elif what == "high" and not last(t):
                                high(2 * t + 2, t + 1, 1 - q, 0)
                steps(act, body)
                part(FT - 1, NCH - 1)

            @block.tensor
            def _(pe):
                def turn(n, u, src):
                    wait(pe, lo_ready, n - 1)
                    for t in range(KT):
                        op = nc.tensor.transpose(turn_banks(u)[:, t * P:(t + 1) * P], src[:, t * P:(t + 1) * P],
                                                 k.ident[:, :])
                    op.then_inc(turned, 1)

                def turn_rounded(n, u):
                    pe.wait_ge(nf4.dq_ready, n - 1)
                    turn(n, u, nf4.dq[:, 0, :])

                for n, src in enumerate((nf4.dq[:, 0, :], nf4.code[:, 1, :])):
                    pe.wait_ge(first_in[n], 16)
                    turn(n, n, src)

                def body(t, j, q):
                    for c in range(NCH):
                        cols = slice(c * CH, (c + 1) * CH)
                        n = t * NCH + c
                        for u, to, free in ((0, GATE, gated), (1, UP, multiplied)):
                            if c == 0:
                                pe.wait_ge(lo_ready, 2 * t + u + 1)
                            wait(pe, free, n - 1)
                            terms = [(w, x, m) for m in range(KT)
                                     for w, x in ((w_hi, xt_hi), (w_hi, xt_lo), (w_lo, xt_hi))]
                            for i, (w, x, m) in enumerate(terms):
                                op = nc.tensor.matmul(k.psum[:, to + c % 2, :], w[:, q, u, m, :], x[:, m, cols],
                                                      start=(i == 0), stop=(i == len(terms) - 1))
                            op.then_inc(summed, 1)
                            if (c, u) == (1, 1) and not last(t):
                                turn_rounded(2 * t + 2, 0)
                            if (c, u) == (3, 0) and not last(t):
                                turn_rounded(2 * t + 3, 1)
                steps(pe, body)

            @block.vector
            def _(dve):

                def low(n, q, u):
                    dve.wait_ge(hi_ready, n + 1)
                    nc.vector.tensor_tensor(w_lo[:, q, u], turn_banks(u).rearrange("p (k h) -> p k h", h=P),
                                            w_hi[:, q, u].bitcast(F32), ALU.subtract).then_inc(lo_ready, 1)

                def finish(n, u):
                    wait(dve, turned, n)
                    nf4.finish(dve, n - 2, u)

                nf4.prepare(dve, 0, 0, 0)
                low(0, 0, 0)

                def product(t, c):
                    n = t * NCH + c
                    dve.wait_ge(summed, 2 * (n + 1))
                    dve.wait_ge(gated, n + 1)
                    wait(dve, h_lo_ready, n - 1)
                    nc.vector.tensor_tensor(full[:, c % 2, :], act_gate[:, c % 2, :], k.psum[:, UP + c % 2, :],
                                            ALU.mult).then_inc(multiplied, 1)

                def rest(t, c):
                    dve.wait_ge(h_hi_ready, t * NCH + c + 1)
                    nc.vector.tensor_tensor(lo[:, c % 2, :], full[:, c % 2, :], hi[:, c % 2, :].bitcast(F32),
                                            ALU.subtract).then_inc(h_lo_ready, 1)

                def body(t, j, q):
                    for m in range(2 * NQ):
                        if not last(t):
                            nf4.take(dve, 2 * t + m // NQ, m // NQ, m % NQ)
                        for what, c in VECTOR_PLAN.get(m, ()):
                            if what in ("product", "rest"):
                                do = product if what == "product" else rest
                                if c >= 0:
                                    do(t, c)
                                elif not first(t):
                                    do(t - 1, NCH - 1)
                            elif what == "low" and c == 1:
                                low(2 * t + 1, q, 1)
                            elif last(t):
                                pass
                            elif what == "low":
                                low(2 * t + 2, 1 - q, 0)
                            elif what == "finish":
                                finish(2 * t + 2 + c, c)
                            elif c == 1:
                                nf4.prepare(dve, 2 * t + 1, t, 1)
                            elif not (isinstance(t, int) and t >= FT - 2):
                                nf4.prepare(dve, 2 * t + 2, t + 1, 0)
                steps(dve, body)
                product(FT - 1, NCH - 1)
                rest(FT - 1, NCH - 1)


def down(nc, k, w3, dq3, h_hi, h_lo, x2, partial, out):
    ROUNDED = FT - NF4_HERE
    SOON = FT // 2 - 1
    assert FT // 2 <= NF4_HERE and ROUNDED % 2 == 0
    HALF = FT // 2
    EARLY = 2
    SLOTS = HALF + EARLY
    with ExitStack() as ctx:
        sb = lambda n, shape, dt: ctx.enter_context(nc.sbuf_tensor(f"down_{n}", shape, dt))
        sem = lambda n: ctx.enter_context(nc.semaphore(f"down_{n}"))
        w_hi = sb("w_hi", [P, SLOTS, D], F32R)
        w_lo = sb("w_lo", [P, SLOTS, D], F32R)
        dq = sb("dq", [P, 2, D], F32)
        a_hi = sb("a_hi", [P, 2, HALF, P], F32R)
        a_lo = sb("a_lo", [P, 2, HALF, P], F32R)
        rows = sb("rows", [P, 2, D], F32)
        before = sb("before", [P, 2, D], F32)
        y = sb("y", [P, 2, D], F32)
        stats = RowStats(nc, k, ctx, "down")
        nf4 = Nf4(nc, k, ctx, "w3_rest", 2, 5)
        dq_stored = [sem(f"dq_stored{s}") for s in range(2)]
        dq_in = [sem(f"dq_in{s}") for s in range(2)]
        a_in = [sem(f"a_in{s}") for s in range(2)]
        rows_in = [sem(f"rows_in{s}") for s in range(2)]
        stored = [sem(f"stored{s}") for s in range(2)]
        kept = [sem(f"kept{s}") for s in range(2)]
        turned, hi_ready, lo_ready, summed = sem("turned"), sem("hi_ready"), sem("lo_ready"), sem("summed")
        taken, flat_ready, added = sem("taken"), sem("flat_ready"), sem("added")

        def acc_bank(p):
            return k.psum[:, 2 * p:2 * p + 2, :].rearrange("p a b -> p (a b)")

        def turn_bank(p):
            return k.psum[:, 4 + 2 * p:6 + 2 * p, :].rearrange("p a b -> p (a b)")

        with nc.Block() as block:
            @block.sync
            def _(sp):
                def load(m, n, j, p):
                    wait(sp, summed, m * NT + n - 1)
                    for to, src in ((a_hi, h_hi), (a_lo, h_lo)):
                        cols = bass.ds(n * P, P)
                        sp.dma_start(to[:, p].bitcast(F32),
                                     src[m * HALF:(m + 1) * HALF, :, cols].rearrange("t p c -> p t c")).then_inc(a_in[p], 16)

                def weights(first, end):
                    for c in range(first, end):
                        wait(sp, turned, c - 1)
                        if c >= NF4_HERE:
                            n = c - NF4_HERE
                            sp.wait_ge(dq_stored[n % 2], 16 * (n // 2 + 1))
                        sp.dma_start(dq[:, c % 2, :], dq3[c]).then_inc(dq_in[c % 2], 16)

                load(0, 0, 0, 0)
                load(0, 1, 0, 1)
                weights(0, HALF)

                def first(j):
                    for p in range(2):
                        n = j * 2 + p
                        if isinstance(n, int) and n in (NT - 4, NT - 2):
                            c = HALF + n - (NT - 4)
                            weights(c, c + 2)
                        if not (isinstance(n, int) and n >= NT - 2):
                            load(0, n + 2, j + 1, p)
                        sp.wait_ge(taken, n + 1)
                        sp.dma_start(partial[n], y[:, p, :]).then_inc(kept[p], 16)
                tiles(sp, NT // 2, first, last=2)
                load(1, 0, 0, 0)
                load(1, 1, 0, 1)
                weights(HALF + 4, FT)
                for s in range(2):
                    sp.wait_ge(kept[s], 16 * NT // 2)

                def rest(n, j, p):
                    wait(sp, added, n - 1)
                    sp.dma_start(before[:, p, :], partial[n]).then_inc(rows_in[p], 16)
                    sp.dma_start(rows[:, p, :], x2[n]).then_inc(rows_in[p], 16)
                rest(0, 0, 0)

                def second(j):
                    for p in range(2):
                        n = j * 2 + p
                        if not (isinstance(n, int) and n == NT - 1):
                            rest(n + 1, j + p, 1 - p)
                        if not (isinstance(n, int) and n >= NT - 2):
                            load(1, n + 2, j + 1, p)
                        sp.wait_ge(added, n + 1)
                        sp.dma_start(out[n], y[:, p, :]).then_inc(stored[p], 16)
                tiles(sp, NT // 2, second, last=1)
                for s in range(2):
                    sp.wait_ge(stored[s], 16 * NT // 2)

            @block.scalar
            def _(act):
                def weights(first, end, signs=False):
                    for c in range(first, end):
                        act.wait_ge(turned, c + 1)
                        nc.scalar.activation(w_hi[:, c % SLOTS, :], turn_bank(c % 2), ACT.Copy).then_inc(hi_ready, 1)
                        if signs and c > 0:
                            nf4.make_sign(act, 0, 0, c - 1)

                def load(n, j, p):
                    nf4.load(act, n, j, p, w3[n + NF4_HERE])

                def store(n, p):
                    act.wait_ge(nf4.dq_ready, n + 1)
                    act.dma_start(dq3[n + NF4_HERE], nf4.dq[:, p, :]).then_inc(dq_stored[p], 16)

                load(0, 0, 0)
                load(1, 0, 1)
                weights(0, HALF, signs=True)

                def take_sums(n):
                    act.wait_ge(summed, n + 1)
                    wait(act, kept[n % 2], 16 * (n // 2))
                    nc.scalar.activation(y[:, n % 2, :], acc_bank(n % 2), ACT.Copy).then_inc(taken, 1)

                take_after = {SOON + 2 + n * (ROUNDED * NQ - SOON) // NT: n for n in range(NT)}
                for n in range(ROUNDED):
                    for i in range(SOON if n == 0 else 0, NQ):
                        nf4.make_sign(act, n, n % 2, i)
                        if n * NQ + i in take_after:
                            tile = take_after[n * NQ + i]
                            if tile == NT - 2:
                                weights(HALF, SLOTS)
                            take_sums(tile)
                    if n > 0:
                        store(n - 1, (n - 1) % 2)
                    if n + 2 < ROUNDED:
                        load(n + 2, n // 2 + 1, n % 2)
                store(ROUNDED - 1, 1)
                act.wait_ge(summed, NT)
                weights(SLOTS, FT)

            @block.gpsimd
            def _(pool):
                def body(j):
                    for p in range(2):
                        stats.invert(pool, j * 2 + p, p)
                tiles(pool, NT // 2, body)

            @block.tensor
            def _(pe):
                def turn(c):
                    pe.wait_ge(dq_in[c % 2], 16 * (c // 2 + 1))
                    wait(pe, lo_ready, c - 1)
                    for b in range(KT):
                        op = nc.tensor.transpose(turn_bank(c % 2)[:, b * P:(b + 1) * P],
                                                 dq[:, c % 2, b * P:(b + 1) * P], k.ident[:, :])
                    op.then_inc(turned, 1)

                def products(m, p, h, t):
                    for i, (a, w) in enumerate(((a_hi, w_hi), (a_hi, w_lo), (a_lo, w_hi))):
                        op = nc.tensor.matmul(k.psum[:, 2 * p + h, :], a[:, p, t, :],
                                              w[:, (m * HALF + t) % SLOTS, h * CH:(h + 1) * CH],
                                              start=(t == 0 and i == 0), stop=(t == HALF - 1 and i == 2))
                    if t == HALF - 1 and h == 1:
                        op.then_inc(summed, 1)

                def half(m):
                    if m == 0:
                        turn(0)
                        turn(1)
                    for p in range(2):
                        pe.wait_ge(a_in[p], 32 * (m * NT // 2 + 1))
                        wait(pe, taken, m * NT + p - 1)
                    TAIL = 4
                    for t in range(HALF):
                        if t + 2 < HALF:
                            turn_next = m * HALF + t + 2
                            if m == 0 or turn_next >= SLOTS:
                                turn(turn_next)
                        if t < HALF - TAIL:
                            pe.wait_ge(lo_ready, m * HALF + t + 1)
                            for p in range(2):
                                for h in range(2):
                                    products(m, p, h, t)
                    for p in range(2):
                        for t in range(HALF - TAIL, HALF):
                            pe.wait_ge(lo_ready, m * HALF + t + 1)
                            for h in range(2):
                                products(m, p, h, t)

                    def body(j):
                        for p in range(2):
                            pe.wait_ge(a_in[p], 32 * (m * NT // 2 + j + 1))
                            pe.wait_ge(taken, m * NT + 2 * j + p - 1)
                            for h in range(2):
                                for t in range(HALF):
                                    products(m, p, h, t)
                    with pe.Fori(1, NT // 2 - 1) as j:
                        body(j)
                    if m == 0:
                        for c in range(HALF, SLOTS):
                            turn(c)
                    body(NT // 2 - 1)
                half(0)
                half(1)

            @block.vector
            def _(dve):

                def weights(first, end, takes=False):
                    for c in range(first, end):
                        dve.wait_ge(hi_ready, c + 1)
                        nc.vector.tensor_tensor(w_lo[:, c % SLOTS, :], turn_bank(c % 2), w_hi[:, c % SLOTS, :].bitcast(F32),
                                                ALU.subtract).then_inc(lo_ready, 1)
                        if takes and c == 0:
                            nf4.prepare(dve, 0, 0, 0)
                        elif takes:
                            nf4.take(dve, 0, 0, c - 1)
                weights(0, HALF, takes=True)

                def rounding(j):
                    for p in range(2):
                        n = j * 2 + p
                        if isinstance(n, int) and n == ROUNDED - 1:
                            weights(HALF, SLOTS)
                        start = SOON if isinstance(n, int) and n == 0 else 0
                        for i in range(start, NQ):
                            nf4.take(dve, n, p, i)
                            if i == max(start, NQ // 2) and not (isinstance(n, int) and n == ROUNDED - 1):
                                nf4.prepare(dve, n + 1, j + p, 1 - p)
                        wait(dve, dq_stored[p], 16 * j)
                        nf4.finish(dve, n, p)
                tiles(dve, ROUNDED // 2, rounding, last=1)
                weights(SLOTS, FT)
                for s in range(2):
                    dve.wait_ge(kept[s], 16 * NT // 2)

                def body(j):
                    for p in range(2):
                        n = j * 2 + p
                        dve.wait_ge(summed, NT + n + 1)
                        dve.wait_ge(rows_in[p], 32 * (j + 1))
                        wait(dve, stored[p], 16 * j)
                        nc.vector.tensor_tensor(y[:, p, :], acc_bank(p), before[:, p, :], ALU.add).then_inc(taken, 1)
                        dve.wait_ge(taken, NT + n + 1)
                        wait(dve, flat_ready, n - 1)
                        stats.moments(dve, n, p, [y[:, p, h * CH:(h + 1) * CH] for h in range(2)])
                        stats.normalise(dve, n, p, y[:, p, :], y[:, p, :]).then_inc(flat_ready, 1)
                        dve.wait_ge(flat_ready, n + 1)
                        nc.vector.tensor_tensor(y[:, p, :], y[:, p, :], rows[:, p, :], ALU.add).then_inc(added, 1)
                tiles(dve, NT // 2, body)


class Shared:
    pass


def block_kernel(nc, x, wqkv, bqkv, wout, bout, w12, w3, slopes, out):
    scratch = lambda name, shape: nc.dram_tensor(name, shape, F32, kind="Internal").ap()
    q_hi, q_lo, k_hi, k_lo, v_all = (scratch(n, (GROUPS, P, S)) for n in ("q_hi", "q_lo", "k_hi", "k_lo", "v_all"))
    alibi = scratch("alibi", (GROUPS, 2, G4, S))
    att_hi, att_lo = (scratch(n, (GROUPS, S // CH, P, CH)) for n in ("att_hi", "att_lo"))
    x2, partial = scratch("x2", (NT, P, D)), scratch("partial", (NT, P, D))
    dq3, dq12 = scratch("dq3", (FT, P, D)), scratch("dq12", (2, P, D))
    h_hi, h_lo = scratch("h_hi", (FT, P, TOK)), scratch("h_lo", (FT, P, TOK))
    with ExitStack() as ctx:
        k = Shared()
        k.passed = ctx.enter_context(nc.semaphore("passed"))
        k.psum = ctx.enter_context(nc.psum_tensor("psum", [P, 8, CH], F32))
        k.ident = ctx.enter_context(nc.sbuf_tensor("ident", [P, P], F32))
        k.ident16 = ctx.enter_context(nc.sbuf_tensor("ident16", [P, P], BF16))
        k.mask_q = ctx.enter_context(nc.sbuf_tensor("mask_q", [P, P], BF16))
        k.mask_k = ctx.enter_context(nc.sbuf_tensor("mask_k", [P, P], BF16))
        k.eps = ctx.enter_context(nc.sbuf_tensor("eps", [P, 1], F32))
        k.power = ctx.enter_context(nc.sbuf_tensor("power", [P, 1], F32))
        k.bounds = ctx.enter_context(nc.sbuf_tensor("bounds", [P, NQ], F32))
        constants(nc, k, slopes, alibi)
        with ExitStack() as part:
            xt_hi = part.enter_context(nc.sbuf_tensor("xt_hi", [P, KT, TOK], F32R))
            xt_lo = part.enter_context(nc.sbuf_tensor("xt_lo", [P, KT, TOK], F32R))
            normalise(nc, k, "ln1", x, xt_hi, xt_lo)
            qkv(nc, k, wqkv, bqkv, w3, xt_hi, xt_lo, q_hi, q_lo, k_hi, k_lo, v_all, dq3)
        attention(nc, k, q_hi, q_lo, k_hi, k_lo, v_all, alibi, att_hi, att_lo)
        chunked = [[a[b * HG:(b + 1) * HG, c].rearrange("g p t -> p g t") for b in range(B) for c in range(S // CH)]
                   for a in (att_hi, att_lo)]
        out_project(nc, k, wout, bout, x, w12, chunked[0], chunked[1], x2, dq12)
        with ExitStack() as part:
            xt_hi = part.enter_context(nc.sbuf_tensor("xt2_hi", [P, KT, TOK], F32R))
            xt_lo = part.enter_context(nc.sbuf_tensor("xt2_lo", [P, KT, TOK], F32R))
            normalise(nc, k, "ln2", x2, xt_hi, xt_lo)
            gate_up(nc, k, w12, dq12, xt_hi, xt_lo, h_hi, h_lo)
        down(nc, k, w3, dq3, h_hi, h_lo, x2, partial, out)


def kernel(**inputs):
    import numpy as np
    import concourse.bacc as bacc
    from concourse.bass_utils import run_bass_kernel_spmd

    get = lambda n: np.asarray(inputs[n])
    pad = FT * P - F
    tiled = {
        "x": get("L0_attn_x").reshape(NT, P, D),
        "wqkv": get("L0_attn_w_qkv").reshape(3 * KT, P, KT, P).transpose(0, 3, 2, 1),
        "bqkv": get("L0_attn_b_qkv").reshape(3 * KT, P).T,
        "wout": get("L0_attn_w_out").T.reshape(KT, P, D),
        "bout": get("L0_attn_b_out"),
        "w12": np.stack([np.pad(get(n), ((0, pad), (0, 0))).reshape(FT, P, D) for n in ("L0_ffn_w1", "L0_ffn_w2")],
                        axis=1).reshape(2 * FT, P, D),
        "w3": np.pad(get("L0_ffn_w3"), ((0, 0), (0, pad))).reshape(KT, P, FT, P).transpose(2, 1, 0, 3).reshape(FT, P, D),
        "slopes": (np.float32(1.0) / np.power(np.float32(2.0), np.arange(1, HEADS + 1, dtype=np.float32)
                                              * np.float32(8.0 / HEADS))).reshape(HEADS, 1).astype(np.float32),
    }
    nc = bacc.Bacc("TRN2", target_bir_lowering=False, num_devices=1)
    arrays, args = {}, []
    for name, a in tiled.items():
        a = np.ascontiguousarray(a)
        arrays[f"in_{name}"] = a
        args.append(nc.dram_tensor(f"in_{name}", a.shape, mybir.dt.from_np(a.dtype), kind="ExternalInput").ap())
    out = nc.dram_tensor("result_rows", (NT, P, D), F32, kind="ExternalOutput").ap()
    block_kernel(nc, *args, out)
    r = run_bass_kernel_spmd(nc, [arrays], core_ids=[0])
    return r.results[0]["result_rows"].reshape(B, S, D)
```
